# Optimizing a Trainium2 kernel written in Bass

```python
import numpy as np
import jax
import jax.numpy as jnp

def _softmax(x, axis=-1):
    return jax.nn.softmax(x, axis=axis)

def _gelu(x):
    return jax.nn.gelu(x, approximate=True)

def _silu(x):
    return jax.nn.silu(x)

def _sigmoid(x):
    return jax.nn.sigmoid(x)

def _layernorm(x, axis=-1, eps=1e-05):
    m = jnp.mean(x, axis=axis, keepdims=True)
    v = jnp.var(x, axis=axis, keepdims=True)
    return (x - m) / jnp.sqrt(v + eps)

def _scatter_add(tgt, idx, src, axis=0):
    return tgt.at[idx].add(src)

def _segment_sum(src, seg, n):
    return jax.ops.segment_sum(src, seg, n)
kernel_name = 'mk_gnn_resnorm_d4_gnn_r32_6ced99'

def setup_inputs(seed: int=0):
    np.random.seed(seed)
    _w = jnp.asarray

    def _rec_inputs():
        import jax
        import jax.numpy as jnp
        _gk = jax.random.key(seed)
        x = -0.000202 + 1 * jax.random.normal(jax.random.fold_in(_gk, 1), (50000, 128), jnp.float32)
        src = jax.random.randint(jax.random.fold_in(_gk, 2), (25000,), 0, 50000, jnp.int32)
        dst = jnp.minimum((50000 * jax.random.uniform(jax.random.fold_in(_gk, 3), (25000,)) ** 2.0).astype(jnp.int32), 49999)
        _o = jnp.argsort(dst, stable=True)
        src = src[_o]
        dst = dst[_o]
        edge_type_2 = jax.random.randint(jax.random.fold_in(_gk, 13), (25000,), 0, 2, jnp.int32)
        edge_type_4 = jax.random.randint(jax.random.fold_in(_gk, 14), (25000,), 0, 4, jnp.int32)
        return (x, src, dst, edge_type_2, edge_type_4)
    x, src, dst, edge_type_2, edge_type_4 = _rec_inputs()

    def _L0_gnn_setup():
        import jax, jax.numpy as jnp
        import numpy as np
        N = 50000
        E = 25000
        IN = 128
        OUT = 128
        R = 4
        H = 8
        D = OUT // H
        NEG_SLOPE = 0.2

        def _hgnn_forward(node_inp, edge_index, edge_type, W_rel, att_src_rel, att_dst_rel, bias_rel, W_self, W_cross, att_src_lang, att_dst_lang, bias_lang):
            src, dst = (edge_index[0], edge_index[1])

            def rel_gat(W, a_s, a_d, b, mask):
                x = (node_inp @ W).reshape(N, H, D)
                es = jnp.einsum('nhd,hd->nh', x, a_s)
                ed = jnp.einsum('nhd,hd->nh', x, a_d)
                logit = jax.nn.leaky_relu(es[src] + ed[dst], NEG_SLOPE)
                logit = jnp.where(mask[:, None], logit, -1e+30)
                mx = jax.ops.segment_max(logit, dst, num_segments=N)
                mx = jnp.maximum(mx, -1e+30)
                p = jnp.exp(logit - mx[dst]) * mask[:, None]
                den = jax.ops.segment_sum(p, dst, num_segments=N)
                alpha = p / jnp.where(den > 0, den, 1.0)[dst]
                msg = alpha[..., None] * x[src]
                out = jax.ops.segment_sum(msg, dst, num_segments=N)
                tmask = jax.ops.segment_sum(mask.astype(jnp.float32), dst, num_segments=N) > 0
                return (out.reshape(N, OUT) + b, tmask)
            rel_masks = edge_type[None, :] == jnp.arange(R)[:, None]
            rel_out, tmask = jax.vmap(rel_gat)(W_rel, att_src_rel, att_dst_rel, bias_rel, rel_masks)
            h = jax.nn.gelu(rel_out, approximate=False) @ W_cross
            S = node_inp @ W_self
            ent = jnp.concatenate([S[None], h], axis=0).reshape(R + 1, N, H, D)
            valid = jnp.concatenate([jnp.ones((1, N), bool), tmask], axis=0)
            ls = jnp.einsum('knhd,hd->knh', ent, att_src_lang)
            ld = jnp.einsum('nhd,hd->nh', ent[0], att_dst_lang)
            logit = jax.nn.leaky_relu(ls + ld[None], NEG_SLOPE)
            logit = jnp.where(valid[..., None], logit, -jnp.inf)
            alpha = jax.nn.softmax(logit, axis=0)
            out = jnp.einsum('knh,knhd->nhd', alpha, ent).reshape(N, OUT)
            return out + bias_lang
        key = jax.random.key(seed)
        ks = jax.random.split(key, 12)
        s = 0.05
        return {'node_inp': jax.random.normal(ks[0], (N, IN), dtype=jnp.float32), 'edge_index': jax.random.randint(ks[1], (2, E), 0, N), 'edge_type': jax.random.randint(ks[2], (E,), 0, R), 'W_rel': jax.random.normal(ks[3], (R, IN, OUT), dtype=jnp.float32) * s, 'att_src_rel': jax.random.normal(ks[4], (R, H, D), dtype=jnp.float32) * s, 'att_dst_rel': jax.random.normal(ks[5], (R, H, D), dtype=jnp.float32) * s, 'bias_rel': jax.random.normal(ks[6], (R, OUT), dtype=jnp.float32) * s, 'W_self': jax.random.normal(ks[7], (IN, OUT), dtype=jnp.float32) * s, 'W_cross': jax.random.normal(ks[8], (OUT, OUT), dtype=jnp.float32) * s, 'att_src_lang': jax.random.normal(ks[9], (H, D), dtype=jnp.float32) * s, 'att_dst_lang': jax.random.normal(ks[10], (H, D), dtype=jnp.float32) * s, 'bias_lang': jax.random.normal(ks[11], (OUT,), dtype=jnp.float32) * s}
    _L0_gnn_all = _L0_gnn_setup()
    _L0_gnn_in = {k: v for k, v in _L0_gnn_all.items() if k in ('W_rel', 'att_src_rel', 'att_dst_rel', 'bias_rel', 'W_self', 'W_cross', 'att_src_lang', 'att_dst_lang', 'bias_lang')}
    del _L0_gnn_all

    def _L1_gnn_setup():
        import jax, jax.numpy as jnp
        import numpy as np
        N_NODES = 10000
        N_EDGES = 20000
        C = 128
        key = jax.random.key(seed)
        k1, k2, k3, k4 = jax.random.split(key, 4)
        x = jax.random.normal(k1, (N_NODES, C), dtype=jnp.float32)
        edge_index = jax.random.randint(k2, (2, N_EDGES), 0, N_NODES, dtype=jnp.int64)
        W2 = jax.random.normal(k3, (C,), dtype=jnp.float32)
        W3 = jax.random.normal(k4, (C,), dtype=jnp.float32)
        return {'x': x, 'edge_index': edge_index, 'W2': W2, 'W3': W3}
    _L1_gnn_all = _L1_gnn_setup()
    _L1_gnn_in = {k: v for k, v in _L1_gnn_all.items() if k in ('W2', 'W3')}
    del _L1_gnn_all

    def _L2_gnn_setup():
        import jax, jax.numpy as jnp
        import numpy as np
        N_NODES = 50000
        N_EDGES = 25000
        IN_DIM = 128
        EDGE_HID = 32
        MLP_HID = 64
        N_LAYERS = 3
        N_ETYPES = 2

        def mlp(x, W1, b1, W2, b2):
            return jax.nn.relu(x @ W1 + b1) @ W2 + b2
        key = jax.random.key(seed)
        ks = jax.random.split(key, 10)
        s = 0.05
        nf = jax.random.normal(ks[0], (N_NODES, IN_DIM), jnp.float32)
        eW1 = jax.random.normal(ks[1], (N_LAYERS, N_ETYPES, 2 * IN_DIM, MLP_HID), jnp.float32) * s
        eb1 = jnp.zeros((N_LAYERS, N_ETYPES, MLP_HID), jnp.float32)
        eW2 = jax.random.normal(ks[2], (N_LAYERS, N_ETYPES, MLP_HID, EDGE_HID), jnp.float32) * s
        eb2 = jnp.zeros((N_LAYERS, N_ETYPES, EDGE_HID), jnp.float32)
        nW1 = jax.random.normal(ks[3], (N_LAYERS, EDGE_HID * N_ETYPES + IN_DIM, MLP_HID), jnp.float32) * s
        nb1 = jnp.zeros((N_LAYERS, MLP_HID), jnp.float32)
        nW2 = jax.random.normal(ks[4], (N_LAYERS, MLP_HID, IN_DIM), jnp.float32) * s
        nb2 = jnp.zeros((N_LAYERS, IN_DIM), jnp.float32)
        src = jax.random.randint(ks[5], (N_EDGES,), 0, N_NODES, jnp.int32)
        dst = jax.random.randint(ks[6], (N_EDGES,), 0, N_NODES, jnp.int32)
        etype = jax.random.randint(ks[7], (N_EDGES,), 0, N_ETYPES, jnp.int32)
        return {'nf': nf, 'eW1': eW1, 'eb1': eb1, 'eW2': eW2, 'eb2': eb2, 'nW1': nW1, 'nb1': nb1, 'nW2': nW2, 'nb2': nb2, 'src': src, 'dst': dst, 'etype': etype}
    _L2_gnn_all = _L2_gnn_setup()
    _L2_gnn_in = {k: v for k, v in _L2_gnn_all.items() if k in ('eW1', 'eb1', 'eW2', 'eb2', 'nW1', 'nb1', 'nW2', 'nb2')}
    del _L2_gnn_all

    def _L3_gnn_setup():
        import jax, jax.numpy as jnp
        import numpy as np
        N_NODES, N_EDGES, N_INC = (50000, 10000, 25000)
        IN_C, HID_C, OUT_C = (128, 128, 128)
        EPS = 1e-05

        def _hconv(x, W, b, node_idx, edge_idx, hw):
            x = x @ W.T
            D = jax.ops.segment_sum(hw[edge_idx], node_idx, num_segments=N_NODES)
            Dinv = jnp.where(D > 0, 1.0 / D, 0.0)
            Bdeg = jax.ops.segment_sum(jnp.ones_like(edge_idx, dtype=x.dtype), edge_idx, num_segments=N_EDGES)
            Binv = jnp.where(Bdeg > 0, 1.0 / Bdeg, 0.0)
            e = jax.ops.segment_sum(Binv[edge_idx][:, None] * x[node_idx], edge_idx, num_segments=N_EDGES)
            out = jax.ops.segment_sum(Dinv[node_idx][:, None] * e[edge_idx], node_idx, num_segments=N_NODES)
            return out + b
        key = jax.random.key(seed)
        ks = jax.random.split(key, 6)
        x = jax.random.normal(ks[0], (N_NODES, IN_C), jnp.float32)
        node_idx = jax.random.randint(ks[1], (N_INC,), 0, N_NODES)
        edge_idx = jax.random.randint(ks[2], (N_INC,), 0, N_EDGES)
        hyperedge_index = jnp.stack([node_idx, edge_idx])
        hyperedge_weight = jnp.ones((N_EDGES,), jnp.float32)
        s1 = 1.0 / np.sqrt(IN_C)
        s2 = 1.0 / np.sqrt(HID_C)
        W1 = jax.random.uniform(ks[3], (HID_C, IN_C), jnp.float32, -s1, s1)
        b1 = jnp.zeros((HID_C,), jnp.float32)
        gamma = jnp.ones((HID_C,), jnp.float32)
        beta = jnp.zeros((HID_C,), jnp.float32)
        W2 = jax.random.uniform(ks[4], (OUT_C, HID_C), jnp.float32, -s2, s2)
        b2 = jnp.zeros((OUT_C,), jnp.float32)
        return dict(x=x, hyperedge_index=hyperedge_index, hyperedge_weight=hyperedge_weight, W1=W1, b1=b1, gamma=gamma, beta=beta, W2=W2, b2=b2)
    _L3_gnn_all = _L3_gnn_setup()
    _L3_gnn_in = {k: v for k, v in _L3_gnn_all.items() if k in ('hyperedge_weight', 'W1', 'b1', 'gamma', 'beta', 'W2', 'b2')}
    del _L3_gnn_all
    return {'x': x, 'src': src, 'dst': dst, 'edge_type_2': edge_type_2, 'edge_type_4': edge_type_4, 'L0_gnn_W_rel': _L0_gnn_in['W_rel'], 'L0_gnn_att_src_rel': _L0_gnn_in['att_src_rel'], 'L0_gnn_att_dst_rel': _L0_gnn_in['att_dst_rel'], 'L0_gnn_bias_rel': _L0_gnn_in['bias_rel'], 'L0_gnn_W_self': _L0_gnn_in['W_self'], 'L0_gnn_W_cross': _L0_gnn_in['W_cross'], 'L0_gnn_att_src_lang': _L0_gnn_in['att_src_lang'], 'L0_gnn_att_dst_lang': _L0_gnn_in['att_dst_lang'], 'L0_gnn_bias_lang': _L0_gnn_in['bias_lang'], 'L1_gnn_W2': _L1_gnn_in['W2'], 'L1_gnn_W3': _L1_gnn_in['W3'], 'L2_gnn_eW1': _L2_gnn_in['eW1'], 'L2_gnn_eb1': _L2_gnn_in['eb1'], 'L2_gnn_eW2': _L2_gnn_in['eW2'], 'L2_gnn_eb2': _L2_gnn_in['eb2'], 'L2_gnn_nW1': _L2_gnn_in['nW1'], 'L2_gnn_nb1': _L2_gnn_in['nb1'], 'L2_gnn_nW2': _L2_gnn_in['nW2'], 'L2_gnn_nb2': _L2_gnn_in['nb2'], 'L3_gnn_hyperedge_weight': _L3_gnn_in['hyperedge_weight'], 'L3_gnn_W1': _L3_gnn_in['W1'], 'L3_gnn_b1': _L3_gnn_in['b1'], 'L3_gnn_gamma': _L3_gnn_in['gamma'], 'L3_gnn_beta': _L3_gnn_in['beta'], 'L3_gnn_W2': _L3_gnn_in['W2'], 'L3_gnn_b2': _L3_gnn_in['b2']}

def reference(x, src, dst, edge_type_2, edge_type_4, L0_gnn_W_rel, L0_gnn_att_src_rel, L0_gnn_att_dst_rel, L0_gnn_bias_rel, L0_gnn_W_self, L0_gnn_W_cross, L0_gnn_att_src_lang, L0_gnn_att_dst_lang, L0_gnn_bias_lang, L1_gnn_W2, L1_gnn_W3, L2_gnn_eW1, L2_gnn_eb1, L2_gnn_eW2, L2_gnn_eb2, L2_gnn_nW1, L2_gnn_nb1, L2_gnn_nW2, L2_gnn_nb2, L3_gnn_hyperedge_weight, L3_gnn_W1, L3_gnn_b1, L3_gnn_gamma, L3_gnn_beta, L3_gnn_W2, L3_gnn_b2):
    import jax
    import jax.numpy as jnp

    def _L0_gnn_ref(node_inp, edge_index, edge_type, W_rel, att_src_rel, att_dst_rel, bias_rel, W_self, W_cross, att_src_lang, att_dst_lang, bias_lang):
        import jax, jax.numpy as jnp
        import numpy as np
        N = 50000
        E = 25000
        IN = 128
        OUT = 128
        R = 4
        H = 8
        D = OUT // H
        NEG_SLOPE = 0.2

        def _hgnn_forward(node_inp, edge_index, edge_type, W_rel, att_src_rel, att_dst_rel, bias_rel, W_self, W_cross, att_src_lang, att_dst_lang, bias_lang):
            src, dst = (edge_index[0], edge_index[1])

            def rel_gat(W, a_s, a_d, b, mask):
                x = (node_inp @ W).reshape(N, H, D)
                es = jnp.einsum('nhd,hd->nh', x, a_s)
                ed = jnp.einsum('nhd,hd->nh', x, a_d)
                logit = jax.nn.leaky_relu(es[src] + ed[dst], NEG_SLOPE)
                logit = jnp.where(mask[:, None], logit, -1e+30)
                mx = jax.ops.segment_max(logit, dst, num_segments=N)
                mx = jnp.maximum(mx, -1e+30)
                p = jnp.exp(logit - mx[dst]) * mask[:, None]
                den = jax.ops.segment_sum(p, dst, num_segments=N)
                alpha = p / jnp.where(den > 0, den, 1.0)[dst]
                msg = alpha[..., None] * x[src]
                out = jax.ops.segment_sum(msg, dst, num_segments=N)
                tmask = jax.ops.segment_sum(mask.astype(jnp.float32), dst, num_segments=N) > 0
                return (out.reshape(N, OUT) + b, tmask)
            rel_masks = edge_type[None, :] == jnp.arange(R)[:, None]
            rel_out, tmask = jax.vmap(rel_gat)(W_rel, att_src_rel, att_dst_rel, bias_rel, rel_masks)
            h = jax.nn.gelu(rel_out, approximate=False) @ W_cross
            S = node_inp @ W_self
            ent = jnp.concatenate([S[None], h], axis=0).reshape(R + 1, N, H, D)
            valid = jnp.concatenate([jnp.ones((1, N), bool), tmask], axis=0)
            ls = jnp.einsum('knhd,hd->knh', ent, att_src_lang)
            ld = jnp.einsum('nhd,hd->nh', ent[0], att_dst_lang)
            logit = jax.nn.leaky_relu(ls + ld[None], NEG_SLOPE)
            logit = jnp.where(valid[..., None], logit, -jnp.inf)
            alpha = jax.nn.softmax(logit, axis=0)
            out = jnp.einsum('knh,knhd->nhd', alpha, ent).reshape(N, OUT)
            return out + bias_lang
        return _hgnn_forward(node_inp, edge_index, edge_type, W_rel, att_src_rel, att_dst_rel, bias_rel, W_self, W_cross, att_src_lang, att_dst_lang, bias_lang)

    def _L1_gnn_ref(x, edge_index, W2, W3):
        import jax, jax.numpy as jnp
        import numpy as np
        N_NODES = 10000
        N_EDGES = 20000
        C = 128
        src = edge_index[0]
        dst = edge_index[1]
        x2 = x * W2
        x3 = x * W3
        attn = jnp.einsum('ec,ec->e', x3[src], x[dst])
        out = jax.ops.segment_sum(attn[:, None] * x2[src], dst, num_segments=x.shape[0])
        return out

    def _L2_gnn_ref(nf, eW1, eb1, eW2, eb2, nW1, nb1, nW2, nb2, src, dst, etype):
        import jax, jax.numpy as jnp
        import numpy as np
        N_NODES = 50000
        N_EDGES = 25000
        IN_DIM = 128
        EDGE_HID = 32
        MLP_HID = 64
        N_LAYERS = 3
        N_ETYPES = 2

        def mlp(x, W1, b1, W2, b2):
            return jax.nn.relu(x @ W1 + b1) @ W2 + b2
        n = nf.shape[0]
        h = nf
        for l in range(N_LAYERS):
            ef = jnp.concatenate([h[src], h[dst]], axis=-1)
            msgs = []
            for e in range(N_ETYPES):
                m = mlp(ef, eW1[l, e], eb1[l, e], eW2[l, e], eb2[l, e])
                mask = (etype == e).astype(h.dtype)
                msum = jax.ops.segment_sum(m * mask[:, None], dst, num_segments=n)
                cnt = jax.ops.segment_sum(mask, dst, num_segments=n)
                msgs.append(msum / jnp.maximum(cnt, 1.0)[:, None])
            upd_in = jnp.concatenate(msgs + [h], axis=-1)
            h = mlp(upd_in, nW1[l], nb1[l], nW2[l], nb2[l])
        return h

    def _L3_gnn_ref(x, hyperedge_index, hyperedge_weight, W1, b1, gamma, beta, W2, b2):
        import jax, jax.numpy as jnp
        import numpy as np
        N_NODES, N_EDGES, N_INC = (50000, 10000, 25000)
        IN_C, HID_C, OUT_C = (128, 128, 128)
        EPS = 1e-05

        def _hconv(x, W, b, node_idx, edge_idx, hw):
            x = x @ W.T
            D = jax.ops.segment_sum(hw[edge_idx], node_idx, num_segments=N_NODES)
            Dinv = jnp.where(D > 0, 1.0 / D, 0.0)
            Bdeg = jax.ops.segment_sum(jnp.ones_like(edge_idx, dtype=x.dtype), edge_idx, num_segments=N_EDGES)
            Binv = jnp.where(Bdeg > 0, 1.0 / Bdeg, 0.0)
            e = jax.ops.segment_sum(Binv[edge_idx][:, None] * x[node_idx], edge_idx, num_segments=N_EDGES)
            out = jax.ops.segment_sum(Dinv[node_idx][:, None] * e[edge_idx], node_idx, num_segments=N_NODES)
            return out + b
        node_idx, edge_idx = (hyperedge_index[0], hyperedge_index[1])
        h = _hconv(x, W1, b1, node_idx, edge_idx, hyperedge_weight)
        mu = h.mean(axis=0)
        var = h.var(axis=0)
        h = gamma * (h - mu) * jax.lax.rsqrt(var + EPS) + beta
        return _hconv(h, W2, b2, node_idx, edge_idx, hyperedge_weight)
    edge_index = jnp.stack([src, dst])
    x = _layernorm(x + _L0_gnn_ref(x, edge_index, edge_type_4, L0_gnn_W_rel, L0_gnn_att_src_rel, L0_gnn_att_dst_rel, L0_gnn_bias_rel, L0_gnn_W_self, L0_gnn_W_cross, L0_gnn_att_src_lang, L0_gnn_att_dst_lang, L0_gnn_bias_lang), axis=-1)
    x = _layernorm(x + _L1_gnn_ref(x, edge_index, L1_gnn_W2, L1_gnn_W3), axis=-1)
    x = _layernorm(x + _L2_gnn_ref(x, L2_gnn_eW1, L2_gnn_eb1, L2_gnn_eW2, L2_gnn_eb2, L2_gnn_nW1, L2_gnn_nb1, L2_gnn_nW2, L2_gnn_nb2, src, dst, edge_type_2), axis=-1)
    x = _layernorm(x + _L3_gnn_ref(x, edge_index, L3_gnn_hyperedge_weight, L3_gnn_W1, L3_gnn_b1, L3_gnn_gamma, L3_gnn_beta, L3_gnn_W2, L3_gnn_b2), axis=-1)
    return x

_drawn_inputs = setup_inputs


def setup_inputs(seed=0):
    import zlib

    import numpy as np

    out = dict(_drawn_inputs(seed))
    spreads = {'L2_gnn_eb1': (0.0, 0.8),
     'L2_gnn_eb2': (0.0, 0.8),
     'L2_gnn_nb1': (0.0, 0.296),
     'L2_gnn_nb2': (0.0, 0.1),
     'L3_gnn_hyperedge_weight': (1.0, 0.2),
     'L3_gnn_b1': (0.0, 2.0),
     'L3_gnn_gamma': (1.0, 0.2),
     'L3_gnn_beta': (0.0, 0.559),
     'L3_gnn_b2': (0.0, 0.1)}
    factors = {'L0_gnn_att_src_rel': 64.0,
     'L0_gnn_att_dst_rel': 64.0,
     'L0_gnn_bias_rel': 4.123,
     'L0_gnn_att_dst_lang': 39.125,
     'L2_gnn_eW1': 8.0,
     'L2_gnn_eW2': 8.0,
     'L2_gnn_nW1': 3.589,
     'L0_gnn_att_src_lang': 3.458}
    for name, (base, spread) in spreads.items():
        noise = np.random.default_rng([zlib.crc32(name.encode()), seed]).standard_normal(out[name].shape)
        drawn = base * np.exp(spread * noise) if base else spread * noise
        out[name] = jnp.asarray(drawn.astype(out[name].dtype))
    for name, factor in factors.items():
        out[name] = (out[name] * factor).astype(out[name].dtype)
    return out
```

```python
from contextlib import ExitStack

import numpy as np

import concourse.bass as bass
from concourse import mybir

F32 = mybir.dt.float32
I32 = mybir.dt.int32
BF16 = mybir.dt.bfloat16
ALU = mybir.AluOpType
ACT = mybir.ActivationFunctionType
AX = mybir.AxisListType

P = 128
N = 50000
E = 25000
H5 = 10000
C = 128
R = 4
H = 8
D = C // H
U = 4
CH = P * U
NC = -(-E // CH)
EP = NC * CH
NT = EP // P
NP = N // CH
RP, RC = 98, EP // 98
HI = -(-(N + 1) // P)
NOWHERE = 1 << 20
EPS = 1e-5
LEAK = 0.2
NEG = 1.0e30
MASKED = 3.0e38


class Phase:

    def __init__(self, nc, name):
        self.nc, self.name, self.stack, self.sems = nc, name, ExitStack(), []

    def __enter__(self):
        self.stack.__enter__()
        return self

    def __exit__(self, *exc):
        done = self.stack.__exit__(*exc)
        self.nc.clear_and_free_semaphores(self.sems)
        self.nc.all_engine_barrier()
        return done

    def sb(self, name, shape, dtype=F32):
        return self.stack.enter_context(self.nc.sbuf_tensor(f"{self.name}_{name}", shape, dtype))

    def ps(self, name, shape=(P, CH)):
        return self.stack.enter_context(self.nc.psum_tensor(f"{self.name}_{name}", list(shape), F32))

    def sem(self, name):
        self.sems.append(self.nc.alloc_semaphore(f"{self.name}_{name}"))
        return self.sems[-1]

    def block(self):
        return self.stack.enter_context(self.nc.Block())


def steps(eng, count, body):
    body(0, True)
    if count > 1:
        with eng.Fori(1, count) as i:
            body(i, False)


def gate(eng, sem, value, passed):
    eng.wait_ge(sem, value)
    eng.sem_inc(passed, 1)


def chunk(flat, i):
    return flat[bass.ds(i * CH, CH)].rearrange("(p u) -> p u", u=U)


def rows(flat, i, parts=P):
    return flat[bass.ds(i * CH, CH)].rearrange("(a e) -> a e", a=1).to_broadcast([parts, CH])


def slot(wide, u):
    return wide[:, u::U]


def gather(pool, tile, table, index, u, done):
    pool.indirect_dma_start(out=tile[:, u, :], out_offset=None, in_=table,
                            in_offset=bass.IndirectOffsetOnAxis(ap=index[:, u:u + 1], axis=0)).then_inc(done, 16)


def scatter(pool, table, tile, index, u, done, last_row):
    pool.indirect_dma_start(out=table, out_offset=bass.IndirectOffsetOnAxis(ap=index[:, u:u + 1], axis=0),
                            in_=tile[:, u, :], in_offset=None, bounds_check=last_row,
                            oob_is_err=False).then_inc(done, 16)



def sort_edges(nc, name, records, key_at, const, ordered):
    with Phase(nc, name) as ph:
        rec = ph.sb("rec", [P, NT, 4], I32)
        keyi = ph.sb("keyi", [P, NT], I32)
        digit = ph.sb("digit", [P, NT], I32)
        key = ph.sb("key", [P, NT])
        hi = ph.sb("hi", [P, NT])
        lo = ph.sb("lo", [P, NT])
        iota = ph.sb("iota", [P, HI])
        tri = ph.sb("tri", [P, P])
        tri_low = ph.sb("tri_low", [P, P])
        ident = ph.sb("ident", [P, P])
        ident_b = ph.sb("ident_b", [P, P], BF16)
        ones = ph.sb("ones", [P, HI])
        lob = ph.sb("lob", [P, P], BF16)
        hib = ph.sb("hib", [P, HI], BF16)
        loT = ph.sb("loT", [P, P])
        diag = ph.sb("diag", [P, P])
        keyrow = ph.sb("keyrow", [P, P])
        same = ph.sb("same", [P, P])
        rank = ph.sb("rank", [P, 1])
        looked = ph.sb("looked", [P, 1])
        junk = ph.sb("junk", [P, HI])
        posf = ph.sb("posf", [P, 1])
        pos = ph.sb("pos", [P, 1], I32)
        recst = ph.sb("recst", [P, 4], I32)
        place = ph.sb("place", [P, HI])
        total = ph.sb("total", [P, HI])
        ends = ph.sb("ends", [P, HI])
        sent = ph.sb("sent", [1, 4], I32)
        ps_count = ph.ps("ps_count")
        ps_before = ph.ps("ps_before")
        ps_total = ph.ps("ps_total")
        ps_loT = ph.stack.enter_context(nc.psum_tensor(f"{name}_ps_loT", [P, 2 * CH], BF16))
        ps_look = ph.ps("ps_look")
        ps_row = ph.ps("ps_row")
        s = {x: ph.sem(x) for x in (
            "loaded", "keys", "ones", "diag", "hot", "counted", "table", "before", "placed", "sentinel", "sent_out",
            "hot2", "loT_ps", "loT", "row_ps", "rank", "look", "looked", "own_counts", "placed2", "posf",
            "pos", "scattered", "same", "passed")}
        block = ph.block()

        @block.sync
        def _(sp):
            sp.dma_start(rec[:], records.rearrange("(t p) f -> p t f", p=P)).then_inc(s["loaded"], 16)
            sp.dma_start(iota[:], const["iota"][:, 0:HI]).then_inc(s["loaded"], 16)
            sp.dma_start(tri[:], const["tri"]).then_inc(s["loaded"], 16)
            sp.dma_start(tri_low[:], const["tri_low"]).then_inc(s["loaded"], 16)
            sp.dma_start(ident[:], const["ident"]).then_inc(s["loaded"], 16)
            sp.wait_ge(s["sentinel"], 1)
            sp.dma_start(ordered[0:1, :], sent[:]).then_inc(s["sent_out"], 16)
            sp.dma_start(ordered[EP + 1:EP + 2, :], sent[:]).then_inc(s["sent_out"], 16)
            sp.wait_ge(s["sent_out"], 32)

        @block.vector
        def _(dve):
            dve.memset(sent[:], -1).then_inc(s["sentinel"], 1)
            dve.memset(ones[:], 1.0).then_inc(s["ones"], 1)
            dve.wait_ge(s["loaded"], 16 * 5)
            dve.tensor_copy(ident_b[:], ident[:]).then_inc(s["ones"], 1)
            dve.wait_ge(s["ones"], 2)
            dve.tensor_copy(keyi[:], rec[:, :, key_at]).then_inc(s["keys"], 1)
            dve.wait_ge(s["keys"], 1)
            dve.tensor_copy(key[:], keyi[:])
            dve.tensor_scalar(digit[:], keyi[:], 7, None, ALU.arith_shift_right).then_inc(s["keys"], 1)
            dve.wait_ge(s["keys"], 2)
            dve.tensor_copy(hi[:], digit[:]).then_inc(s["keys"], 1)
            dve.wait_ge(s["keys"], 3)
            dve.tensor_scalar(digit[:], keyi[:], 127, None, ALU.bitwise_and).then_inc(s["keys"], 1)
            dve.wait_ge(s["keys"], 4)
            dve.tensor_copy(lo[:], digit[:]).then_inc(s["keys"], 1)
            dve.wait_ge(s["keys"], 5)

            def count(t, first):
                if not first:
                    dve.wait_ge(s["counted"], t)
                dve.tensor_scalar(lob[:], iota[:, 0:P], lo[:, bass.ds(t, 1)], None, ALU.is_equal)
                dve.tensor_scalar(hib[:], iota[:], hi[:, bass.ds(t, 1)], None, ALU.is_equal).then_inc(s["hot"], 1)
            steps(dve, NT, count)

            dve.wait_ge(s["counted"], NT)
            dve.tensor_copy(place[:], ps_count[:, 0:HI]).then_inc(s["table"], 1)
            dve.wait_ge(s["before"], 1)
            dve.tensor_copy(total[:], ps_total[:, 0:HI]).then_inc(s["placed"], 1)
            dve.wait_ge(s["placed"], 1)
            dve.tensor_tensor_scan(ends[:], ones[:], total[:], 0.0, ALU.mult, ALU.add).then_inc(s["placed"], 1)
            dve.wait_ge(s["placed"], 2)
            dve.tensor_tensor(ends[:], ends[:], total[:], ALU.subtract).then_inc(s["placed"], 1)
            dve.wait_ge(s["placed"], 3)
            dve.tensor_tensor(place[:], ends[:], ps_before[:, 0:HI], ALU.add).then_inc(s["placed2"], 1)
            dve.wait_ge(s["placed2"], 1)

            def position(t, first):
                if not first:
                    dve.wait_ge(s["own_counts"], t)
                dve.tensor_scalar(diag[:], ident[:], key[:, bass.ds(t, 1)], None, ALU.mult).then_inc(s["diag"], 1)
                dve.tensor_scalar(lob[:], iota[:, 0:P], lo[:, bass.ds(t, 1)], None, ALU.is_equal)
                dve.tensor_scalar(hib[:], iota[:], hi[:, bass.ds(t, 1)], None, ALU.is_equal).then_inc(s["hot2"], 1)
                dve.wait_ge(s["row_ps"], t + 1)
                dve.tensor_scalar(same[:], ps_row[:, 0:P], key[:, bass.ds(t, 1)], None, ALU.is_equal).then_inc(s["same"], 1)
                dve.wait_ge(s["same"], t + 1)
                dve.tensor_tensor_reduce(keyrow[:], same[:], tri_low[:], 1.0, 0.0, ALU.mult, ALU.add,
                                         rank[:]).then_inc(s["rank"], 1)
                dve.wait_ge(s["hot2"], t + 1)
                dve.wait_ge(s["look"], t + 1)
                dve.tensor_tensor_reduce(junk[:], ps_look[:, 0:HI], hib[:], 1.0, 0.0, ALU.mult, ALU.add,
                                         looked[:]).then_inc(s["looked"], 1)
                dve.wait_ge(s["looked"], t + 1)
                dve.wait_ge(s["rank"], t + 1)
                dve.scalar_tensor_tensor(out=posf[:], in0=looked[:], scalar=1.0, in1=rank[:],
                                         op0=ALU.add, op1=ALU.add).then_inc(s["posf"], 1)
                dve.wait_ge(s["own_counts"], t + 1)
                dve.tensor_tensor(place[:], place[:], ps_count[:, 0:HI], ALU.add).then_inc(s["placed2"], 1)
                dve.wait_ge(s["posf"], t + 1)
                if not first:
                    dve.wait_ge(s["scattered"], 16 * t)
                dve.tensor_copy(recst[:], rec[:, bass.ds(t, 1), :].rearrange("p a f -> p (a f)"))
                dve.tensor_copy(pos[:], posf[:]).then_inc(s["pos"], 1)
                dve.wait_ge(s["placed2"], t + 2)
            steps(dve, NT, position)

        @block.tensor
        def _(pe):
            pe.wait_ge(s["loaded"], 16 * 5)

            def count(t, first):
                pe.wait_ge(s["hot"], t + 1)
                pe.matmul(ps_count[:, 0:HI], lob[:], hib[:], start=first, stop=False,
                          skip_group_check=True).then_inc(s["counted"], 1)
            steps(pe, NT, count)
            pe.wait_ge(s["table"], 1)
            pe.matmul(ps_before[:, 0:HI], tri[:], place[:], start=True, stop=True)
            pe.matmul(ps_total[:, 0:HI], ones[:, 0:P], place[:], start=True, stop=True).then_inc(s["before"], 1)

            def position(t, first):
                pe.wait_ge(s["diag"], t + 1)
                pe.matmul(ps_row[:, 0:P], ones[:, 0:P], diag[:], start=True, stop=True).then_inc(s["row_ps"], 1)
                pe.wait_ge(s["hot2"], t + 1)
                pe.transpose(ps_loT[:, 0:P], lob[:], ident_b[:]).then_inc(s["loT_ps"], 1)
                pe.matmul(ps_count[:, 0:HI], lob[:], hib[:], start=True, stop=True).then_inc(s["own_counts"], 1)
                pe.wait_ge(s["placed2"], t + 1)
                pe.wait_ge(s["loT"], t + 1)
                pe.matmul(ps_look[:, 0:HI], loT[:], place[:], start=True, stop=True).then_inc(s["look"], 1)
            steps(pe, NT, position)

        @block.scalar
        def _(act):
            def position(t, first):
                act.wait_ge(s["loT_ps"], t + 1)
                if not first:
                    act.wait_ge(s["look"], t)
                act.copy(loT[:], ps_loT[:, 0:P]).then_inc(s["loT"], 1)
            steps(act, NT, position)

        @block.gpsimd
        def _(pool):
            def position(t, first):
                gate(pool, s["pos"], t + 1, s["passed"])
                pool.indirect_dma_start(out=ordered, out_offset=bass.IndirectOffsetOnAxis(ap=pos[:], axis=0),
                                        in_=recst[:], in_offset=None).then_inc(s["scattered"], 16)
            steps(pool, NT, position)
            pool.wait_ge(s["scattered"], 16 * NT)



def derive_orders(nc, by_dst, by_src, flat):
    with Phase(nc, "orders") as ph:
        s = {x: ph.sem(x) for x in ("loaded", "step", "ready", "stored")}
        cur, prev, nxt, f = {}, {}, {}, {}
        for o in "ds":
            cur[o] = ph.sb(f"cur_{o}", [RP, RC, 4], I32)
            prev[o] = ph.sb(f"prev_{o}", [RP, RC, 4], I32)
            nxt[o] = ph.sb(f"next_{o}", [RP, RC, 4], I32)
        names = ["src_d", "dst_d", "put_d", "src_s", "dst_s", "put_s"]
        for n in names:
            f[n] = ph.sb(n, [RP, RC], I32)
        fl = ["run_d", "run_s", "last_s", "rel_d", "kind0_d", "kind1_d"]
        for n in fl:
            f[n] = ph.sb(n, [RP, RC])
        goes_on = ph.sb("goes_on", [RP, RC])
        goes_on2 = ph.sb("goes_on2", [RP, RC])
        real = ph.sb("real", [RP, RC])
        block = ph.block()

        @block.sync
        def _(sp):
            for o, rec in (("d", by_dst), ("s", by_src)):
                for where, at in ((prev, 0), (cur, 1), (nxt, 2)):
                    sp.dma_start(where[o][:], rec[at:at + EP, :].rearrange("(p k) f -> p k f", p=RP)
                                 ).then_inc(s["loaded"], 16)
            sp.wait_ge(s["ready"], 1)
            for n in names + fl:
                sp.dma_start(flat[n].rearrange("(p k) -> p k", p=RP), f[n][:]).then_inc(s["stored"], 16)
            sp.wait_ge(s["stored"], 16 * len(names + fl))

        @block.vector
        def _(dve):
            dve.wait_ge(s["loaded"], 16 * 6)
            for o, k, other in (("d", 0, 1), ("s", 1, 0)):
                key = cur[o][:, :, k]
                own = "dst_d" if o == "d" else "src_s"
                far = "src_d" if o == "d" else "dst_s"
                dve.tensor_tensor(f[f"run_{o}"][:], key, prev[o][:, :, k], ALU.is_equal)
                g = goes_on if o == "d" else goes_on2
                dve.tensor_tensor(g[:], key, nxt[o][:, :, k], ALU.is_equal)
                dve.tensor_scalar(f[own][:], key, float(N - 1), None, ALU.min)
                dve.tensor_scalar(f[far][:], cur[o][:, :, other], float(N - 1 if o == "d" else H5 - 1), None,
                                  ALU.min).then_inc(s["step"], 1)
            dve.wait_ge(s["step"], 2)
            dve.scalar_tensor_tensor(out=f["put_d"][:], in0=goes_on[:], scalar=float(NOWHERE),
                                     in1=cur["d"][:, :, 0], op0=ALU.mult, op1=ALU.add)
            dve.scalar_tensor_tensor(out=f["put_s"][:], in0=goes_on2[:], scalar=float(NOWHERE),
                                     in1=cur["s"][:, :, 1], op0=ALU.mult, op1=ALU.add)
            dve.tensor_scalar(real[:], cur["s"][:, :, 1], float(N), None, ALU.is_lt)
            dve.tensor_scalar(f["kind0_d"][:], cur["d"][:, :, 3], 0.0, None, ALU.is_equal)
            dve.tensor_scalar(f["kind1_d"][:], cur["d"][:, :, 3], 1.0, None, ALU.is_equal)
            dve.tensor_copy(f["rel_d"][:], cur["d"][:, :, 2]).then_inc(s["step"], 1)
            dve.wait_ge(s["step"], 3)
            dve.tensor_tensor(f["last_s"][:], real[:], goes_on2[:], ALU.is_gt).then_inc(s["ready"], 1)


def gather_weights(nc, weight, flat):
    with Phase(nc, "hw") as ph:
        s = {x: ph.sem(x) for x in ("index", "gathered", "kept", "stored", "passed")}
        index = ph.sb("index", [P, U], I32)
        got = ph.sb("got", [P, U, 1])
        kept = ph.sb("kept", [P, NC, U])
        block = ph.block()

        @block.sync
        def _(sp):
            def body(i, first):
                if not first:
                    sp.wait_ge(s["kept"], i)
                sp.dma_start(index[:], chunk(flat["dst_s"], i)).then_inc(s["index"], 16)
            steps(sp, NC, body)
            sp.wait_ge(s["kept"], NC)
            sp.dma_start(flat["weight_s"].rearrange("(c p u) -> p c u", p=P, u=U), kept[:]).then_inc(s["stored"], 16)
            sp.wait_ge(s["stored"], 16)

        @block.gpsimd
        def _(pool):
            def body(i, first):
                gate(pool, s["index"], 16 * (i + 1), s["passed"])
                for u in range(U):
                    gather(pool, got, weight, index, u, s["gathered"])
            steps(pool, NC, body)

        @block.vector
        def _(dve):
            def body(i, first):
                dve.wait_ge(s["gathered"], 16 * U * (i + 1))
                dve.tensor_copy(kept[:, bass.ds(i, 1), :], got[:].rearrange("p u a -> p a u")).then_inc(s["kept"], 1)
            steps(dve, NC, body)


def count_runs(nc, flat, sums):
    SC = EP // 7
    with Phase(nc, "runs") as ph:
        s = {x: ph.sem(x) for x in ("ones", "loaded", "summed", "stored", "back", "step", "ready", "out")}
        run = [ph.sb(f"run{j}", [4, SC]) for j in range(2)]
        val = [ph.sb(f"val{j}", [4, SC]) for j in range(2)]
        out = [ph.sb(f"out{j}", [4, SC]) for j in range(2)]
        b = {n: ph.sb(n, [RP, RC]) for n in ("inv0", "inv1", "inv_deg", "weight", "pos", "safe", "inv", "inv_w",
                                             "gap", "t0", "t1", "t2")}
        ones_row = ph.sb("ones_row", [P, EP // P])
        block = ph.block()
        vals = ["kind0_d", "kind1_d", "ones", "weight_s"]
        facs = ["inv0_d", "inv1_d", "inv_deg_d", "inv_w_s"]

        @block.sync
        def _(sp):
            sp.wait_ge(s["ones"], 1)
            sp.dma_start(flat["ones"].rearrange("(p k) -> p k", p=P), ones_row[:]).then_inc(s["out"], 16)
            sp.wait_ge(s["out"], 16)
            for j in range(7):
                if j >= 2:
                    sp.wait_ge(s["summed"], j - 1)
                at = slice(j * SC, (j + 1) * SC)
                for q in range(4):
                    order = "run_s" if q == 3 else "run_d"
                    sp.dma_start(run[j % 2][q:q + 1, :], flat[order][at].rearrange("(a e) -> a e", a=1)).then_inc(s["loaded"], 16)
                    sp.dma_start(val[j % 2][q:q + 1, :], flat[vals[q]][at].rearrange("(a e) -> a e", a=1)).then_inc(s["loaded"], 16)
                sp.wait_ge(s["loaded"], 128 * (j + 1))
                sp.wait_ge(s["summed"], j + 1)
                sp.dma_start(sums[:, at], out[j % 2][:]).then_inc(s["stored"], 16)
                sp.wait_ge(s["stored"], 16 * (j + 1))
            for q, n in enumerate(("inv0", "inv1", "inv_deg", "weight")):
                sp.dma_start(b[n][:], sums[q].rearrange("(p k) -> p k", p=RP)).then_inc(s["back"], 16)
            sp.wait_ge(s["ready"], 1)
            for n, q in zip(facs, ("t0", "t1", "t2", "inv_w")):
                sp.dma_start(flat[n].rearrange("(p k) -> p k", p=RP), b[q][:]).then_inc(s["out"], 16)
            sp.wait_ge(s["out"], 16 * 5)

        @block.vector
        def _(dve):
            dve.memset(ones_row[:], 1.0).then_inc(s["ones"], 1)
            for j in range(7):
                dve.wait_ge(s["loaded"], 128 * (j + 1))
                if j >= 2:
                    dve.wait_ge(s["stored"], 16 * (j - 1))
                if j >= 1:
                    dve.wait_ge(s["summed"], j)
                dve.tensor_tensor_scan(out[j % 2][:], run[j % 2][:], val[j % 2][:],
                                       0.0 if j == 0 else out[1 - j % 2][:, SC - 1:SC], ALU.mult, ALU.add
                                       ).then_inc(s["summed"], 1)
            dve.wait_ge(s["back"], 64)
            for n in ("inv0", "inv1", "inv_deg"):
                dve.tensor_scalar(b[n][:], b[n][:], 1.0, None, ALU.max)
            dve.tensor_scalar(b["pos"][:], b["weight"][:], 0.0, None, ALU.is_gt).then_inc(s["step"], 1)
            dve.wait_ge(s["step"], 1)
            dve.tensor_scalar(b["gap"][:], b["pos"][:], -1.0, 1.0, ALU.mult, ALU.add)
            dve.tensor_tensor(b["safe"][:], b["weight"][:], b["pos"][:], ALU.mult).then_inc(s["step"], 1)
            dve.wait_ge(s["step"], 2)
            dve.tensor_tensor(b["inv"][:], b["safe"][:], b["gap"][:], ALU.add).then_inc(s["step"], 1)
            dve.wait_ge(s["step"], 3)
            for n, q in (("inv0", "t0"), ("inv1", "t1"), ("inv_deg", "t2")):
                dve.reciprocal(b[q][:], b[n][:])
            dve.reciprocal(b["safe"][:], b["inv"][:]).then_inc(s["step"], 1)
            dve.wait_ge(s["step"], 4)
            dve.tensor_tensor(b["inv_w"][:], b["safe"][:], b["pos"][:], ALU.mult).then_inc(s["ready"], 1)



class Norm:

    def __init__(self, ph, name, eps):
        self.stats = ph.sb(f"{name}_stats", [P, U, 6])
        self.mv = ph.sb(f"{name}_mv", [P, U, 2])
        self.root = ph.sb(f"{name}_root", [P, U])
        self.rstd = ph.sb(f"{name}_rstd", [P, U])
        self.shift = ph.sb(f"{name}_shift", [P, U])
        self.eps = eps
        self.s_stats, self.s_mv, self.s_root, self.s_rstd, self.s_shift, self.s_passed = (
            ph.sem(f"{name}_{x}") for x in ("stats", "mv", "root", "rstd", "shift", "passed"))

    def statistics(self, dve, src, i, first):
        for u in range(U):
            ins = dve.bn_stats(self.stats[:, u, :], src[:, u, :])
        ins.then_inc(self.s_stats, 1)
        gate(dve, self.s_stats, i + 1, self.s_passed)
        for u in range(U):
            ins = dve.bn_aggr(self.mv[:, u, :], self.stats[:, u, :])
        ins.then_inc(self.s_mv, 1)

    def rootof(self, act, i, first):
        act.wait_ge(self.s_mv, i + 1)
        act.activation(self.root[:], self.mv[:, :, 1], ACT.Sqrt, bias=self.eps[:, 0:1]).then_inc(self.s_root, 1)

    def factors(self, dve, i, first):
        dve.wait_ge(self.s_root, i + 1)
        dve.reciprocal(self.rstd[:], self.root[:]).then_inc(self.s_rstd, 1)
        dve.wait_ge(self.s_rstd, i + 1)
        dve.scalar_tensor_tensor(out=self.shift[:], in0=self.mv[:, :, 0], scalar=-1.0, in1=self.rstd[:],
                                 op0=ALU.mult, op1=ALU.mult).then_inc(self.s_shift, 1)

    def apply(self, act, out, src, i, done):
        act.wait_ge(self.s_shift, i + 1)
        for u in range(U):
            ins = act.activation(out[:, u, :], src[:, u, :], ACT.Identity, scale=self.rstd[:, u:u + 1],
                                 bias=self.shift[:, u:u + 1])
        ins.then_inc(done, 1)



def dense_pass(nc, w, tab):
    with Phase(nc, "dense") as ph:
        ident = ph.sb("ident", [P, P])
        wself = ph.sb("wself", [P, C])
        wplus = ph.sb("wplus", [P, C])
        bias = ph.sb("bias", [P, U, C])
        b2 = ph.sb("b2", [P, U, C])
        eps = ph.sb("eps", [P, 1])
        w1 = [ph.sb(f"w1_{l}", [P, 64]) for l in range(3)]
        w2 = [ph.sb(f"w2_{l}", [65, C]) for l in range(3)]
        b1 = ph.sb("b1", [64, 3])
        b2c = ph.sb("b2c", [P, 3])
        x = ph.sb("x", [P, U, C])
        xT = ph.sb("xT", [P, CH])
        u = ph.sb("u", [P, U, C])
        x1 = ph.sb("x1", [P, U, C])
        x2 = ph.sb("x2", [P, U, C])
        hT = [ph.sb(f"hT{l}", [P, CH]) for l in range(3)]
        hid = [ph.sb(f"hid{l}", [65, CH]) for l in range(3)]
        hn = [ph.sb(f"hn{l}", [P, U, C]) for l in range(2)]
        u3 = ph.sb("u3", [P, U, C])
        x3 = ph.sb("x3", [P, U, C])
        u4 = ph.sb("u4", [P, U, C])
        x4 = ph.sb("x4", [P, U, C])
        r2 = {n: ph.sb(n, [P, U]) for n in ("v1", "root1", "rstd1")}
        norm0, norm3, norm4 = (Norm(ph, n, eps) for n in ("norm0", "norm3", "norm4"))
        ps_t, ps_s, ps_t2, ps_hid, ps_h, ps_n = (ph.ps(n) for n in ("ps_t", "ps_s", "ps_t2", "ps_hid", "ps_h", "ps_n"))
        s = {n: ph.sem(n) for n in (
            "weights", "ready", "x_in", "xT_ps", "xT", "s_ps", "u", "x1", "v1", "root1", "rstd1", "x2", "x2T_ps",
            "hT0", "hid_ps0", "hid_ps1", "hid_ps2", "hid0", "hid1", "hid2", "h_ps0", "h_ps1", "h_ps2", "hT1", "hT2",
            "n_ps0", "n_ps1", "hn0", "hn1", "u3", "x3", "u4", "x4", "stored", "passed")}
        block = ph.block()
        groups = NP + 1

        def at(table, g):
            lo = g * CH if not isinstance(g, int) or g < NP else N - CH
            return table[bass.ds(lo, CH), :].rearrange("(p u) c -> p u c", u=U)

        def groups_of(eng, body):
            body(0, True)
            with eng.Fori(1, NP) as g:
                body(g, False)
            body(NP, False)

        @block.sync
        def _(sp):
            loads = [(ident[:], w["ident"]), (wself[:], w["W_self"]), (b1[:], w["nb1"]), (b2c[:], w["nb2"]),
                     (bias[:], w["bias_lang"].rearrange("(a b c) -> a b c", a=1, b=1).to_broadcast([P, U, C])),
                     (b2[:], w["b2"].rearrange("(a b c) -> a b c", a=1, b=1).to_broadcast([P, U, C]))]
            for l in range(3):
                loads += [(w1[l][:], w["nW1"][l, 64:192, :]), (w2[l][0:64, :], w["nW2"][l]),
                          (w2[l][64:65, :], w["nb2_rows"][l:l + 1, :])]
            for dst, src in loads:
                sp.dma_start(dst, src).then_inc(s["weights"], 16)
            sp.wait_ge(s["weights"], 16 * len(loads))

            def body(g, first):
                if not first:
                    sp.wait_ge(s["xT_ps"], g)
                sp.dma_start(x[:], at(w["x"], g)).then_inc(s["x_in"], 16)
            groups_of(sp, body)

        NW = 15

        @block.gpsimd
        def _(pool):
            def body(g, first):
                if isinstance(g, int) and g == NP:
                    pool.wait_ge(s["stored"], 16 * 6 * NP)
                for name, tile, made in (("x1", x1, "x1"), ("x2", x2, "x2"), ("h1", hn[0], "hn0"),
                                         ("h2", hn[1], "hn1"), ("x3", x3, "x3"), ("out", x4, "x4")):
                    gate(pool, s[made], g + 1, s["passed"])
                    pool.dma_start(at(tab[name], g), tile[:]).then_inc(s["stored"], 16)
            groups_of(pool, body)
            pool.wait_ge(s["stored"], 16 * 6 * groups)

        @block.tensor
        def _(pe):
            pe.wait_ge(s["weights"], 16 * NW)
            pe.wait_ge(s["ready"], 1)

            def body(g, first):
                pe.wait_ge(s["x_in"], 16 * (g + 1))
                if not first:
                    pe.wait_ge(s["xT"], g)
                for j in range(U):
                    ins = pe.transpose(slot(ps_t, j), x[:, j, :], ident[:])
                ins.then_inc(s["xT_ps"], 1)
                pe.wait_ge(s["xT"], g + 1)
                if not first:
                    pe.wait_ge(s["u"], g)
                for j in range(U):
                    ins = pe.matmul(ps_s[:, j * C:(j + 1) * C], slot(xT, j), wplus[:], start=True, stop=True)
                ins.then_inc(s["s_ps"], 1)
                pe.wait_ge(s["x2"], g + 1)
                for j in range(U):
                    ins = pe.transpose(slot(ps_t2, j), x2[:, j, :], ident[:])
                ins.then_inc(s["x2T_ps"], 1)
                for l in range(3):
                    pe.wait_ge(s[f"hT{l}"], g + 1)
                    pe.matmul(ps_hid[0:64, :], w1[l][:], hT[l][:], start=True, stop=True).then_inc(s[f"hid_ps{l}"], 1)
                    pe.wait_ge(s[f"hid{l}"], g + 1)
                    if l < 2:
                        pe.matmul(ps_h[:], w2[l][0:64, :], hid[l][0:64, :], start=True, stop=True).then_inc(s[f"h_ps{l}"], 1)
                        pe.wait_ge(s[f"hT{l + 1}"], g + 1)
                        if l == 1:
                            pe.wait_ge(s["hn0"], g + 1)
                        elif not first:
                            pe.wait_ge(s["hn1"], g)
                        for j in range(U):
                            ins = pe.transpose(ps_n[:, j * C:(j + 1) * C], slot(hT[l + 1], j), ident[:])
                        ins.then_inc(s[f"n_ps{l}"], 1)
                    else:
                        for j in range(U):
                            ins = pe.matmul(ps_h[:, j * C:(j + 1) * C], slot(hid[2], j), w2[2][:], start=True, stop=True)
                        ins.then_inc(s["h_ps2"], 1)
            groups_of(pe, body)

        @block.scalar
        def _(act):
            def body(g, first):
                act.wait_ge(s["xT_ps"], g + 1)
                if not first:
                    act.wait_ge(s["s_ps"], g)
                act.copy(xT[:], ps_t[:]).then_inc(s["xT"], 1)
                norm0.rootof(act, g, first)
                if not first:
                    act.wait_ge(s["stored"], 16 * 6 * g)
                norm0.apply(act, x1, u, g, s["x1"])
                act.wait_ge(s["v1"], g + 1)
                act.activation(r2["root1"][:], r2["v1"][:], ACT.Sqrt, bias=eps[:, 0:1]).then_inc(s["root1"], 1)
                act.wait_ge(s["rstd1"], g + 1)
                act.wait_ge(s["x1"], g + 1)
                for j in range(U):
                    ins = act.activation(x2[:, j, :], x1[:, j, :], ACT.Identity, scale=r2["rstd1"][:, j:j + 1])
                ins.then_inc(s["x2"], 1)
                act.wait_ge(s["x2T_ps"], g + 1)
                act.copy(hT[0][:], ps_t2[:]).then_inc(s["hT0"], 1)
                for l in range(3):
                    act.wait_ge(s[f"hid_ps{l}"], g + 1)
                    act.activation(hid[l][0:64, :], ps_hid[0:64, :], ACT.Relu, bias=b1[:, l:l + 1]).then_inc(s[f"hid{l}"], 1)
                    if l < 2:
                        act.wait_ge(s[f"n_ps{l}"], g + 1)
                        act.copy(hn[l][:], ps_n[:].rearrange("p (u c) -> p u c", u=U)).then_inc(s[f"hn{l}"], 1)
                norm3.rootof(act, g, first)
                norm3.apply(act, x3, u3, g, s["x3"])
                norm4.rootof(act, g, first)
                norm4.apply(act, x4, u4, g, s["x4"])
            groups_of(act, body)

        @block.vector
        def _(dve):
            dve.memset(eps[:], EPS)
            for l in range(3):
                dve.memset(hid[l][64:65, :], 1.0)
            dve.wait_ge(s["weights"], 16 * NW)
            dve.tensor_tensor(wplus[:], wself[:], ident[:], ALU.add).then_inc(s["ready"], 1)

            def body(g, first):
                dve.wait_ge(s["s_ps"], g + 1)
                if not first:
                    dve.wait_ge(s["x1"], g)
                dve.tensor_tensor(u[:], ps_s[:].rearrange("p (u c) -> p u c", u=U), bias[:], ALU.add).then_inc(s["u"], 1)
                dve.wait_ge(s["u"], g + 1)
                norm0.statistics(dve, u, g, first)
                norm0.factors(dve, g, first)
                dve.wait_ge(norm0.s_shift, g + 1)
                dve.tensor_tensor(r2["v1"][:], norm0.rstd[:], norm0.rstd[:], ALU.mult).then_inc(s["ready"], 1)
                dve.wait_ge(s["ready"], g + 2)
                dve.tensor_tensor(r2["v1"][:], r2["v1"][:], norm0.mv[:, :, 1], ALU.mult).then_inc(s["v1"], 1)
                dve.wait_ge(s["root1"], g + 1)
                dve.reciprocal(r2["rstd1"][:], r2["root1"][:]).then_inc(s["rstd1"], 1)
                for l in range(2):
                    dve.wait_ge(s[f"h_ps{l}"], g + 1)
                    dve.tensor_scalar(hT[l + 1][:], ps_h[:], b2c[:, l:l + 1], None, ALU.add).then_inc(s[f"hT{l + 1}"], 1)
                dve.wait_ge(s["h_ps2"], g + 1)
                dve.tensor_tensor(u3[:], ps_h[:].rearrange("p (u c) -> p u c", u=U), x2[:], ALU.add).then_inc(s["u3"], 1)
                dve.wait_ge(s["u3"], g + 1)
                norm3.statistics(dve, u3, g, first)
                norm3.factors(dve, g, first)
                dve.wait_ge(s["x3"], g + 1)
                dve.tensor_tensor(u4[:], x3[:], b2[:], ALU.add).then_inc(s["u4"], 1)
                dve.wait_ge(s["u4"], g + 1)
                norm4.statistics(dve, u4, g, first)
                norm4.factors(dve, g, first)
            groups_of(dve, body)



class Stream:

    def __init__(self, ph, name, table, index, ps, after=None):
        self.table, self.flat, self.ps = table, index, ps
        self.index = ph.sb(f"{name}_index", [P, U], I32)
        self.tile = ph.sb(f"{name}_tile", [P, U, C])
        self.s_index, self.s_rows, self.s_turned, self.s_T = (
            ph.sem(f"{name}_{x}") for x in ("index", "rows", "turned", "T"))
        self.T = ph.sb(f"{name}_T", [P, CH])

    def load_index(self, sp, i, first):
        if not first:
            sp.wait_ge(self.s_turned, i)
        sp.dma_start(self.index[:], chunk(self.flat, i)).then_inc(self.s_index, 16)

    def fetch(self, pool, i, first, s_passed):
        if not first:
            gate(pool, self.s_turned, i, s_passed)
        gate(pool, self.s_index, 16 * (i + 1), s_passed)
        for u in range(U):
            gather(pool, self.tile, self.table, self.index, u, self.s_rows)

    def turn(self, pe, i, first, ident, busy=None):
        pe.wait_ge(self.s_rows, 16 * U * (i + 1))
        if busy is not None:
            pe.wait_ge(*busy)
        for u in range(U):
            ins = pe.transpose(slot(self.ps, u), self.tile[:, u, :], ident[:])
        ins.then_inc(self.s_turned, 1)

    def copy_out(self, act, i, first, free=None):
        act.wait_ge(self.s_turned, i + 1)
        if free is not None:
            act.wait_ge(*free)
        act.copy(self.T[:], self.ps[:]).then_inc(self.s_T, 1)


class Put:

    def __init__(self, ph, name, table, index, last_row):
        self.table, self.flat, self.last_row = table, index, last_row
        self.index = ph.sb(f"{name}_index", [P, U], I32)
        self.tile = ph.sb(f"{name}_tile", [P, U, C])
        self.s_index, self.s_made, self.s_put = (ph.sem(f"{name}_{x}") for x in ("index", "made", "put"))

    def load_index(self, sp, i, first):
        if not first:
            sp.wait_ge(self.s_put, 16 * U * i)
        sp.dma_start(self.index[:], chunk(self.flat, i)).then_inc(self.s_index, 16)

    def put(self, pool, i, s_passed):
        gate(pool, self.s_made, i + 1, s_passed)
        gate(pool, self.s_index, 16 * (i + 1), s_passed)
        for u in range(U):
            scatter(pool, self.table, self.tile, self.index, u, self.s_put, self.last_row)

    def free(self, eng, i, first):
        if not first:
            eng.wait_ge(self.s_put, 16 * U * i)


def pool_steps(pool, streams, puts, s_passed, last=lambda pool: None):
    for st in streams:
        st.fetch(pool, 0, True, s_passed)
    with pool.Fori(1, NC) as i:
        for st in streams:
            st.fetch(pool, i, False, s_passed)
        for put in puts:
            put.put(pool, i - 1, s_passed)
    for put in puts:
        put.put(pool, NC - 1, s_passed)
    for put in puts:
        pool.wait_ge(put.s_put, 16 * U * NC)


def edge_attention(nc, w, tab, flat):
    with Phase(nc, "l1") as ph:
        ident = ph.sb("ident", [P, P])
        w23 = ph.sb("w23", [P, 2])
        w3b = ph.sb("w3b", [P, P])
        ones = ph.sb("ones", [P, P])
        eps = ph.sb("eps", [P, 1])
        run = ph.sb("run", [P, CH])
        prod = ph.sb("prod", [P, CH])
        msg = ph.sb("msg", [P, CH])
        agg = ph.sb("agg", [P, CH])
        carry = ph.sb("carry", [P, 1])
        both = ph.sb("both", [P, CH])
        ps_src, ps_dst, ps_att, ps_out = (ph.ps(n) for n in ("ps_src", "ps_dst", "ps_att", "ps_out"))
        src = Stream(ph, "src", tab["x1"], flat["src_d"], ps_src)
        dst = Stream(ph, "dst", tab["x1"], flat["dst_d"], ps_dst)
        put = Put(ph, "x2", tab["x2"], flat["put_d"], N - 1)
        norm = Norm(ph, "norm", eps)
        s = {n: ph.sem(n) for n in ("weights", "ready", "run", "prod", "att", "msg", "agg", "carry", "both", "out",
                                    "passed")}
        block = ph.block()

        @block.sync
        def _(sp):
            sp.dma_start(ident[:], w["ident"]).then_inc(s["weights"], 16)
            sp.dma_start(w23[:], w["l1_w23"]).then_inc(s["weights"], 16)

            def body(i, first):
                src.load_index(sp, i, first)
                dst.load_index(sp, i, first)
                if not first:
                    sp.wait_ge(s["agg"], i)
                sp.dma_start(run[:], rows(flat["run_d"], i)).then_inc(s["run"], 16)
                put.load_index(sp, i, first)
            steps(sp, NC, body)

        @block.gpsimd
        def _(pool):
            pool_steps(pool, (src, dst), (put,), s["passed"])

        @block.tensor
        def _(pe):
            pe.wait_ge(s["weights"], 32)
            pe.wait_ge(s["ready"], 3)

            def body(i, first):
                src.turn(pe, i, first, ident, None if first else (src.s_T, i))
                dst.turn(pe, i, first, ident, None if first else (dst.s_T, i))
                pe.wait_ge(s["prod"], i + 1)
                pe.matmul(ps_att[:], w3b[:], prod[:], start=True, stop=True).then_inc(s["att"], 1)
                pe.wait_ge(s["both"], i + 1)
                if not first:
                    pe.wait_ge(put.s_made, i)
                for u in range(U):
                    ins = pe.transpose(ps_out[:, u * C:(u + 1) * C], slot(both, u), ident[:])
                ins.then_inc(s["out"], 1)
            steps(pe, NC, body)

        @block.scalar
        def _(act):
            def body(i, first):
                src.copy_out(act, i, first, None if first else (s["msg"], i))
                dst.copy_out(act, i, first, None if first else (s["both"], i))
                norm.rootof(act, i, first)
                put.free(act, i, first)
                norm.apply(act, put.tile, ps_out[:].rearrange("p (u c) -> p u c", u=U), i, put.s_made)
            steps(act, NC, body)

        @block.vector
        def _(dve):
            dve.memset(eps[:], EPS)
            dve.memset(carry[:], 0.0)
            dve.memset(ones[:], 1.0).then_inc(s["ready"], 1)
            dve.wait_ge(s["ready"], 1)
            dve.wait_ge(s["weights"], 32)
            dve.tensor_scalar(w3b[:], ones[:], w23[:, 1:2], None, ALU.mult).then_inc(s["ready"], 1)
            dve.wait_ge(s["ready"], 2)
            dve.sem_inc(s["ready"], 1)

            def body(i, first):
                dve.wait_ge(src.s_T, i + 1)
                dve.wait_ge(dst.s_T, i + 1)
                if not first:
                    dve.wait_ge(s["att"], i)
                dve.tensor_tensor(prod[:], src.T[:], dst.T[:], ALU.mult).then_inc(s["prod"], 1)
                dve.wait_ge(s["att"], i + 1)
                if not first:
                    dve.wait_ge(s["carry"], i)
                dve.scalar_tensor_tensor(out=msg[:], in0=src.T[:], scalar=w23[:, 0:1], in1=ps_att[:],
                                         op0=ALU.mult, op1=ALU.mult).then_inc(s["msg"], 1)
                dve.wait_ge(s["msg"], i + 1)
                dve.wait_ge(s["run"], 16 * (i + 1))
                dve.tensor_tensor_scan(agg[:], run[:], msg[:], carry[:, 0:1], ALU.mult, ALU.add).then_inc(s["agg"], 1)
                dve.wait_ge(s["agg"], i + 1)
                dve.tensor_copy(carry[:], agg[:, CH - 1:CH]).then_inc(s["carry"], 1)
                if not first:
                    dve.wait_ge(s["out"], i)
                dve.tensor_tensor(both[:], agg[:], dst.T[:], ALU.add).then_inc(s["both"], 1)
                dve.wait_ge(s["out"], i + 1)
                norm.statistics(dve, ps_out[:].rearrange("p (u c) -> p u c", u=U), i, first)
                norm.factors(dve, i, first)
            steps(dve, NC, body)


def edge_perceptrons(nc, l, w, tab, flat):
    last = l == 2
    with Phase(nc, f"l2_{l}") as ph:
        ident = ph.sb("ident", [P, P])
        e1 = [ph.sb(f"e1_{x}", [P, C]) for x in ("src", "dst")]
        e2 = ph.sb("e2", [P, 64])
        eb1 = ph.sb("eb1", [P, 1])
        eb2 = ph.sb("eb2", [64, 1])
        n1m = ph.sb("n1m", [64, 64])
        n1h = ph.sb("n1h", [P, 64])
        nb1 = ph.sb("nb1", [64, 1])
        n2 = ph.sb("n2", [65, C])
        eps = ph.sb("eps", [P, 1])
        run = ph.sb("run", [64, CH])
        kind = ph.sb("kind", [64, CH])
        inv = ph.sb("inv", [64, CH])
        z = ph.sb("z", [P, CH])
        msg = ph.sb("msg", [64, CH])
        agg = ph.sb("agg", [64, CH])
        carry = ph.sb("carry", [64, 1])
        mean = ph.sb("mean", [64, CH])
        hid = ph.sb("hid", [65, CH])
        ps_src, ps_dst, ps_z, ps_m, ps_hid, ps_out = (
            ph.ps(n) for n in ("ps_src", "ps_dst", "ps_z", "ps_m", "ps_hid", "ps_out"))
        table = tab[("x2", "h1", "h2")[l]]
        src = Stream(ph, "src", table, flat["src_d"], ps_src)
        dst = Stream(ph, "dst", table, flat["dst_d"], ps_dst)
        put = Put(ph, "put", tab[("h1", "h2", "x3")[l]], flat["put_d"], N - 1)
        puts = [put]
        s = {n: ph.sem(n) for n in ("weights", "ready", "masks", "z_ps", "z", "m_ps", "msg", "agg", "carry", "mean",
                                    "hid_ps", "hid", "out", "passed", "pe_passed")}
        if last:
            b2 = ph.sb("b2", [P, U, C])
            res = ph.sb("res_tile", [P, U, C])
            res_index = ph.sb("res_index", [P, U], I32)
            u3 = ph.sb("u3", [P, U, C])
            u4 = ph.sb("u4", [P, U, C])
            s |= {n: ph.sem(n) for n in ("res_index", "res", "u3", "u4")}
            norm3, norm4 = Norm(ph, "norm3", eps), Norm(ph, "norm4", eps)
            put4 = Put(ph, "put4", tab["out"], flat["put_d"], N - 1)
            puts.append(put4)
        block = ph.block()
        loads = [(ident[:], w["ident"]), (e1[0][:], w["eW1"][l, 0]), (e1[1][:], w["eW1"][l, 1]),
                 (eb1[:], w["eb1"][l]), (eb2[:], w["eb2"][l]), (n1m[:], w["nW1"][l, 0:64, :]),
                 (n1h[:], w["nW1"][l, 64:192, :]), (nb1[:], w["nb1_cols"][l]), (n2[0:64, :], w["nW2"][l]),
                 (n2[64:65, :], w["nb2_rows"][l:l + 1, :])]
        late = [(e2[0:64, 0:32], w["eW2"][l, 0]), (e2[64:128, 32:64], w["eW2"][l, 1])]
        if last:
            loads.append((b2[:], w["b2"].rearrange("(a b c) -> a b c", a=1, b=1).to_broadcast([P, U, C])))
        NW = 16 * (len(loads) + len(late))

        @block.sync
        def _(sp):
            for d, f in loads:
                sp.dma_start(d, f).then_inc(s["weights"], 16)
            sp.wait_ge(s["ready"], 1)
            for d, f in late:
                sp.dma_start(d, f).then_inc(s["weights"], 16)

            def body(i, first):
                src.load_index(sp, i, first)
                dst.load_index(sp, i, first)
                if not first:
                    sp.wait_ge(s["mean"], i)
                sp.dma_start(run[:], rows(flat["run_d"], i, 64)).then_inc(s["masks"], 16)
                for q in range(2):
                    sp.dma_start(kind[32 * q:32 * q + 32, :], rows(flat[f"kind{q}_d"], i, 32)).then_inc(s["masks"], 16)
                    sp.dma_start(inv[32 * q:32 * q + 32, :], rows(flat[f"inv{q}_d"], i, 32)).then_inc(s["masks"], 16)
                for p in puts:
                    p.load_index(sp, i, first)
                if last:
                    if not first:
                        sp.wait_ge(s["u3"], i)
                    sp.dma_start(res_index[:], chunk(flat["dst_d"], i)).then_inc(s["res_index"], 16)
            steps(sp, NC, body)

        @block.gpsimd
        def _(pool):
            if not last:
                pool_steps(pool, (src, dst), puts, s["passed"])
                return

            def residual(i, first):
                if not first:
                    gate(pool, s["u3"], i, s["passed"])
                gate(pool, s["res_index"], 16 * (i + 1), s["passed"])
                for u in range(U):
                    gather(pool, res, tab["x2"], res_index, u, s["res"])
            src.fetch(pool, 0, True, s["passed"])
            dst.fetch(pool, 0, True, s["passed"])
            residual(0, True)
            with pool.Fori(1, NC) as i:
                src.fetch(pool, i, False, s["passed"])
                dst.fetch(pool, i, False, s["passed"])
                for p in puts:
                    p.put(pool, i - 1, s["passed"])
                residual(i, False)
            for p in puts:
                p.put(pool, NC - 1, s["passed"])
            for p in puts:
                pool.wait_ge(p.s_put, 16 * U * NC)

        @block.tensor
        def _(pe):
            pe.wait_ge(s["weights"], NW)
            pe.wait_ge(s["ready"], 1)

            def body(i, first):
                src.turn(pe, i, first, ident, None if first else (src.s_T, i))
                dst.turn(pe, i, first, ident, None if first else (dst.s_T, i))
                pe.wait_ge(src.s_T, i + 1)
                if not first:
                    pe.wait_ge(s["z"], i)
                pe.matmul(ps_z[:], e1[0][:], src.T[:], start=True, stop=False)
                pe.wait_ge(dst.s_T, i + 1)
                pe.matmul(ps_z[:], e1[1][:], dst.T[:], start=False, stop=True).then_inc(s["z_ps"], 1)
                pe.wait_ge(s["z"], i + 1)
                if not first:
                    pe.wait_ge(s["msg"], i)
                pe.matmul(ps_m[0:64, :], e2[:], z[:], start=True, stop=True).then_inc(s["m_ps"], 1)
                if not first:
                    pe.wait_ge(s["hid"], i)
                pe.matmul(ps_hid[0:64, :], n1h[:], dst.T[:], start=True, stop=False)
                gate(pe, s["mean"], i + 1, s["pe_passed"])
                pe.matmul(ps_hid[0:64, :], n1m[:], mean[:], start=False, stop=True).then_inc(s["hid_ps"], 1)
                pe.wait_ge(s["hid"], i + 1)
                if not first:
                    pe.wait_ge(s["u3"] if last else put.s_made, i)
                for u in range(U):
                    ins = pe.matmul(ps_out[:, u * C:(u + 1) * C], slot(hid, u), n2[:], start=True, stop=True)
                ins.then_inc(s["out"], 1)
            steps(pe, NC, body)

        @block.scalar
        def _(act):
            def body(i, first):
                src.copy_out(act, i, first, None if first else (s["z_ps"], i))
                dst.copy_out(act, i, first, None if first else (s["hid_ps"], i))
                act.wait_ge(s["z_ps"], i + 1)
                if not first:
                    act.wait_ge(s["m_ps"], i)
                act.activation(z[:], ps_z[:], ACT.Relu, bias=eb1[:, 0:1]).then_inc(s["z"], 1)
                act.wait_ge(s["hid_ps"], i + 1)
                if not first:
                    act.wait_ge(s["out"], i)
                act.activation(hid[0:64, :], ps_hid[0:64, :], ACT.Relu, bias=nb1[:, 0:1]).then_inc(s["hid"], 1)
                if last:
                    norm3.rootof(act, i, first)
                    put.free(act, i, first)
                    norm3.apply(act, put.tile, u3, i, put.s_made)
                    norm4.rootof(act, i, first)
                    put4.free(act, i, first)
                    norm4.apply(act, put4.tile, u4, i, put4.s_made)
                else:
                    act.wait_ge(s["out"], i + 1)
                    put.free(act, i, first)
                    act.copy(put.tile[:], ps_out[:].rearrange("p (u c) -> p u c", u=U)).then_inc(put.s_made, 1)
            steps(act, NC, body)

        @block.vector
        def _(dve):
            dve.memset(e2[:], 0.0)
            dve.memset(eps[:], EPS)
            dve.memset(hid[64:65, :], 1.0)
            dve.memset(carry[:], 0.0).then_inc(s["ready"], 1)
            dve.wait_ge(s["weights"], NW)
            dve.wait_ge(s["ready"], 1)

            def body(i, first):
                dve.wait_ge(s["m_ps"], i + 1)
                dve.wait_ge(s["masks"], 80 * (i + 1))
                dve.scalar_tensor_tensor(out=msg[:], in0=ps_m[0:64, :], scalar=eb2[:, 0:1], in1=kind[:],
                                         op0=ALU.add, op1=ALU.mult).then_inc(s["msg"], 1)
                dve.wait_ge(s["msg"], i + 1)
                if not first:
                    dve.wait_ge(s["carry"], i)
                dve.tensor_tensor_scan(agg[:], run[:], msg[:], carry[:, 0:1], ALU.mult, ALU.add).then_inc(s["agg"], 1)
                dve.wait_ge(s["agg"], i + 1)
                dve.tensor_copy(carry[:], agg[:, CH - 1:CH]).then_inc(s["carry"], 1)
                if not first:
                    dve.wait_ge(s["hid_ps"], i)
                dve.tensor_tensor(mean[:], agg[:], inv[:], ALU.mult).then_inc(s["mean"], 1)
                if last:
                    dve.wait_ge(s["out"], i + 1)
                    dve.wait_ge(s["res"], 16 * U * (i + 1))
                    if not first:
                        dve.wait_ge(put.s_made, i)
                    dve.tensor_tensor(u3[:], ps_out[:].rearrange("p (u c) -> p u c", u=U), res[:], ALU.add
                                      ).then_inc(s["u3"], 1)
                    dve.wait_ge(s["u3"], i + 1)
                    norm3.statistics(dve, u3, i, first)
                    norm3.factors(dve, i, first)
                    dve.wait_ge(put.s_made, i + 1)
                    if not first:
                        dve.wait_ge(put4.s_made, i)
                    dve.tensor_tensor(u4[:], put.tile[:], b2[:], ALU.add).then_inc(s["u4"], 1)
                    dve.wait_ge(s["u4"], i + 1)
                    norm4.statistics(dve, u4, i, first)
                    norm4.factors(dve, i, first)
            steps(dve, NC, body)


def hyper_edges(nc, name, source, w_name, target, w, flat, affine=None):
    with Phase(nc, name) as ph:
        ident = ph.sb("ident", [P, P])
        wt = ph.sb("wt", [P, C])
        ac = ph.sb("ac", [P, 2])
        run = ph.sb("run", [P, CH])
        inv = ph.sb("inv", [P, CH])
        agg = ph.sb("agg", [P, CH])
        carry = ph.sb("carry", [P, 1])
        mean = ph.sb("mean", [P, CH])
        zero = ph.sb("zero", [1, C])
        ps_src, ps_out = ph.ps("ps_src"), ph.ps("ps_out")
        src = Stream(ph, "src", source, flat["src_d"], ps_src)
        put = Put(ph, "put", target, flat["put_d"], H5 - 1)
        s = {n: ph.sem(n) for n in ("weights", "ready", "masks", "agg", "carry", "mean", "aff", "out", "passed",
                                    "zeroed")}
        block = ph.block()

        @block.sync
        def _(sp):
            sp.dma_start(ident[:], w["ident"]).then_inc(s["weights"], 16)
            sp.dma_start(wt[:], w[w_name]).then_inc(s["weights"], 16)
            if affine is not None:
                sp.dma_start(ac[:], affine).then_inc(s["weights"], 16)
            sp.wait_ge(s["ready"], 1)
            sp.dma_start(target[H5 - 1:H5, :], zero[:]).then_inc(s["zeroed"], 16)

            def body(i, first):
                src.load_index(sp, i, first)
                if not first:
                    sp.wait_ge(s["mean"], i)
                sp.dma_start(run[:], rows(flat["run_d"], i)).then_inc(s["masks"], 16)
                sp.dma_start(inv[:], rows(flat["inv_deg_d"], i)).then_inc(s["masks"], 16)
                put.load_index(sp, i, first)
            steps(sp, NC, body)

        @block.gpsimd
        def _(pool):
            gate(pool, s["zeroed"], 16, s["passed"])
            pool_steps(pool, (src,), (put,), s["passed"])

        NW = 32 if affine is None else 48

        @block.tensor
        def _(pe):
            pe.wait_ge(s["weights"], NW)

            def body(i, first):
                src.turn(pe, i, first, ident, None if first else (s["agg"], i))
                made = s["mean"] if affine is None else s["aff"]
                pe.wait_ge(made, i + 1)
                if not first:
                    pe.wait_ge(put.s_made, i)
                for u in range(U):
                    ins = pe.matmul(ps_out[:, u * C:(u + 1) * C], slot(mean, u), wt[:], start=True, stop=True)
                ins.then_inc(s["out"], 1)
            steps(pe, NC, body)

        @block.scalar
        def _(act):
            act.wait_ge(s["weights"], NW)

            def body(i, first):
                if affine is not None:
                    act.wait_ge(s["mean"], i + 1)
                    act.activation(mean[:], mean[:], ACT.Identity, scale=ac[:, 0:1], bias=ac[:, 1:2]).then_inc(s["aff"], 1)
                act.wait_ge(s["out"], i + 1)
                put.free(act, i, first)
                act.copy(put.tile[:], ps_out[:].rearrange("p (u c) -> p u c", u=U)).then_inc(put.s_made, 1)
            steps(act, NC, body)

        @block.vector
        def _(dve):
            dve.memset(carry[:], 0.0)
            dve.memset(zero[:], 0.0).then_inc(s["ready"], 1)
            dve.wait_ge(s["ready"], 1)

            def body(i, first):
                dve.wait_ge(src.s_turned, i + 1)
                dve.wait_ge(s["masks"], 32 * (i + 1))
                if not first:
                    dve.wait_ge(s["carry"], i)
                dve.tensor_tensor_scan(agg[:], run[:], ps_src[:], carry[:, 0:1], ALU.mult, ALU.add).then_inc(s["agg"], 1)
                dve.wait_ge(s["agg"], i + 1)
                dve.tensor_copy(carry[:], agg[:, CH - 1:CH]).then_inc(s["carry"], 1)
                if not first:
                    dve.wait_ge(s["out"], i)
                dve.tensor_tensor(mean[:], agg[:], inv[:], ALU.mult).then_inc(s["mean"], 1)
            steps(dve, NC, body)


def nodes_of_edges(nc, name, source, target, w, tab, flat, affine):
    final = target is None
    with Phase(nc, name) as ph:
        ident = ph.sb("ident", [P, P])
        run = ph.sb("run", [P, CH])
        inv = ph.sb("inv", [P, CH])
        agg = ph.sb("agg", [P, CH])
        carry = ph.sb("carry", [P, 1])
        g = ph.sb("g", [P, CH])
        ps_src, ps_out = ph.ps("ps_src"), ph.ps("ps_out")
        src = Stream(ph, "src", source, flat["dst_s"], ps_src)
        put = Put(ph, "put", tab["out"] if final else target, flat["put_s"], N - 1)
        s = {n: ph.sem(n) for n in ("weights", "ready", "masks", "agg", "carry", "g", "out", "passed",
                                    "gl", "bn", "step", "affine", "stats")}
        eps = ph.sb("eps", [P, 1])
        if final:
            b2 = ph.sb("b2", [P, U, C])
            res = Stream(ph, "res", tab["x3"], flat["src_s"], None)
            res.s_turned = ph.sem("res_used")
            resb = ph.sb("resb", [P, U, C])
            u4 = ph.sb("u4", [P, U, C])
            norm = Norm(ph, "norm", eps)
            s |= {n: ph.sem(n) for n in ("resb", "u4")}
        else:
            last = ph.sb("last", [P, CH])
            gl = ph.sb("gl", [P, CH])
            stats = ph.sb("stats", [P, NC, 6])
            gb = ph.sb("gb", [P, 2])
            mv = ph.sb("mv", [P, 2])
            t = {n: ph.sb(n, [P, 1]) for n in ("mean", "sq", "var", "var2", "root", "rstd", "am")}
            ac = ph.sb("ac", [P, 2])
        block = ph.block()

        @block.sync
        def _(sp):
            sp.dma_start(ident[:], w["ident"]).then_inc(s["weights"], 16)
            if final:
                sp.dma_start(b2[:], w["b2"].rearrange("(a b c) -> a b c", a=1, b=1).to_broadcast([P, U, C])
                             ).then_inc(s["weights"], 16)
            else:
                sp.dma_start(gb[:], w["gamma_beta"]).then_inc(s["weights"], 16)

            def body(i, first):
                src.load_index(sp, i, first)
                if final:
                    res.load_index(sp, i, first)
                if not first:
                    sp.wait_ge(s["g"] if final else s["gl"], i)
                sp.dma_start(run[:], rows(flat["run_s"], i)).then_inc(s["masks"], 16)
                sp.dma_start(inv[:], rows(flat["inv_w_s"], i)).then_inc(s["masks"], 16)
                if not final:
                    sp.dma_start(last[:], rows(flat["last_s"], i)).then_inc(s["masks"], 16)
                put.load_index(sp, i, first)
            steps(sp, NC, body)
            if not final:
                sp.wait_ge(s["bn"], 1)
                sp.dma_start(affine, ac[:]).then_inc(s["affine"], 16)
                sp.wait_ge(s["affine"], 16)

        @block.gpsimd
        def _(pool):
            pool_steps(pool, (src, res) if final else (src,), (put,), s["passed"])

        @block.tensor
        def _(pe):
            pe.wait_ge(s["weights"], 32)

            def body(i, first):
                src.turn(pe, i, first, ident, None if first else (s["agg"], i))
                pe.wait_ge(s["g"], i + 1)
                if not first:
                    pe.wait_ge(s["u4"] if final else put.s_made, i)
                for u in range(U):
                    ins = pe.transpose(ps_out[:, u * C:(u + 1) * C], slot(g, u), ident[:])
                ins.then_inc(s["out"], 1)
            steps(pe, NC, body)

        @block.scalar
        def _(act):
            def body(i, first):
                if final:
                    norm.rootof(act, i, first)
                    put.free(act, i, first)
                    norm.apply(act, put.tile, u4, i, put.s_made)
                else:
                    act.wait_ge(s["out"], i + 1)
                    put.free(act, i, first)
                    act.copy(put.tile[:], ps_out[:].rearrange("p (u c) -> p u c", u=U)).then_inc(put.s_made, 1)
            steps(act, NC, body)
            if not final:
                act.wait_ge(s["step"], 5)
                act.activation(t["root"][:], t["var2"][:], ACT.Sqrt, bias=eps[:, 0:1]).then_inc(s["step"], 1)

        @block.vector
        def _(dve):
            dve.memset(eps[:], EPS)
            dve.memset(carry[:], 0.0)
            dve.memset(g[:], 0.0).then_inc(s["ready"], 1)
            dve.wait_ge(s["ready"], 1)
            dve.wait_ge(s["weights"], 32)

            def body(i, first):
                dve.wait_ge(src.s_turned, i + 1)
                dve.wait_ge(s["masks"], (32 if final else 48) * (i + 1))
                if not first:
                    dve.wait_ge(s["carry"], i)
                dve.tensor_tensor_scan(agg[:], run[:], ps_src[:], carry[:, 0:1], ALU.mult, ALU.add).then_inc(s["agg"], 1)
                dve.wait_ge(s["agg"], i + 1)
                dve.tensor_copy(carry[:], agg[:, CH - 1:CH]).then_inc(s["carry"], 1)
                if not first:
                    dve.wait_ge(s["out"], i)
                dve.tensor_tensor(g[:], agg[:], inv[:], ALU.mult).then_inc(s["g"], 1)
                if final:
                    dve.wait_ge(res.s_rows, 16 * U * (i + 1))
                    dve.tensor_tensor(resb[:], res.tile[:], b2[:], ALU.add).then_inc(res.s_turned, 1)
                    dve.wait_ge(res.s_turned, i + 1)
                    dve.wait_ge(s["out"], i + 1)
                    if not first:
                        dve.wait_ge(put.s_made, i)
                    dve.tensor_tensor(u4[:], ps_out[:].rearrange("p (u c) -> p u c", u=U), resb[:], ALU.add
                                      ).then_inc(s["u4"], 1)
                    dve.wait_ge(s["u4"], i + 1)
                    norm.statistics(dve, u4, i, first)
                    norm.factors(dve, i, first)
                else:
                    dve.wait_ge(s["g"], i + 1)
                    dve.tensor_tensor(gl[:], g[:], last[:], ALU.mult).then_inc(s["gl"], 1)
                    dve.wait_ge(s["gl"], i + 1)
                    dve.bn_stats(stats[:, bass.ds(i, 1), :].rearrange("p a f -> p (a f)"), gl[:]
                                 ).then_inc(s["stats"], 1)
                    dve.wait_ge(s["stats"], i + 1)
            steps(dve, NC, body)
            if not final:
                dve.bn_aggr(mv[:], stats[:].rearrange("p n f -> p (n f)")).then_inc(s["step"], 1)
                dve.wait_ge(s["step"], 1)
                dve.tensor_scalar(t["mean"][:], mv[:, 0:1], EP / N, None, ALU.mult)
                dve.tensor_tensor(t["sq"][:], mv[:, 0:1], mv[:, 0:1], ALU.mult).then_inc(s["step"], 1)
                dve.wait_ge(s["step"], 2)
                dve.tensor_scalar(t["sq"][:], t["sq"][:], (EP / N) * ((N - EP) / N), None, ALU.mult).then_inc(s["step"], 1)
                dve.wait_ge(s["step"], 3)
                dve.tensor_scalar(t["var"][:], mv[:, 1:2], EP / N, None, ALU.mult).then_inc(s["step"], 1)
                dve.wait_ge(s["step"], 4)
                dve.tensor_tensor(t["var2"][:], t["var"][:], t["sq"][:], ALU.add).then_inc(s["step"], 1)
                dve.wait_ge(s["step"], 6)
                dve.reciprocal(t["rstd"][:], t["root"][:]).then_inc(s["step"], 1)
                dve.wait_ge(s["step"], 7)
                dve.tensor_tensor(ac[:, 0:1], t["rstd"][:], gb[:, 0:1], ALU.mult).then_inc(s["step"], 1)
                dve.wait_ge(s["step"], 8)
                dve.tensor_tensor(t["am"][:], ac[:, 0:1], t["mean"][:], ALU.mult).then_inc(s["step"], 1)
                dve.wait_ge(s["step"], 9)
                dve.tensor_tensor(ac[:, 1:2], gb[:, 1:2], t["am"][:], ALU.subtract).then_inc(s["bn"], 1)


def fold_attention(nc, w, att):
    with Phase(nc, "fold") as ph:
        wrt = ph.sb("wrt", [P, R, C])
        wct = ph.sb("wct", [P, C])
        wst = ph.sb("wst", [P, C])
        vec = ph.sb("vec", [P, 2 * R + 2])
        heads = ph.sb("heads", [P, H])
        blocks = ph.sb("blocks", [P, 2 * R + 2, H])
        ps = ph.ps("ps")
        s = {n: ph.sem(n) for n in ("weights", "blocks", "ps", "done")}
        block = ph.block()

        @block.sync
        def _(sp):
            for d, f in ((wrt, "W_rel_T"), (wct, "W_cross_T"), (wst, "W_self_T"), (vec, "att_vectors"), (heads, "heads")):
                sp.dma_start(d[:], w[f]).then_inc(s["weights"], 16)

        @block.vector
        def _(dve):
            dve.wait_ge(s["weights"], 80)
            for q in range(2 * R + 2):
                ins = dve.tensor_scalar(blocks[:, q, :], heads[:], vec[:, q:q + 1], None, ALU.mult)
            ins.then_inc(s["blocks"], 1)
            dve.wait_ge(s["ps"], 1)
            dve.tensor_copy(att[:], ps[:, 0:11 * H]).then_inc(s["done"], 1)
            dve.wait_ge(s["done"], 1)

        @block.tensor
        def _(pe):
            pe.wait_ge(s["blocks"], 1)
            at = 0
            for q in range(2 * R):
                pe.matmul(ps[:, at:at + H], wrt[:, q % R, :], blocks[:, q, :], start=True, stop=True)
                at += H
            for m, q in ((wct, 2 * R), (wst, 2 * R), (wst, 2 * R + 1)):
                ins = pe.matmul(ps[:, at:at + H], m[:], blocks[:, q, :], start=True, stop=True)
                at += H
            ins.then_inc(s["ps"], 1)


def relational_attention(nc, w, tab, flat, att):
    RH = R * H
    K = R + 1
    with Phase(nc, "l0") as ph:
        ident = ph.sb("ident", [P, P])
        wrel = ph.sb("wrel", [P, R, C])
        wcross = ph.sb("wcross", [P, C])
        wself = ph.sb("wself", [P, C])
        spread = ph.sb("spread", [RH, R, C])
        brel = ph.sb("brel", [P, R])
        rid = ph.sb("rid", [RH, 1])
        bias = ph.sb("bias", [P, U, C])
        eps = ph.sb("eps", [P, 1])
        run = ph.sb("run", [P, CH])
        rel = ph.sb("rel", [RH, CH])
        small = {n: ph.sb(n, [RH, CH]) for n in ("lk", "lk2", "m4", "neg", "reset", "lm", "lm2", "d1", "d2", "e",
                                                 "c", "pe", "p", "rd")}
        mbuf = ph.sb("mbuf", [RH, CH + 1])
        den = ph.sb("den", [RH, CH])
        dcarry = ph.sb("dcarry", [RH, 1])
        denT = ph.sb("denT", [P, U, RH])
        has = ph.sb("has", [P, U, RH])
        hneg = ph.sb("hneg", [P, U, RH])
        dmax = ph.sb("dmax", [P, U, RH])
        rdT = ph.sb("rdT", [P, U, RH])
        y = ph.sb("y", [P, CH])
        py = ph.sb("py", [P, CH])
        num = [ph.sb(f"num{r}", [P, CH]) for r in range(R)]
        ncarry = ph.sb("ncarry", [P, R])
        ro = ph.sb("ro", [P, CH])
        g = ph.sb("g", [P, CH])
        ent = ph.sb("ent", [P, U, K, C])
        lg = {n: ph.sb(n, [P, U, K, H]) for n in ("lg0", "lg1", "lg2", "lg3", "lge", "alpha")}
        ld = ph.sb("ld", [P, U, H])
        mx = ph.sb("mx", [P, U, H])
        sm = ph.sb("sm", [P, U, H])
        rs = ph.sb("rs", [P, U, H])
        mixed = ph.sb("mixed", [P, U, K, C])
        outc = ph.sb("outc", [P, U, C])
        outb = ph.sb("outb", [P, U, C])
        u0 = ph.sb("u0", [P, U, C])
        ps_x, ps_l, ps_a, ps_y, ps_p, ps_c, ps_q, ps_h = (
            ph.ps(n) for n in ("ps_x", "ps_l", "ps_a", "ps_y", "ps_p", "ps_c", "ps_q", "ps_h"))
        src = Stream(ph, "src", tab["x"], flat["src_d"], ps_x)
        dst = Stream(ph, "dst", tab["x"], flat["dst_d"], ps_x)
        put = Put(ph, "put", tab["x1"], flat["put_d"], N - 1)
        norm = Norm(ph, "norm", eps)
        names = ["weights", "ready", "masks", "logit", "lk", "lk2", "m4", "reset", "lm", "lm2", "m", "mshift", "d1",
                 "d2", "e", "c", "p", "den", "dcarry", "denT_ps", "denT", "dmax", "rdT", "rd_ps", "rd", "hd_ps",
                 "ld", "lg0", "lg1", "lg2", "lg3", "lg4", "mx", "lg5", "lge", "sm", "rs", "alpha", "mixed", "outc",
                 "x_ps", "outb", "u0", "passed", "ent0", "ent_ps0", "pe_passed"]
        names += [f"{n}{r}" for r in range(R) for n in ("y_ps", "y", "py", "num", "ro", "g", "h_ps", "ent_r")]
        s = {n: ph.sem(n) for n in names}
        block = ph.block()
        loads = [(ident[:], w["ident"]), (wrel[:], w["W_rel"]), (wcross[:], w["W_cross"]), (wself[:], w["W_self"]),
                 (spread[:], w["spread"]), (brel[:], w["bias_rel"]), (rid[:], w["rid"]),
                 (bias[:], w["bias_lang"].rearrange("(a b c) -> a b c", a=1, b=1).to_broadcast([P, U, C]))]
        NW = 16 * len(loads)
        ps_dT = ps_a[:, 0:U * RH].rearrange("p (u x) -> p u x", u=U)
        ps_lg = ps_a[:, U * RH:U * (RH + K * H + H)].rearrange("p (u k h) -> p u k h", u=U, k=K + 1)

        @block.sync
        def _(sp):
            for d, f in loads:
                sp.dma_start(d, f).then_inc(s["weights"], 16)

            def body(i, first):
                src.load_index(sp, i, first)
                dst.load_index(sp, i, first)
                if not first:
                    sp.wait_ge(s["reset"], i)
                    sp.wait_ge(s["m4"], i)
                sp.dma_start(run[0:RH, :], rows(flat["run_d"], i, RH)).then_inc(s["masks"], 16)
                sp.dma_start(rel[:], rows(flat["rel_d"], i, RH)).then_inc(s["masks"], 16)
                put.load_index(sp, i, first)
            steps(sp, NC, body)

        @block.gpsimd
        def _(pool):
            pool_steps(pool, (src, dst), (put,), s["passed"])

        @block.tensor
        def _(pe):
            pe.wait_ge(s["weights"], NW)

            def body(i, first):
                src.turn(pe, i, first, ident, None if first else (dst.s_T, i))
                dst.turn(pe, i, first, ident, (src.s_T, i + 1))
                pe.wait_ge(dst.s_T, i + 1)
                if not first:
                    pe.wait_ge(s["rd"], i)
                pe.matmul(ps_l[0:RH, :], att[:, 0:RH], src.T[:], start=True, stop=False)
                pe.matmul(ps_l[0:RH, :], att[:, RH:2 * RH], dst.T[:], start=False, stop=True).then_inc(s["logit"], 1)
                if not first:
                    pe.wait_ge(s["u0"], i)
                for u in range(U):
                    ins = pe.matmul(ps_h[:, u * C:(u + 1) * C], slot(dst.T, u), wself[:], start=True, stop=True)
                ins.then_inc(s["ent_ps0"], 1)
                if not first:
                    pe.wait_ge(s["lg0"], i)
                gate(pe, s["den"], i + 1, s["pe_passed"])
                for u in range(U):
                    ins = pe.transpose(ps_dT[:, u, :], slot(den, u), ident[0:RH, 0:RH])
                ins.then_inc(s["denT_ps"], 1)
                pe.wait_ge(s["rdT"], i + 1)
                for u in range(U):
                    ins = pe.transpose(slot(ps_l[0:RH], u), rdT[:, u, :], ident[:])
                ins.then_inc(s["rd_ps"], 1)
                pe.wait_ge(s["ent0"], i + 1)
                for u in range(U):
                    pe.matmul(ps_lg[:, u, 0, :], slot(dst.T, u), att[:, 9 * H:10 * H], start=True, stop=True)
                    ins = pe.matmul(ps_lg[:, u, K, :], slot(dst.T, u), att[:, 10 * H:11 * H], start=True, stop=True)
                for r in range(R):
                    if r:
                        pe.wait_ge(s[f"y{r - 1}"], i + 1)
                        pe.wait_ge(s[f"py{r - 1}"], i + 1)
                        pe.wait_ge(s[f"num{r - 1}"], i + 1)
                        pe.wait_ge(s[f"ro{r - 1}"], i + 1)
                    elif not first:
                        pe.wait_ge(s[f"ro{R - 1}"], i)
                    pe.matmul(ps_y[:], wrel[:, r, :], src.T[:], start=True, stop=True).then_inc(s[f"y_ps{r}"], 1)
                    pe.wait_ge(s["p"], i + 1)
                    pe.wait_ge(s["rd"], i + 1)
                    pe.matmul(ps_p[:], spread[:, r, :], small["p"][:], start=True, stop=True)
                    pe.matmul(ps_c[:], spread[:, r, :], small["c"][:], start=True, stop=True)
                    pe.matmul(ps_q[:], spread[:, r, :], small["rd"][:], start=True, stop=True).then_inc(s[f"h_ps{r}"], 1)
                    pe.wait_ge(s[f"g{r}"], i + 1)
                    pe.wait_ge(s["ent0"] if r == 0 else s[f"ent_r{r - 1}"], i + 1)
                    for u in range(U):
                        pe.matmul(ps_h[:, u * C:(u + 1) * C], slot(g, u), wcross[:], start=True, stop=True)
                        ins = pe.matmul(ps_lg[:, u, r + 1, :], slot(g, u), att[:, 8 * H:9 * H], start=True, stop=True)
                    ins.then_inc(s[f"y_ps{r}"], 1)
                pe.wait_ge(s[f"ent_r{R - 1}"], i + 1)
                for u in range(U):
                    ins = pe.transpose(ps_h[:, u * C:(u + 1) * C], slot(dst.T, u), ident[:])
                ins.then_inc(s["x_ps"], 1)
            steps(pe, NC, body)

        @block.scalar
        def _(act):
            act.wait_ge(s["weights"], NW)

            def body(i, first):
                src.copy_out(act, i, first, None if first else (s["x_ps"], i))
                dst.copy_out(act, i, first, None if first else (s["x_ps"], i))
                if not first:
                    act.wait_ge(s["mixed"], i)
                act.wait_ge(s["ent_ps0"], i + 1)
                act.copy(ent[:, :, 0, :], ps_h[:].rearrange("p (u c) -> p u c", u=U)).then_inc(s["ent0"], 1)
                act.wait_ge(s["d2"], i + 1)
                act.activation(small["c"][:], small["d2"][:], ACT.Exp)
                act.wait_ge(s["e"], i + 1)
                act.activation(small["pe"][:], small["e"][:], ACT.Exp).then_inc(s["c"], 1)
                act.wait_ge(s["rd_ps"], i + 1)
                act.copy(small["rd"][:], ps_l[0:RH, :]).then_inc(s["rd"], 1)
                for r in range(R):
                    act.wait_ge(s[f"y_ps{r}"], 2 * i + 1)
                    if r:
                        act.wait_ge(s[f"py{r - 1}"], i + 1)
                    elif not first:
                        act.wait_ge(s[f"py{R - 1}"], i)
                    act.copy(y[:], ps_y[:]).then_inc(s[f"y{r}"], 1)
                    act.wait_ge(s[f"ro{r}"], i + 1)
                    act.activation(g[:], ro[:], ACT.Gelu, bias=brel[:, r:r + 1]).then_inc(s[f"g{r}"], 1)
                    act.wait_ge(s[f"y_ps{r}"], 2 * i + 2)
                    act.copy(ent[:, :, r + 1, :], ps_h[:].rearrange("p (u c) -> p u c", u=U)).then_inc(s[f"ent_r{r}"], 1)
                act.wait_ge(s["lg5"], i + 1)
                act.activation(lg["lge"][:], lg["lg2"][:], ACT.Exp).then_inc(s["lge"], 1)
                norm.rootof(act, i, first)
                put.free(act, i, first)
                norm.apply(act, put.tile, u0, i, put.s_made)
            steps(act, NC, body)

        @block.vector
        def _(dve):
            dve.memset(eps[:], EPS)
            dve.memset(mbuf[:], -NEG)
            dve.memset(dcarry[:], 0.0)
            dve.memset(ncarry[:], 0.0).then_inc(s["ready"], 1)
            dve.wait_ge(s["weights"], NW)
            dve.wait_ge(s["ready"], 1)
            q = small

            def body(i, first):
                dve.wait_ge(s["masks"], 32 * (i + 1))
                dve.tensor_scalar(q["m4"][:], rel[:], rid[:, 0:1], None, ALU.is_equal).then_inc(s["m4"], 1)
                dve.tensor_scalar(q["reset"][:], run[0:RH, :], -1.0, MASKED, ALU.add, ALU.mult).then_inc(s["reset"], 1)
                dve.wait_ge(s["logit"], i + 1)
                dve.tensor_scalar(q["lk"][:], ps_l[0:RH, :], LEAK, None, ALU.mult).then_inc(s["lk"], 1)
                dve.wait_ge(s["lk"], i + 1)
                dve.wait_ge(s["m4"], i + 1)
                dve.tensor_tensor(q["lk2"][:], ps_l[0:RH, :], q["lk"][:], ALU.max)
                dve.tensor_scalar(q["neg"][:], q["m4"][:], -1.0, NEG, ALU.add, ALU.mult).then_inc(s["lk2"], 1)
                dve.wait_ge(s["lk2"], i + 1)
                dve.tensor_tensor(q["lm"][:], q["lk2"][:], q["m4"][:], ALU.mult).then_inc(s["lm"], 1)
                dve.wait_ge(s["lm"], i + 1)
                dve.tensor_tensor(q["lm2"][:], q["lm"][:], q["neg"][:], ALU.add).then_inc(s["lm2"], 1)
                dve.wait_ge(s["lm2"], i + 1)
                dve.wait_ge(s["reset"], i + 1)
                dve.tensor_tensor_scan(mbuf[:, 1:CH + 1], q["reset"][:], q["lm2"][:], mbuf[:, 0:1], ALU.add, ALU.max
                                       ).then_inc(s["m"], 1)
                dve.wait_ge(s["m"], i + 1)
                dve.tensor_tensor(q["d1"][:], mbuf[:, 0:CH], q["reset"][:], ALU.add).then_inc(s["d1"], 1)
                dve.wait_ge(s["d1"], i + 1)
                if not first:
                    dve.wait_ge(s["c"], i)
                dve.tensor_tensor(q["d2"][:], q["d1"][:], mbuf[:, 1:CH + 1], ALU.subtract).then_inc(s["d2"], 1)
                dve.tensor_tensor(q["e"][:], q["lm2"][:], mbuf[:, 1:CH + 1], ALU.subtract).then_inc(s["e"], 1)
                dve.wait_ge(s["d2"], i + 1)
                dve.wait_ge(s["e"], i + 1)
                dve.tensor_copy(mbuf[:, 0:1], mbuf[:, CH:CH + 1]).then_inc(s["mshift"], 1)
                dve.wait_ge(s["c"], i + 1)
                dve.tensor_tensor(q["p"][:], q["pe"][:], q["m4"][:], ALU.mult).then_inc(s["p"], 1)
                dve.wait_ge(s["p"], i + 1)
                dve.tensor_tensor_scan(den[:], q["c"][:], q["p"][:], dcarry[:, 0:1], ALU.mult, ALU.add).then_inc(s["den"], 1)
                dve.wait_ge(s["den"], i + 1)
                dve.tensor_copy(dcarry[:], den[:, CH - 1:CH]).then_inc(s["dcarry"], 1)
                dve.wait_ge(s["denT_ps"], i + 1)
                dve.tensor_scalar(has[:], ps_dT, 0.0, None, ALU.is_gt)
                dve.tensor_scalar(dmax[:], ps_dT, 1e-30, None, ALU.max).then_inc(s["dmax"], 1)
                dve.wait_ge(s["dmax"], i + 1)
                dve.tensor_scalar(hneg[:], has[:], -1.0, NEG, ALU.add, ALU.mult)
                dve.reciprocal(rdT[:], dmax[:]).then_inc(s["rdT"], 1)
                for r in range(R):
                    dve.wait_ge(s[f"h_ps{r}"], i + 1)
                    dve.wait_ge(s[f"y{r}"], i + 1)
                    dve.tensor_tensor(py[:], ps_p[:], y[:], ALU.mult).then_inc(s[f"py{r}"], 1)
                    dve.wait_ge(s[f"py{r}"], i + 1)
                    dve.tensor_tensor_scan(num[r][:], ps_c[:], py[:], ncarry[:, r:r + 1], ALU.mult, ALU.add
                                           ).then_inc(s[f"num{r}"], 1)
                    dve.wait_ge(s[f"num{r}"], i + 1)
                    dve.tensor_copy(ncarry[:, r:r + 1], num[r][:, CH - 1:CH])
                    if r:
                        dve.wait_ge(s[f"g{r - 1}"], i + 1)
                    elif not first:
                        dve.wait_ge(s[f"g{R - 1}"], i)
                    dve.tensor_tensor(ro[:], num[r][:], ps_q[:], ALU.mult).then_inc(s[f"ro{r}"], 1)
                dve.wait_ge(s[f"y_ps{R - 1}"], 2 * i + 2)
                dve.tensor_copy(ld[:], ps_lg[:, :, K, :]).then_inc(s["ld"], 1)
                dve.wait_ge(s["ld"], i + 1)
                for u in range(U):
                    ins = dve.tensor_tensor(lg["lg0"][:, u], ps_lg[:, u, 0:K, :],
                                            ld[:, u:u + 1, :].to_broadcast([P, K, H]), ALU.add)
                ins.then_inc(s["lg0"], 1)
                dve.wait_ge(s["lg0"], i + 1)
                dve.tensor_scalar(lg["lg1"][:], lg["lg0"][:], LEAK, None, ALU.mult).then_inc(s["lg1"], 1)
                dve.wait_ge(s["lg1"], i + 1)
                dve.tensor_tensor(lg["lg3"][:], lg["lg0"][:], lg["lg1"][:], ALU.max).then_inc(s["lg2"], 1)
                dve.wait_ge(s["lg2"], i + 1)
                hasv = has[:].rearrange("p u (r h) -> p u r h", r=R)
                hnegv = hneg[:].rearrange("p u (r h) -> p u r h", r=R)
                dve.tensor_tensor(lg["lg3"][:, :, 1:K, :], lg["lg3"][:, :, 1:K, :], hasv, ALU.mult).then_inc(s["lg3"], 1)
                dve.wait_ge(s["lg3"], i + 1)
                dve.tensor_tensor(lg["lg3"][:, :, 1:K, :], lg["lg3"][:, :, 1:K, :], hnegv, ALU.add).then_inc(s["lg4"], 1)
                dve.wait_ge(s["lg4"], i + 1)
                dve.tensor_reduce(mx[:], lg["lg3"][:].rearrange("p u k h -> p u h k"), AX.X, ALU.max).then_inc(s["mx"], 1)
                dve.wait_ge(s["mx"], i + 1)
                for u in range(U):
                    ins = dve.tensor_tensor(lg["lg2"][:, u], lg["lg3"][:, u], mx[:, u:u + 1, :].to_broadcast([P, K, H]),
                                            ALU.subtract)
                ins.then_inc(s["lg5"], 1)
                dve.wait_ge(s["lge"], i + 1)
                dve.tensor_reduce(sm[:], lg["lge"][:].rearrange("p u k h -> p u h k"), AX.X, ALU.add).then_inc(s["sm"], 1)
                dve.wait_ge(s["sm"], i + 1)
                dve.reciprocal(rs[:], sm[:]).then_inc(s["rs"], 1)
                dve.wait_ge(s["rs"], i + 1)
                for u in range(U):
                    ins = dve.tensor_tensor(lg["alpha"][:, u], lg["lge"][:, u], rs[:, u:u + 1, :].to_broadcast([P, K, H]),
                                            ALU.mult)
                ins.then_inc(s["alpha"], 1)
                dve.wait_ge(s["alpha"], i + 1)
                dve.wait_ge(s[f"ent_r{R - 1}"], i + 1)
                for u in range(U):
                    a = lg["alpha"][:, u].rearrange("p k h -> p (k h)").rearrange("p (x a) -> p x a", a=1)
                    ins = dve.tensor_tensor(mixed[:, u].rearrange("p k (h d) -> p (k h) d", h=H),
                                            ent[:, u].rearrange("p k (h d) -> p (k h) d", h=H),
                                            a.to_broadcast([P, K * H, D]), ALU.mult)
                ins.then_inc(s["mixed"], 1)
                dve.wait_ge(s["mixed"], i + 1)
                dve.tensor_reduce(outc[:], mixed[:].rearrange("p u k c -> p u c k"), AX.X, ALU.add).then_inc(s["outc"], 1)
                dve.wait_ge(s["outc"], i + 1)
                dve.tensor_tensor(outb[:], outc[:], bias[:], ALU.add).then_inc(s["outb"], 1)
                dve.wait_ge(s["outb"], i + 1)
                dve.wait_ge(s["x_ps"], i + 1)
                if not first:
                    dve.wait_ge(put.s_made, i)
                dve.tensor_tensor(u0[:], ps_h[:].rearrange("p (u c) -> p u c", u=U), outb[:], ALU.add).then_inc(s["u0"], 1)
                dve.wait_ge(s["u0"], i + 1)
                norm.statistics(dve, u0, i, first)
                norm.factors(dve, i, first)
            steps(dve, NC, body)



def graph_layers(nc, w, out):
    def dram(name, shape, dtype=F32):
        return nc.dram_tensor(name, shape, dtype).ap()

    tab = {n: dram(f"t_{n}", [N, C]) for n in ("x1", "x2", "h1", "h2", "x3")}
    tab |= {"x": w["x"], "out": out}
    edge_tab = [tab["x1"][0:H5, :], tab["x2"][0:H5, :]]
    node_sums = tab["h1"]
    by_dst, by_src = dram("by_dst", [EP + 2, 4], I32), dram("by_src", [EP + 2, 4], I32)
    flat = {n: dram(f"f_{n}", [EP], I32) for n in ("src_d", "dst_d", "put_d", "src_s", "dst_s", "put_s")}
    flat |= {n: dram(f"f_{n}", [EP]) for n in ("run_d", "run_s", "last_s", "rel_d", "kind0_d", "kind1_d", "ones",
                                               "weight_s", "inv0_d", "inv1_d", "inv_deg_d", "inv_w_s")}
    sums = dram("sums", [4, EP])
    affine = dram("affine", [P, 2])

    sort_edges(nc, "sortd", w["records"], 0, w, by_dst)
    sort_edges(nc, "sorts", w["records"], 1, w, by_src)
    derive_orders(nc, by_dst, by_src, flat)
    gather_weights(nc, w["hyper_w"], flat)
    count_runs(nc, flat, sums)
    dense_pass(nc, w, tab)
    with nc.sbuf_tensor("att", [P, 11 * H], F32) as att:
        fold_attention(nc, w, att)
        relational_attention(nc, w, tab, flat, att)
    edge_attention(nc, w, tab, flat)
    for l in range(3):
        edge_perceptrons(nc, l, w, tab, flat)
    hyper_edges(nc, "l3a", tab["x3"], "W1_T", edge_tab[0], w, flat)
    nodes_of_edges(nc, "l3b", edge_tab[0], node_sums, w, tab, flat, affine)
    hyper_edges(nc, "l3c", node_sums, "W2_T", edge_tab[1], w, flat, affine)
    nodes_of_edges(nc, "l3d", edge_tab[1], None, w, tab, flat, affine)


def layouts(i):
    a = np.ascontiguousarray
    records = np.stack([i["dst"], i["src"], i["edge_type_4"], i["edge_type_2"]], axis=1).astype(np.int32)
    padding = np.array([[N, N, R, R]], np.int32).repeat(EP - E, axis=0)
    heads = (np.arange(C)[:, None] // D == np.arange(H)[None]).astype(np.float32)
    spread = np.zeros((R, H, R, C), np.float32)
    for r in range(R):
        spread[r, :, r, :] = heads.T
    return {
        "x": i["x"],
        "records": np.concatenate([records, padding]),
        "hyper_w": i["L3_gnn_hyperedge_weight"].reshape(H5, 1),
        "iota": np.tile(np.arange(CH, dtype=np.float32), (P, 1)),
        "tri": np.triu(np.ones((P, P), np.float32), 1),
        "tri_low": np.tril(np.ones((P, P), np.float32), -1),
        "ident": np.eye(P, dtype=np.float32),
        "heads": heads,
        "spread": spread.reshape(R * H, R, C),
        "rid": (np.arange(R * H) // H).astype(np.float32).reshape(R * H, 1),
        "W_rel": a(i["L0_gnn_W_rel"].transpose(1, 0, 2)),
        "W_rel_T": a(i["L0_gnn_W_rel"].transpose(2, 0, 1)),
        "W_cross": i["L0_gnn_W_cross"],
        "W_cross_T": a(i["L0_gnn_W_cross"].T),
        "W_self": i["L0_gnn_W_self"],
        "W_self_T": a(i["L0_gnn_W_self"].T),
        "att_vectors": a(np.concatenate([i["L0_gnn_att_src_rel"].reshape(R, C), i["L0_gnn_att_dst_rel"].reshape(R, C),
                                         i["L0_gnn_att_src_lang"].reshape(1, C),
                                         i["L0_gnn_att_dst_lang"].reshape(1, C)]).T),
        "bias_rel": a(i["L0_gnn_bias_rel"].T),
        "bias_lang": i["L0_gnn_bias_lang"],
        "l1_w23": a(np.stack([i["L1_gnn_W2"], i["L1_gnn_W3"]], axis=1)),
        "eW1": a(i["L2_gnn_eW1"].reshape(3, 2, 2, C, 64).transpose(0, 2, 3, 1, 4)).reshape(3, 2, C, 2 * 64),
        "eb1": i["L2_gnn_eb1"].reshape(3, 128, 1),
        "eW2": i["L2_gnn_eW2"],
        "eb2": i["L2_gnn_eb2"].reshape(3, 64, 1),
        "nW1": i["L2_gnn_nW1"],
        "nb1": a(i["L2_gnn_nb1"].T),
        "nb1_cols": i["L2_gnn_nb1"].reshape(3, 64, 1),
        "nW2": i["L2_gnn_nW2"],
        "nb2": a(i["L2_gnn_nb2"].T),
        "nb2_rows": i["L2_gnn_nb2"],
        "W1_T": a(i["L3_gnn_W1"].T),
        "W2_T": a(i["L3_gnn_W2"].T),
        "b2": i["L3_gnn_b2"],
        "gamma_beta": a(np.stack([i["L3_gnn_gamma"], i["L3_gnn_beta"]], axis=1)),
    }


def kernel(**inputs):
    import concourse.bacc as bacc
    from concourse.bass_utils import run_bass_kernel_spmd as run

    nc = bacc.Bacc("TRN2", target_bir_lowering=False, num_devices=1)
    arrays = {f"in_{n}": np.ascontiguousarray(v)
              for n, v in layouts({k: np.asarray(v) for k, v in inputs.items()}).items()}
    w = {n[3:]: nc.dram_tensor(n, list(v.shape), mybir.dt.from_np(v.dtype), kind="ExternalInput").ap()
         for n, v in arrays.items()}
    out = nc.dram_tensor("out", [N, C], F32, kind="ExternalOutput").ap()
    graph_layers(nc, w, out)
    nc.compile()
    return run(nc, [arrays], core_ids=[0]).results[0]["out"]
```

```python
from contextlib import ExitStack

import numpy as np

import concourse.bass as bass
from concourse import mybir

F32 = mybir.dt.float32
I32 = mybir.dt.int32
BF16 = mybir.dt.bfloat16
ALU = mybir.AluOpType
ACT = mybir.ActivationFunctionType
AX = mybir.AxisListType

P = 128
N = 50000
E = 25000
H5 = 10000
C = 128
R = 4
H = 8
D = C // H
U = 4
CH = P * U
NC = -(-E // CH)
EP = NC * CH
NT = EP // P
NP = N // CH
RP, RC = 98, EP // 98
HI = -(-(N + 1) // P)
NOWHERE = 1 << 20
EPS = 1e-5
LEAK = 0.2
NEG = 1.0e30
MASKED = 3.0e38


class Phase:

    def __init__(self, nc, name):
        self.nc, self.name, self.stack, self.sems = nc, name, ExitStack(), []

    def __enter__(self):
        self.stack.__enter__()
        return self

    def __exit__(self, *exc):
        done = self.stack.__exit__(*exc)
        self.nc.clear_and_free_semaphores(self.sems)
        self.nc.all_engine_barrier()
        return done

    def sb(self, name, shape, dtype=F32):
        return self.stack.enter_context(self.nc.sbuf_tensor(f"{self.name}_{name}", shape, dtype))

    def ps(self, name, shape=(P, CH)):
        return self.stack.enter_context(self.nc.psum_tensor(f"{self.name}_{name}", list(shape), F32))

    def sem(self, name):
        self.sems.append(self.nc.alloc_semaphore(f"{self.name}_{name}"))
        return self.sems[-1]

    def block(self):
        return self.stack.enter_context(self.nc.Block())


def steps(eng, count, body):
    body(0, True)
    if count > 1:
        with eng.Fori(1, count) as i:
            body(i, False)


def gate(eng, sem, value, passed):
    eng.wait_ge(sem, value)
    eng.sem_inc(passed, 1)


def chunk(flat, i):
    return flat[bass.ds(i * CH, CH)].rearrange("(p u) -> p u", u=U)


def rows(flat, i, parts=P):
    return flat[bass.ds(i * CH, CH)].rearrange("(a e) -> a e", a=1).to_broadcast([parts, CH])


def slot(wide, u):
    return wide[:, u::U]


def gather(pool, tile, table, index, u, done):
    pool.indirect_dma_start(out=tile[:, u, :], out_offset=None, in_=table,
                            in_offset=bass.IndirectOffsetOnAxis(ap=index[:, u:u + 1], axis=0)).then_inc(done, 16)


def scatter(pool, table, tile, index, u, done, last_row):
    pool.indirect_dma_start(out=table, out_offset=bass.IndirectOffsetOnAxis(ap=index[:, u:u + 1], axis=0),
                            in_=tile[:, u, :], in_offset=None, bounds_check=last_row,
                            oob_is_err=False).then_inc(done, 16)



def sort_edges(nc, records, const, by_dst, by_src):
    both = range(2)
    with Phase(nc, "sort") as ph:
        def two(name, shape, dtype=F32):
            return [ph.sb(f"{name}{k}", shape, dtype) for k in both]

        rec = ph.sb("rec", [P, NT, 4], I32)
        keyi, digit = two("keyi", [P, NT], I32), two("digit", [P, NT], I32)
        key, hi, lo = two("key", [P, NT]), two("hi", [P, NT]), two("lo", [P, NT])
        keys_of = two("keys_of", [P, CH], I32)
        iota = ph.sb("iota", [P, HI])
        tri = ph.sb("tri", [P, P])
        low = ph.sb("low", [P, CH])
        ident = ph.sb("ident", [P, P])
        ident_b = ph.sb("ident_b", [P, P], BF16)
        ones = ph.sb("ones", [P, HI])
        lob, hib = two("lob", [P, U, P], BF16), two("hib", [P, U, HI], BF16)
        loT = two("loT", [P, CH])
        same = [ph.sb(f"same{j}", [P, CH]) for j in range(U)]
        hit = [ph.sb(f"hit{j}", [P, HI]) for j in range(U)]
        rank, looked, posf = two("rank", [P, U]), two("looked", [P, U]), two("posf", [P, U])
        pos, recst = two("pos", [P, U], I32), two("recst", [P, U, 4], I32)
        place = two("place", [P, HI])
        total, ends = two("total", [P, HI]), two("ends", [P, HI])
        sent = ph.sb("sent", [1, 4], I32)
        ps_place = [ph.ps(f"ps_place{k}") for k in both]
        ps_look = [[ph.ps(f"ps_look{k}{q}") for q in range(2)] for k in both]
        ps_loT = [ph.stack.enter_context(nc.psum_tensor(f"sort_ps_loT{k}", [P, 2 * CH], BF16)) for k in both]
        s = {x: ph.sem(x) for x in ("loaded", "ones", "sentinel", "sent_out", "passed", "digits")}
        s |= {f"{x}{k}": ph.sem(f"{x}{k}") for k in both for x in (
            "hot", "counted", "table", "before", "ends", "first_place", "hot2", "loT_ps", "loT", "rank", "look",
            "looked", "own_counts", "place", "posf", "pos", "scattered", "keys_of")}
        block = ph.block()

        @block.sync
        def _(sp):
            sp.dma_start(rec[:], records.rearrange("(t p) f -> p t f", p=P)).then_inc(s["loaded"], 16)
            sp.dma_start(iota[:], const["iota"][:, 0:HI]).then_inc(s["loaded"], 16)
            sp.dma_start(tri[:], const["tri"]).then_inc(s["loaded"], 16)
            sp.dma_start(low[:, CH - P:CH], const["tri_low"]).then_inc(s["loaded"], 16)
            sp.dma_start(ident[:], const["ident"]).then_inc(s["loaded"], 16)
            sp.wait_ge(s["sentinel"], 1)
            for ordered in (by_dst, by_src):
                sp.dma_start(ordered[0:1, :], sent[:]).then_inc(s["sent_out"], 16)
                sp.dma_start(ordered[EP + 1:EP + 2, :], sent[:]).then_inc(s["sent_out"], 16)
            sp.wait_ge(s["sent_out"], 64)

            def position(g, first):
                for k in both:
                    if not first:
                        sp.wait_ge(s[f"rank{k}"], g)
                    sp.dma_start(keys_of[k][:], rows(const["dst_src"][k], g)).then_inc(s[f"keys_of{k}"], 16)
            steps(sp, NC, position)

        @block.vector
        def _(dve):
            dve.memset(sent[:], -1).then_inc(s["sentinel"], 1)
            dve.memset(low[:, 0:CH - P], 1.0)
            dve.memset(ones[:], 1.0).then_inc(s["ones"], 1)
            dve.wait_ge(s["loaded"], 16 * 5)
            dve.tensor_copy(ident_b[:], ident[:]).then_inc(s["ones"], 1)
            dve.wait_ge(s["ones"], 2)
            for k in both:
                dve.tensor_copy(keyi[k][:], rec[:, :, k]).then_inc(s["digits"], 1)
                dve.wait_ge(s["digits"], 5 * k + 1)
                dve.tensor_copy(key[k][:], keyi[k][:])
                dve.tensor_scalar(digit[k][:], keyi[k][:], 7, None, ALU.arith_shift_right).then_inc(s["digits"], 1)
                dve.wait_ge(s["digits"], 5 * k + 2)
                dve.tensor_copy(hi[k][:], digit[k][:]).then_inc(s["digits"], 1)
                dve.wait_ge(s["digits"], 5 * k + 3)
                dve.tensor_scalar(digit[k][:], keyi[k][:], 127, None, ALU.bitwise_and).then_inc(s["digits"], 1)
                dve.wait_ge(s["digits"], 5 * k + 4)
                dve.tensor_copy(lo[k][:], digit[k][:]).then_inc(s["digits"], 1)
                dve.wait_ge(s["digits"], 5 * k + 5)

            def one_hot(g, k, made):
                for j in range(U):
                    at = bass.ds(g * U + j, 1)
                    dve.tensor_scalar(lob[k][:, j, :], iota[:, 0:P], lo[k][:, at], None, ALU.is_equal)
                    ins = dve.tensor_scalar(hib[k][:, j, :], iota[:], hi[k][:, at], None, ALU.is_equal)
                ins.then_inc(made, 1)

            def count(g, first):
                for k in both:
                    if not first:
                        dve.wait_ge(s[f"counted{k}"], g)
                    one_hot(g, k, s[f"hot{k}"])
            steps(dve, NC, count)

            for k in both:
                dve.wait_ge(s[f"counted{k}"], NC)
                dve.tensor_copy(place[k][:], ps_place[k][:, 0:HI]).then_inc(s[f"table{k}"], 1)
            for k in both:
                dve.wait_ge(s[f"before{k}"], 1)
                dve.tensor_copy(total[k][:], ps_look[k][1][:, 0:HI]).then_inc(s[f"ends{k}"], 1)
                dve.wait_ge(s[f"ends{k}"], 1)
                dve.tensor_tensor_scan(ends[k][:], ones[:], total[k][:], 0.0, ALU.mult, ALU.add).then_inc(s[f"ends{k}"], 1)
                dve.wait_ge(s[f"ends{k}"], 2)
                dve.tensor_tensor(ends[k][:], ends[k][:], total[k][:], ALU.subtract).then_inc(s[f"ends{k}"], 1)
                dve.wait_ge(s[f"ends{k}"], 3)
                dve.tensor_tensor(place[k][:], ends[k][:], ps_look[k][0][:, 0:HI], ALU.add).then_inc(s[f"first_place{k}"], 1)

            def position(g, first):
                for k in both:
                    if not first:
                        dve.wait_ge(s[f"own_counts{k}"], g)
                    one_hot(g, k, s[f"hot2{k}"])
                for k in both:
                    dve.wait_ge(s[f"keys_of{k}"], 16 * (g + 1))
                    if not first:
                        dve.wait_ge(s[f"posf{k}"], g)
                    for j in range(U):
                        n = P * (j + 1)
                        if k:
                            dve.wait_ge(s["rank0"], g + 1)
                        elif not first:
                            dve.wait_ge(s["rank1"], g)
                        ins = dve.scalar_tensor_tensor(out=same[j][:, 0:n], in0=keys_of[k][:, 0:n],
                                                       scalar=key[k][:, bass.ds(g * U + j, 1)], in1=low[:, CH - n:CH],
                                                       op0=ALU.is_equal, op1=ALU.mult, accum_out=rank[k][:, j:j + 1])
                        if j == U - 1:
                            ins.then_inc(s[f"rank{k}"], 1)
                        dve.wait_ge(s[f"look{k}"], g * U + j + 1)
                        if k:
                            dve.wait_ge(s["looked0"], (g + 1) * U)
                        elif not first:
                            dve.wait_ge(s["looked1"], g * U)
                        dve.tensor_tensor_reduce(hit[j][:], ps_look[k][j % 2][:, 0:HI], hib[k][:, j, :], 1.0, 0.0,
                                                 ALU.mult, ALU.add, looked[k][:, j:j + 1]).then_inc(s[f"looked{k}"], 1)
                    dve.wait_ge(s[f"looked{k}"], (g + 1) * U)
                    dve.wait_ge(s[f"rank{k}"], g + 1)
                    if not first:
                        dve.wait_ge(s[f"scattered{k}"], 16 * U * g)
                    dve.scalar_tensor_tensor(out=posf[k][:], in0=looked[k][:], scalar=1.0, in1=rank[k][:],
                                             op0=ALU.add, op1=ALU.add).then_inc(s[f"posf{k}"], 1)
                    dve.tensor_copy(recst[k][:], rec[:, bass.ds(g * U, U), :])
                    dve.wait_ge(s[f"posf{k}"], g + 1)
                    dve.tensor_copy(pos[k][:], posf[k][:]).then_inc(s[f"pos{k}"], 1)
            steps(dve, NC, position)

        @block.tensor
        def _(pe):
            pe.wait_ge(s["loaded"], 16 * 5)

            def add_counts(k, start, stop, done):
                for j in range(U):
                    ins = pe.matmul(ps_place[k][:, 0:HI], lob[k][:, j, :], hib[k][:, j, :], start=start and j == 0,
                                    stop=stop, skip_group_check=True)
                ins.then_inc(done, 1)

            def count(g, first):
                for k in both:
                    pe.wait_ge(s[f"hot{k}"], g + 1)
                    add_counts(k, first, False, s[f"counted{k}"])
            steps(pe, NC, count)
            for k in both:
                pe.wait_ge(s[f"table{k}"], 1)
                pe.matmul(ps_look[k][0][:, 0:HI], tri[:], place[k][:], start=True, stop=True)
                pe.matmul(ps_look[k][1][:, 0:HI], ones[:, 0:P], place[k][:], start=True, stop=True).then_inc(s[f"before{k}"], 1)
            for k in both:
                pe.wait_ge(s[f"first_place{k}"], 1)
                pe.matmul(ps_place[k][:, 0:HI], ident[:], place[k][:], start=True, stop=False, skip_group_check=True)

            def position(g, first):
                for k in both:
                    pe.wait_ge(s[f"hot2{k}"], g + 1)
                    if not first:
                        pe.wait_ge(s[f"loT{k}"], g)
                    for j in range(U):
                        ins = pe.transpose(ps_loT[k][:, j * P:(j + 1) * P], lob[k][:, j, :], ident_b[:])
                    ins.then_inc(s[f"loT_ps{k}"], 1)
                    if not first:
                        pe.wait_ge(s[f"place{k}"], g)
                    add_counts(k, False, False, s[f"own_counts{k}"])
                for k in both:
                    pe.wait_ge(s[f"loT{k}"], g + 1)
                    for j in range(U):
                        if j >= 2 or not first:
                            pe.wait_ge(s[f"looked{k}"], g * U + j - 1)
                        pe.matmul(ps_look[k][j % 2][:, 0:HI], loT[k][:, j * P:(j + 1) * P], place[k][:],
                                  start=True, stop=True).then_inc(s[f"look{k}"], 1)
            steps(pe, NC, position)

        @block.scalar
        def _(act):
            def position(g, first):
                for k in both:
                    act.wait_ge(s[f"loT_ps{k}"], g + 1)
                    if not first:
                        act.wait_ge(s[f"look{k}"], g * U)
                    act.copy(loT[k][:], ps_loT[k][:, 0:CH]).then_inc(s[f"loT{k}"], 1)
                for k in both:
                    act.wait_ge(s[f"own_counts{k}"], g + 1)
                    act.wait_ge(s[f"look{k}"], (g + 1) * U)
                    act.copy(place[k][:], ps_place[k][:, 0:HI]).then_inc(s[f"place{k}"], 1)
            steps(act, NC, position)

        @block.gpsimd
        def _(pool):
            def position(g, first):
                for k, ordered in enumerate((by_dst, by_src)):
                    gate(pool, s[f"pos{k}"], g + 1, s["passed"])
                    for j in range(U):
                        pool.indirect_dma_start(out=ordered, out_offset=bass.IndirectOffsetOnAxis(ap=pos[k][:, j:j + 1], axis=0),
                                                in_=recst[k][:, j, :], in_offset=None).then_inc(s[f"scattered{k}"], 16)
            steps(pool, NC, position)
            for k in both:
                pool.wait_ge(s[f"scattered{k}"], 16 * NT)



def derive_orders(nc, by_dst, by_src, flat):
    with Phase(nc, "orders") as ph:
        s = {x: ph.sem(x) for x in ("loaded", "step", "ready", "stored")}
        cur, prev, nxt, f = {}, {}, {}, {}
        for o in "ds":
            cur[o] = ph.sb(f"cur_{o}", [RP, RC, 4], I32)
            prev[o] = ph.sb(f"prev_{o}", [RP, RC, 4], I32)
            nxt[o] = ph.sb(f"next_{o}", [RP, RC, 4], I32)
        names = ["src_d", "dst_d", "put_d", "src_s", "dst_s", "put_s"]
        for n in names:
            f[n] = ph.sb(n, [RP, RC], I32)
        fl = ["run_d", "run_s", "last_s", "rel_d", "kind0_d", "kind1_d", "reset_d"]
        for n in fl:
            f[n] = ph.sb(n, [RP, RC])
        goes_on = ph.sb("goes_on", [RP, RC])
        goes_on2 = ph.sb("goes_on2", [RP, RC])
        real = ph.sb("real", [RP, RC])
        block = ph.block()

        @block.sync
        def _(sp):
            for o, rec in (("d", by_dst), ("s", by_src)):
                for where, at in ((prev, 0), (cur, 1), (nxt, 2)):
                    sp.dma_start(where[o][:], rec[at:at + EP, :].rearrange("(p k) f -> p k f", p=RP)
                                 ).then_inc(s["loaded"], 16)
            sp.wait_ge(s["ready"], 1)
            for n in names + fl:
                sp.dma_start(flat[n].rearrange("(p k) -> p k", p=RP), f[n][:]).then_inc(s["stored"], 16)
            sp.wait_ge(s["stored"], 16 * len(names + fl))

        @block.vector
        def _(dve):
            dve.wait_ge(s["loaded"], 16 * 6)
            for o, k, other in (("d", 0, 1), ("s", 1, 0)):
                key = cur[o][:, :, k]
                own = "dst_d" if o == "d" else "src_s"
                far = "src_d" if o == "d" else "dst_s"
                dve.tensor_tensor(f[f"run_{o}"][:], key, prev[o][:, :, k], ALU.is_equal)
                g = goes_on if o == "d" else goes_on2
                dve.tensor_tensor(g[:], key, nxt[o][:, :, k], ALU.is_equal)
                dve.tensor_scalar(f[own][:], key, float(N - 1), None, ALU.min)
                dve.tensor_scalar(f[far][:], cur[o][:, :, other], float(N - 1 if o == "d" else H5 - 1), None,
                                  ALU.min).then_inc(s["step"], 1)
            dve.wait_ge(s["step"], 2)
            dve.tensor_scalar(f["reset_d"][:], f["run_d"][:], -1.0, MASKED, ALU.add, ALU.mult)
            dve.scalar_tensor_tensor(out=f["put_d"][:], in0=goes_on[:], scalar=float(NOWHERE),
                                     in1=cur["d"][:, :, 0], op0=ALU.mult, op1=ALU.add)
            dve.scalar_tensor_tensor(out=f["put_s"][:], in0=goes_on2[:], scalar=float(NOWHERE),
                                     in1=cur["s"][:, :, 1], op0=ALU.mult, op1=ALU.add)
            dve.tensor_scalar(real[:], cur["s"][:, :, 1], float(N), None, ALU.is_lt)
            dve.tensor_scalar(f["kind0_d"][:], cur["d"][:, :, 3], 0.0, None, ALU.is_equal)
            dve.tensor_scalar(f["kind1_d"][:], cur["d"][:, :, 3], 1.0, None, ALU.is_equal)
            dve.tensor_copy(f["rel_d"][:], cur["d"][:, :, 2]).then_inc(s["step"], 1)
            dve.wait_ge(s["step"], 3)
            dve.tensor_tensor(f["last_s"][:], real[:], goes_on2[:], ALU.is_gt).then_inc(s["ready"], 1)


def count_runs(nc, flat, sums):
    SC = EP // 7
    with Phase(nc, "runs") as ph:
        s = {x: ph.sem(x) for x in ("ones", "loaded", "summed", "stored", "back", "step", "ready", "out")}
        run = [ph.sb(f"run{j}", [4, SC]) for j in range(2)]
        val = [ph.sb(f"val{j}", [4, SC]) for j in range(2)]
        out = [ph.sb(f"out{j}", [4, SC]) for j in range(2)]
        b = {n: ph.sb(n, [RP, RC]) for n in ("inv0", "inv1", "inv_deg", "weight", "pos", "safe", "inv", "inv_w",
                                             "gap", "t0", "t1", "t2")}
        ones_row = ph.sb("ones_row", [P, EP // P])
        block = ph.block()
        vals = ["kind0_d", "kind1_d", "ones", "weight_s"]
        facs = ["inv0_d", "inv1_d", "inv_deg_d", "inv_w_s"]

        @block.sync
        def _(sp):
            sp.wait_ge(s["ones"], 1)
            sp.dma_start(flat["ones"].rearrange("(p k) -> p k", p=P), ones_row[:]).then_inc(s["out"], 16)
            sp.wait_ge(s["out"], 16)
            for j in range(7):
                if j >= 2:
                    sp.wait_ge(s["summed"], j - 1)
                at = slice(j * SC, (j + 1) * SC)
                for q in range(4):
                    order = "run_s" if q == 3 else "run_d"
                    sp.dma_start(run[j % 2][q:q + 1, :], flat[order][at].rearrange("(a e) -> a e", a=1)).then_inc(s["loaded"], 16)
                    sp.dma_start(val[j % 2][q:q + 1, :], flat[vals[q]][at].rearrange("(a e) -> a e", a=1)).then_inc(s["loaded"], 16)
                sp.wait_ge(s["loaded"], 128 * (j + 1))
                sp.wait_ge(s["summed"], j + 1)
                sp.dma_start(sums[:, at], out[j % 2][:]).then_inc(s["stored"], 16)
                sp.wait_ge(s["stored"], 16 * (j + 1))
            for q, n in enumerate(("inv0", "inv1", "inv_deg", "weight")):
                sp.dma_start(b[n][:], sums[q].rearrange("(p k) -> p k", p=RP)).then_inc(s["back"], 16)
            sp.wait_ge(s["ready"], 1)
            for n, q in zip(facs, ("t0", "t1", "t2", "inv_w")):
                sp.dma_start(flat[n].rearrange("(p k) -> p k", p=RP), b[q][:]).then_inc(s["out"], 16)
            sp.wait_ge(s["out"], 16 * 5)

        @block.vector
        def _(dve):
            dve.memset(ones_row[:], 1.0).then_inc(s["ones"], 1)
            for j in range(7):
                dve.wait_ge(s["loaded"], 128 * (j + 1))
                if j >= 2:
                    dve.wait_ge(s["stored"], 16 * (j - 1))
                if j >= 1:
                    dve.wait_ge(s["summed"], j)
                dve.tensor_tensor_scan(out[j % 2][:], run[j % 2][:], val[j % 2][:],
                                       0.0 if j == 0 else out[1 - j % 2][:, SC - 1:SC], ALU.mult, ALU.add
                                       ).then_inc(s["summed"], 1)
            dve.wait_ge(s["back"], 64)
            for n in ("inv0", "inv1", "inv_deg"):
                dve.tensor_scalar(b[n][:], b[n][:], 1.0, None, ALU.max)
            dve.tensor_scalar(b["pos"][:], b["weight"][:], 0.0, None, ALU.is_gt).then_inc(s["step"], 1)
            dve.wait_ge(s["step"], 1)
            dve.tensor_scalar(b["gap"][:], b["pos"][:], -1.0, 1.0, ALU.mult, ALU.add)
            dve.tensor_tensor(b["safe"][:], b["weight"][:], b["pos"][:], ALU.mult).then_inc(s["step"], 1)
            dve.wait_ge(s["step"], 2)
            dve.tensor_tensor(b["inv"][:], b["safe"][:], b["gap"][:], ALU.add).then_inc(s["step"], 1)
            dve.wait_ge(s["step"], 3)
            for n, q in (("inv0", "t0"), ("inv1", "t1"), ("inv_deg", "t2")):
                dve.reciprocal(b[q][:], b[n][:])
            dve.reciprocal(b["safe"][:], b["inv"][:]).then_inc(s["step"], 1)
            dve.wait_ge(s["step"], 4)
            dve.tensor_tensor(b["inv_w"][:], b["safe"][:], b["pos"][:], ALU.mult).then_inc(s["ready"], 1)



class Norm:

    def __init__(self, ph, name, eps, tiles=1):
        self.stats = ph.sb(f"{name}_stats", [P, tiles * U, 6])
        self.mv = ph.sb(f"{name}_mv", [P, tiles * U, 2])
        self.root = ph.sb(f"{name}_root", [P, tiles * U])
        self.rstd = ph.sb(f"{name}_rstd", [P, tiles * U])
        self.eps = eps
        self.s_stats, self.s_mv, self.s_root, self.s_rstd, self.s_passed = (
            ph.sem(f"{name}_{x}") for x in ("stats", "mv", "root", "rstd", "passed"))

    def statistics(self, dve, srcs, i):
        for k, src in enumerate(srcs):
            for u in range(U):
                ins = dve.bn_stats(self.stats[:, k * U + u, :], src[:, u, :])
        ins.then_inc(self.s_stats, 1)
        gate(dve, self.s_stats, i + 1, self.s_passed)
        for u in range(U * len(srcs)):
            ins = dve.bn_aggr(self.mv[:, u, :], self.stats[:, u, :])
        ins.then_inc(self.s_mv, 1)

    def rootof(self, act, i, tiles=1):
        n = tiles * U
        act.wait_ge(self.s_mv, i + 1)
        act.activation(self.root[:, 0:n], self.mv[:, 0:n, 1], ACT.Sqrt, bias=self.eps[:, 0:1]).then_inc(self.s_root, 1)

    def inverse(self, dve, i, tiles=1):
        n = tiles * U
        dve.wait_ge(self.s_root, i + 1)
        dve.reciprocal(self.rstd[:, 0:n], self.root[:, 0:n]).then_inc(self.s_rstd, 1)
        dve.wait_ge(self.s_rstd, i + 1)

    def normalize(self, dve, out, src, done, k=0):
        for u in range(U):
            at = k * U + u
            ins = dve.tensor_scalar(out[:, u, :], src[:, u, :], self.mv[:, at, 0:1], self.rstd[:, at:at + 1],
                                    ALU.subtract, ALU.mult)
        ins.then_inc(done, 1)



def dense_pass(nc, w, tab):
    W = 4
    GROUPS = NP + 1
    BLOCKS, REST = divmod(GROUPS, W)
    with Phase(nc, "dense") as ph:
        ident = ph.sb("ident", [P, P])
        wself = ph.sb("wself", [P, C])
        wplus = ph.sb("wplus", [P, C])
        bias = ph.sb("bias", [P, U, C])
        b2 = ph.sb("b2", [P, U, C])
        eps = ph.sb("eps", [P, 1])
        w1 = [ph.sb(f"w1_{l}", [P, 64]) for l in range(3)]
        w2 = [ph.sb(f"w2_{l}", [65, C]) for l in range(3)]
        b1 = ph.sb("b1", [64, 3])
        b2c = ph.sb("b2c", [P, 3])

        def tiles(name, shape):
            return [ph.sb(f"{name}_{k}", shape) for k in range(W)]
        x, u, x1, x2, u3, x3, u4, x4 = (tiles(n, [P, U, C]) for n in ("x", "u", "x1", "x2", "u3", "x3", "u4", "x4"))
        hn = [tiles(f"hn{l}", [P, U, C]) for l in range(2)]
        xT = tiles("xT", [P, CH])
        hT = [tiles(f"hT{l}", [P, CH]) for l in range(3)]
        hid = tiles("hid", [65, CH])
        v1, root1, rstd1, sq = (ph.sb(n, [P, W * U]) for n in ("v1", "root1", "rstd1", "sq"))
        norm0, norm3, norm4 = (Norm(ph, n, eps, W) for n in ("norm0", "norm3", "norm4"))
        ps_a = [ph.ps(f"ps_a{k}") for k in range(W)]
        ps_b = [ph.ps(f"ps_b{k}") for k in range(W)]
        s = {n: ph.sem(n) for n in (
            "weights", "ready", "xT_ps", "xT", "s_ps", "u", "x1", "sq", "v1", "root1", "rstd1", "x2", "x2T_ps",
            "hT0", "hid_ps0", "hid_ps1", "hid_ps2", "hid0", "hid1", "hid2", "h_ps0", "h_ps1", "h_ps2", "hT1", "hT2",
            "n_ps0", "n_ps1", "hn0", "hn1", "u3", "x3", "u4", "x4", "passed")}
        s_x = [ph.sem(f"x_in{k}") for k in range(W)]
        s_stored = [ph.sem(f"stored{k}") for k in range(W)]
        block = ph.block()
        STORES = 6

        def at(table, g):
            lo = g * CH if not isinstance(g, int) or g < NP else N - CH
            return table[bass.ds(lo, CH), :].rearrange("(p u) c -> p u c", u=U)

        def blocks_of(eng, body):
            body(0, W, True)
            with eng.Fori(1, BLOCKS) as i:
                body(i, W, False)
            if REST:
                body(BLOCKS, REST, False)

        def each(i, width, step):
            for k in range(width):
                step(i * W + k, k)

        def wide(t):
            return t[:].rearrange("p (u c) -> p u c", u=U)

        loads = [(ident[:], w["ident"]), (wself[:], w["W_self"]), (b1[:], w["nb1"]), (b2c[:], w["nb2"]),
                 (bias[:], w["bias_lang"].rearrange("(a b c) -> a b c", a=1, b=1).to_broadcast([P, U, C])),
                 (b2[:], w["b2"].rearrange("(a b c) -> a b c", a=1, b=1).to_broadcast([P, U, C]))]
        for l in range(3):
            loads += [(w1[l][:], w["nW1"][l, 64:192, :]), (w2[l][0:64, :], w["nW2"][l]),
                      (w2[l][64:65, :], w["nb2_rows"][l:l + 1, :])]
        NW = 16 * len(loads)

        @block.sync
        def _(sp):
            for dst, src in loads:
                sp.dma_start(dst, src).then_inc(s["weights"], 16)

            def body(i, width, first):
                def load(g, k):
                    if not first:
                        sp.wait_ge(s["xT_ps"], g - W + 1)
                    sp.dma_start(x[k][:], at(w["x"], g)).then_inc(s_x[k], 16)
                each(i, width, load)
            blocks_of(sp, body)

        @block.gpsimd
        def _(pool):
            def body(i, width, first):
                def store(name, src, made):
                    def one(g, k):
                        if isinstance(g, int) and g == GROUPS - 1:
                            pool.wait_ge(s_stored[(g - 1) % W], 16 * (STORES * i + order.index(name) + 1))
                        gate(pool, s[made], g + 1, s["passed"])
                        pool.dma_start(at(tab[name], g), src[k][:]).then_inc(s_stored[k], 16)
                    each(i, width, one)
                order = ["x1", "x2", "h1", "h2", "x3", "out"]
                for name, src, made in (("x1", x1, "x1"), ("x2", x2, "x2"), ("h1", hn[0], "hn0"),
                                        ("h2", hn[1], "hn1"), ("x3", x3, "x3"), ("out", x4, "x4")):
                    store(name, src, made)
            blocks_of(pool, body)
            for k in range(W):
                pool.wait_ge(s_stored[k], 16 * STORES * (BLOCKS + (k < REST)))

        @block.tensor
        def _(pe):
            pe.wait_ge(s["weights"], NW)
            pe.wait_ge(s["ready"], 1)

            def body(i, width, first):
                def turn_x(g, k):
                    pe.wait_ge(s_x[k], 16 * (i + 1))
                    if not first:
                        pe.wait_ge(s["u3"], g - W + 1)
                    for j in range(U):
                        ins = pe.transpose(slot(ps_a[k], j), x[k][:, j, :], ident[:])
                    ins.then_inc(s["xT_ps"], 1)

                def self_map(g, k):
                    pe.wait_ge(s["xT"], g + 1)
                    for j in range(U):
                        ins = pe.matmul(ps_b[k][:, j * C:(j + 1) * C], slot(xT[k], j), wplus[:], start=True, stop=True)
                    ins.then_inc(s["s_ps"], 1)

                def turn_x2(g, k):
                    pe.wait_ge(s["x2"], g + 1)
                    for j in range(U):
                        ins = pe.transpose(slot(ps_a[k], j), x2[k][:, j, :], ident[:])
                    ins.then_inc(s["x2T_ps"], 1)

                def hidden(l):
                    def one(g, k):
                        pe.wait_ge(s[f"hT{l}"], g + 1)
                        ps = ps_b[k] if l != 1 else ps_a[k]
                        if l == 2:
                            pe.wait_ge(s["hT2"], g + 1)
                        pe.matmul(ps[0:64, :], w1[l][:], hT[l][k][:], start=True, stop=True).then_inc(s[f"hid_ps{l}"], 1)
                    return one

                def up(l):
                    def one(g, k):
                        pe.wait_ge(s[f"hid{l}"], g + 1)
                        if l == 1:
                            pe.wait_ge(s["hn0"], g + 1)
                        ps = ps_a[k] if l == 0 else ps_b[k]
                        pe.matmul(ps[:], w2[l][0:64, :], hid[k][0:64, :], start=True, stop=True).then_inc(s[f"h_ps{l}"], 1)
                    return one

                def turn_h(l):
                    def one(g, k):
                        pe.wait_ge(s[f"hT{l + 1}"], g + 1)
                        ps = ps_b[k] if l == 0 else ps_a[k]
                        for j in range(U):
                            ins = pe.transpose(ps[:, j * C:(j + 1) * C], slot(hT[l + 1][k], j), ident[:])
                        ins.then_inc(s[f"n_ps{l}"], 1)
                        hidden(l + 1)(g, k)
                    return one

                def out_rows(g, k):
                    pe.wait_ge(s["hid2"], g + 1)
                    pe.wait_ge(s["hn1"], g + 1)
                    for j in range(U):
                        ins = pe.matmul(ps_a[k][:, j * C:(j + 1) * C], slot(hid[k], j), w2[2][:], start=True, stop=True)
                    ins.then_inc(s["h_ps2"], 1)

                for step in (turn_x, self_map, turn_x2, hidden(0), up(0), turn_h(0), up(1), turn_h(1), out_rows):
                    each(i, width, step)
            blocks_of(pe, body)

        @block.scalar
        def _(act):
            def body(i, width, first):
                def copy_x(g, k):
                    act.wait_ge(s["xT_ps"], g + 1)
                    if not first:
                        act.wait_ge(s["s_ps"], g - W + 1)
                    act.copy(xT[k][:], ps_a[k][:]).then_inc(s["xT"], 1)

                def scale_x2(g, k):
                    act.wait_ge(s["x1"], g + 1)
                    if not first:
                        act.wait_ge(s_stored[k], 16 * STORES * i)
                    for j in range(U):
                        ins = act.activation(x2[k][:, j, :], x1[k][:, j, :], ACT.Identity,
                                             scale=rstd1[:, k * U + j:k * U + j + 1])
                    ins.then_inc(s["x2"], 1)

                def copy_x2(g, k):
                    act.wait_ge(s["x2T_ps"], g + 1)
                    act.copy(hT[0][k][:], ps_a[k][:]).then_inc(s["hT0"], 1)

                def relu(l):
                    def one(g, k):
                        act.wait_ge(s[f"hid_ps{l}"], g + 1)
                        ps = ps_b[k] if l != 1 else ps_a[k]
                        if l:
                            act.wait_ge(s[f"h_ps{l - 1}"], g + 1)
                        elif not first:
                            act.wait_ge(s["h_ps2"], g - W + 1)
                        act.activation(hid[k][0:64, :], ps[0:64, :], ACT.Relu, bias=b1[:, l:l + 1]).then_inc(s[f"hid{l}"], 1)
                    return one

                def rows_out(l):
                    def one(g, k):
                        act.wait_ge(s[f"n_ps{l}"], g + 1)
                        ps = ps_b[k] if l == 0 else ps_a[k]
                        act.copy(hn[l][k][:], wide(ps)).then_inc(s[f"hn{l}"], 1)
                        relu(l + 1)(g, k)
                    return one

                each(i, width, copy_x)
                norm0.rootof(act, i, width)
                n = width * U
                act.wait_ge(s["v1"], i + 1)
                act.activation(root1[:, 0:n], v1[:, 0:n], ACT.Sqrt, bias=eps[:, 0:1]).then_inc(s["root1"], 1)
                act.wait_ge(s["rstd1"], i + 1)
                each(i, width, scale_x2)
                each(i, width, copy_x2)
                each(i, width, relu(0))
                each(i, width, rows_out(0))
                each(i, width, rows_out(1))
                norm3.rootof(act, i, width)
                norm4.rootof(act, i, width)
            blocks_of(act, body)

        @block.vector
        def _(dve):
            dve.memset(eps[:], EPS)
            for k in range(W):
                dve.memset(hid[k][64:65, :], 1.0)
            dve.wait_ge(s["weights"], NW)
            dve.tensor_tensor(wplus[:], wself[:], ident[:], ALU.add).then_inc(s["ready"], 1)

            def body(i, width, first):
                n = width * U

                def add_bias(g, k):
                    dve.wait_ge(s["s_ps"], g + 1)
                    dve.tensor_tensor(u[k][:], wide(ps_b[k]), bias[:], ALU.add).then_inc(s["u"], 1)

                def bias_h(l):
                    def one(g, k):
                        dve.wait_ge(s[f"h_ps{l}"], g + 1)
                        ps = ps_a[k] if l == 0 else ps_b[k]
                        dve.tensor_scalar(hT[l + 1][k][:], ps[:], b2c[:, l:l + 1], None, ALU.add).then_inc(s[f"hT{l + 1}"], 1)
                    return one

                def residual(g, k):
                    dve.wait_ge(s["h_ps2"], g + 1)
                    dve.tensor_tensor(u3[k][:], wide(ps_a[k]), x2[k][:], ALU.add).then_inc(s["u3"], 1)

                def add_b2(g, k):
                    dve.wait_ge(s["x3"], g + 1)
                    dve.tensor_tensor(u4[k][:], x3[k][:], b2[:], ALU.add).then_inc(s["u4"], 1)

                each(i, width, add_bias)
                dve.wait_ge(s["u"], i * W + width)
                norm0.statistics(dve, u[:width], i)
                norm0.inverse(dve, i, width)
                dve.tensor_tensor(sq[:, 0:n], norm0.rstd[:, 0:n], norm0.rstd[:, 0:n], ALU.mult).then_inc(s["sq"], 1)
                dve.wait_ge(s["sq"], i + 1)
                dve.tensor_tensor(v1[:, 0:n], sq[:, 0:n], norm0.mv[:, 0:n, 1], ALU.mult).then_inc(s["v1"], 1)
                for k in range(width):
                    if not first:
                        dve.wait_ge(s_stored[k], 16 * STORES * i)
                    norm0.normalize(dve, x1[k], u[k], s["x1"], k)
                dve.wait_ge(s["root1"], i + 1)
                dve.reciprocal(rstd1[:, 0:n], root1[:, 0:n]).then_inc(s["rstd1"], 1)
                each(i, width, bias_h(0))
                each(i, width, bias_h(1))
                each(i, width, residual)
                dve.wait_ge(s["u3"], i * W + width)
                norm3.statistics(dve, u3[:width], i)
                norm3.inverse(dve, i, width)
                for k in range(width):
                    norm3.normalize(dve, x3[k], u3[k], s["x3"], k)
                each(i, width, add_b2)
                dve.wait_ge(s["u4"], i * W + width)
                norm4.statistics(dve, u4[:width], i)
                norm4.inverse(dve, i, width)
                for k in range(width):
                    norm4.normalize(dve, x4[k], u4[k], s["x4"], k)
            blocks_of(dve, body)



class Stream:

    def __init__(self, ph, name, table, index, ps, after=None):
        self.table, self.flat, self.ps = table, index, ps
        self.index = ph.sb(f"{name}_index", [P, U], I32)
        self.tile = ph.sb(f"{name}_tile", [P, U, C])
        self.s_index, self.s_rows, self.s_turned, self.s_T = (
            ph.sem(f"{name}_{x}") for x in ("index", "rows", "turned", "T"))
        self.T = ph.sb(f"{name}_T", [P, CH])

    def load_index(self, sp, i, first):
        if not first:
            sp.wait_ge(self.s_turned, i)
        sp.dma_start(self.index[:], chunk(self.flat, i)).then_inc(self.s_index, 16)

    def fetch(self, pool, i, first, s_passed):
        if not first:
            gate(pool, self.s_turned, i, s_passed)
        gate(pool, self.s_index, 16 * (i + 1), s_passed)
        for u in range(U):
            gather(pool, self.tile, self.table, self.index, u, self.s_rows)

    def turn(self, pe, i, first, ident, busy=None):
        pe.wait_ge(self.s_rows, 16 * U * (i + 1))
        if busy is not None:
            pe.wait_ge(*busy)
        for u in range(U):
            ins = pe.transpose(slot(self.ps, u), self.tile[:, u, :], ident[:])
        ins.then_inc(self.s_turned, 1)

    def copy_out(self, act, i, first, free=None):
        act.wait_ge(self.s_turned, i + 1)
        if free is not None:
            act.wait_ge(*free)
        act.copy(self.T[:], self.ps[:]).then_inc(self.s_T, 1)


class Put:

    def __init__(self, ph, name, table, index, last_row):
        self.table, self.flat, self.last_row = table, index, last_row
        self.index = ph.sb(f"{name}_index", [P, U], I32)
        self.tile = ph.sb(f"{name}_tile", [P, U, C])
        self.s_index, self.s_made, self.s_put = (ph.sem(f"{name}_{x}") for x in ("index", "made", "put"))

    def load_index(self, sp, i, first):
        if not first:
            sp.wait_ge(self.s_put, 16 * U * i)
        sp.dma_start(self.index[:], chunk(self.flat, i)).then_inc(self.s_index, 16)

    def put(self, pool, i, s_passed):
        gate(pool, self.s_made, i + 1, s_passed)
        gate(pool, self.s_index, 16 * (i + 1), s_passed)
        for u in range(U):
            scatter(pool, self.table, self.tile, self.index, u, self.s_put, self.last_row)

    def free(self, eng, i, first):
        if not first:
            eng.wait_ge(self.s_put, 16 * U * i)


def sp_steps(sp, body, puts, ahead=1):
    for i in range(ahead + 1):
        body(i, i == 0)
    for p in puts:
        p.load_index(sp, 0, True)
    with sp.Fori(ahead + 1, NC) as i:
        body(i, False)
        for p in puts:
            p.load_index(sp, i - ahead, False)
    for i in range(NC - ahead, NC):
        for p in puts:
            p.load_index(sp, i, False)


def pool_steps(pool, streams, puts, s_passed, more=None, ahead=1):
    def fetch(i, first):
        for st in streams:
            st.fetch(pool, i, first, s_passed)
        if more:
            more(i, first)

    for i in range(ahead):
        fetch(i, i == 0)
    with pool.Fori(ahead, NC) as i:
        fetch(i, False)
        for put in puts:
            put.put(pool, i - ahead, s_passed)
    for i in range(NC - ahead, NC):
        for put in puts:
            put.put(pool, i, s_passed)
    for put in puts:
        pool.wait_ge(put.s_put, 16 * U * NC)


def edge_attention(nc, w, tab, flat):
    with Phase(nc, "l1") as ph:
        ident = ph.sb("ident", [P, P])
        w23 = ph.sb("w23", [P, 2])
        w3b = ph.sb("w3b", [P, P])
        ones = ph.sb("ones", [P, P])
        eps = ph.sb("eps", [P, 1])
        run = ph.sb("run", [P, CH])
        prod = ph.sb("prod", [P, CH])
        msg = ph.sb("msg", [P, CH])
        agg = ph.sb("agg", [P, CH])
        carry = ph.sb("carry", [P, 1])
        both = ph.sb("both", [P, CH])
        ps_src, ps_dst, ps_att, ps_out = (ph.ps(n) for n in ("ps_src", "ps_dst", "ps_att", "ps_out"))
        src = Stream(ph, "src", tab["x1"], flat["src_d"], ps_src)
        dst = Stream(ph, "dst", tab["x1"], flat["dst_d"], ps_dst)
        put = Put(ph, "x2", tab["x2"], flat["put_d"], N - 1)
        norm = Norm(ph, "norm", eps)
        s = {n: ph.sem(n) for n in ("weights", "ready", "run", "prod", "att", "msg", "agg", "carry", "both", "out",
                                    "passed")}
        block = ph.block()

        @block.sync
        def _(sp):
            sp.dma_start(ident[:], w["ident"]).then_inc(s["weights"], 16)
            sp.dma_start(w23[:], w["l1_w23"]).then_inc(s["weights"], 16)

            def body(i, first):
                src.load_index(sp, i, first)
                dst.load_index(sp, i, first)
                if not first:
                    sp.wait_ge(s["agg"], i)
                sp.dma_start(run[:], rows(flat["run_d"], i)).then_inc(s["run"], 16)
            sp_steps(sp, body, (put,))

        @block.gpsimd
        def _(pool):
            pool_steps(pool, (src, dst), (put,), s["passed"])

        @block.tensor
        def _(pe):
            pe.wait_ge(s["weights"], 32)
            pe.wait_ge(s["ready"], 3)

            def body(i, first):
                src.turn(pe, i, first, ident, None if first else (src.s_T, i))
                dst.turn(pe, i, first, ident, None if first else (dst.s_T, i))
                pe.wait_ge(s["prod"], i + 1)
                pe.matmul(ps_att[:], w3b[:], prod[:], start=True, stop=True).then_inc(s["att"], 1)
                pe.wait_ge(s["both"], i + 1)
                if not first:
                    pe.wait_ge(put.s_made, i)
                for u in range(U):
                    ins = pe.transpose(ps_out[:, u * C:(u + 1) * C], slot(both, u), ident[:])
                ins.then_inc(s["out"], 1)
            steps(pe, NC, body)

        @block.scalar
        def _(act):
            def body(i, first):
                src.copy_out(act, i, first, None if first else (s["msg"], i))
                dst.copy_out(act, i, first, None if first else (s["both"], i))
                norm.rootof(act, i)
            steps(act, NC, body)

        @block.vector
        def _(dve):
            dve.memset(eps[:], EPS)
            dve.memset(carry[:], 0.0)
            dve.memset(ones[:], 1.0).then_inc(s["ready"], 1)
            dve.wait_ge(s["ready"], 1)
            dve.wait_ge(s["weights"], 32)
            dve.tensor_scalar(w3b[:], ones[:], w23[:, 1:2], None, ALU.mult).then_inc(s["ready"], 1)
            dve.wait_ge(s["ready"], 2)
            dve.sem_inc(s["ready"], 1)

            def body(i, first):
                dve.wait_ge(src.s_T, i + 1)
                dve.wait_ge(dst.s_T, i + 1)
                if not first:
                    dve.wait_ge(s["att"], i)
                dve.tensor_tensor(prod[:], src.T[:], dst.T[:], ALU.mult).then_inc(s["prod"], 1)
                dve.wait_ge(s["att"], i + 1)
                if not first:
                    dve.wait_ge(s["carry"], i)
                dve.scalar_tensor_tensor(out=msg[:], in0=src.T[:], scalar=w23[:, 0:1], in1=ps_att[:],
                                         op0=ALU.mult, op1=ALU.mult).then_inc(s["msg"], 1)
                dve.wait_ge(s["msg"], i + 1)
                dve.wait_ge(s["run"], 16 * (i + 1))
                dve.tensor_tensor_scan(agg[:], run[:], msg[:], carry[:, 0:1], ALU.mult, ALU.add).then_inc(s["agg"], 1)
                dve.wait_ge(s["agg"], i + 1)
                dve.tensor_copy(carry[:], agg[:, CH - 1:CH]).then_inc(s["carry"], 1)
                if not first:
                    dve.wait_ge(s["out"], i)
                dve.tensor_tensor(both[:], agg[:], dst.T[:], ALU.add).then_inc(s["both"], 1)
                dve.wait_ge(s["out"], i + 1)
                norm.statistics(dve, [ps_out[:].rearrange("p (u c) -> p u c", u=U)], i)
                norm.inverse(dve, i)
                put.free(dve, i, first)
                norm.normalize(dve, put.tile, ps_out[:].rearrange("p (u c) -> p u c", u=U), put.s_made)
            steps(dve, NC, body)


def edge_perceptrons(nc, l, w, tab, flat):
    last = l == 2
    with Phase(nc, f"l2_{l}") as ph:
        ident = ph.sb("ident", [P, P])
        e1 = [ph.sb(f"e1_{x}", [P, C]) for x in ("src", "dst")]
        e2 = ph.sb("e2", [P, 64])
        eb1 = ph.sb("eb1", [P, 1])
        eb2 = ph.sb("eb2", [64, 1])
        n1m = ph.sb("n1m", [64, 64])
        n1h = ph.sb("n1h", [P, 64])
        nb1 = ph.sb("nb1", [64, 1])
        n2 = ph.sb("n2", [65, C])
        eps = ph.sb("eps", [P, 1])
        run = ph.sb("run", [64, CH])
        kind = ph.sb("kind", [64, CH])
        inv = ph.sb("inv", [64, CH])
        z = ph.sb("z", [P, CH])
        msg = ph.sb("msg", [64, CH])
        agg = ph.sb("agg", [64, CH])
        carry = ph.sb("carry", [64, 1])
        mean = ph.sb("mean", [64, CH])
        hid = ph.sb("hid", [65, CH])
        ps_src, ps_dst, ps_z, ps_m, ps_hid, ps_out = (
            ph.ps(n) for n in ("ps_src", "ps_dst", "ps_z", "ps_m", "ps_hid", "ps_out"))
        table = tab[("x2", "h1", "h2")[l]]
        src = Stream(ph, "src", table, flat["src_d"], ps_src)
        dst = Stream(ph, "dst", table, flat["dst_d"], ps_dst)
        put = Put(ph, "put", tab[("h1", "h2", "x3")[l]], flat["put_d"], N - 1)
        puts = [put]
        s = {n: ph.sem(n) for n in ("weights", "ready", "masks", "z_ps", "z", "m_ps", "msg", "agg", "carry", "mean",
                                    "hid_ps", "hid", "out", "passed", "pe_passed")}
        if last:
            b2 = ph.sb("b2", [P, U, C])
            res = ph.sb("res_tile", [P, U, C])
            res_index = ph.sb("res_index", [P, U], I32)
            u3 = ph.sb("u3", [P, U, C])
            u4 = ph.sb("u4", [P, U, C])
            s |= {n: ph.sem(n) for n in ("res_index", "res", "u3", "u4")}
            norm3, norm4 = Norm(ph, "norm3", eps), Norm(ph, "norm4", eps)
            put4 = Put(ph, "put4", tab["out"], flat["put_d"], N - 1)
            puts.append(put4)
        block = ph.block()
        loads = [(ident[:], w["ident"]), (e1[0][:], w["eW1"][l, 0]), (e1[1][:], w["eW1"][l, 1]),
                 (eb1[:], w["eb1"][l]), (eb2[:], w["eb2"][l]), (n1m[:], w["nW1"][l, 0:64, :]),
                 (n1h[:], w["nW1"][l, 64:192, :]), (nb1[:], w["nb1_cols"][l]), (n2[0:64, :], w["nW2"][l]),
                 (n2[64:65, :], w["nb2_rows"][l:l + 1, :])]
        late = [(e2[0:64, 0:32], w["eW2"][l, 0]), (e2[64:128, 32:64], w["eW2"][l, 1])]
        if last:
            loads.append((b2[:], w["b2"].rearrange("(a b c) -> a b c", a=1, b=1).to_broadcast([P, U, C])))
        NW = 16 * (len(loads) + len(late))

        @block.sync
        def _(sp):
            for d, f in loads:
                sp.dma_start(d, f).then_inc(s["weights"], 16)
            sp.wait_ge(s["ready"], 1)
            for d, f in late:
                sp.dma_start(d, f).then_inc(s["weights"], 16)

            def body(i, first):
                src.load_index(sp, i, first)
                dst.load_index(sp, i, first)
                if not first:
                    sp.wait_ge(s["mean"], i)
                sp.dma_start(run[:], rows(flat["run_d"], i, 64)).then_inc(s["masks"], 16)
                for q in range(2):
                    sp.dma_start(kind[32 * q:32 * q + 32, :], rows(flat[f"kind{q}_d"], i, 32)).then_inc(s["masks"], 16)
                    sp.dma_start(inv[32 * q:32 * q + 32, :], rows(flat[f"inv{q}_d"], i, 32)).then_inc(s["masks"], 16)
                if last:
                    if not first:
                        sp.wait_ge(s["u3"], i)
                    sp.dma_start(res_index[:], chunk(flat["dst_d"], i)).then_inc(s["res_index"], 16)
            sp_steps(sp, body, puts)

        @block.gpsimd
        def _(pool):
            if not last:
                pool_steps(pool, (src, dst), puts, s["passed"])
                return

            def residual(i, first):
                if not first:
                    gate(pool, s["u3"], i, s["passed"])
                gate(pool, s["res_index"], 16 * (i + 1), s["passed"])
                for u in range(U):
                    gather(pool, res, tab["x2"], res_index, u, s["res"])
            src.fetch(pool, 0, True, s["passed"])
            dst.fetch(pool, 0, True, s["passed"])
            residual(0, True)
            with pool.Fori(1, NC) as i:
                src.fetch(pool, i, False, s["passed"])
                dst.fetch(pool, i, False, s["passed"])
                for p in puts:
                    p.put(pool, i - 1, s["passed"])
                residual(i, False)
            for p in puts:
                p.put(pool, NC - 1, s["passed"])
            for p in puts:
                pool.wait_ge(p.s_put, 16 * U * NC)

        @block.tensor
        def _(pe):
            pe.wait_ge(s["weights"], NW)
            pe.wait_ge(s["ready"], 1)

            def body(i, first):
                src.turn(pe, i, first, ident, None if first else (src.s_T, i))
                dst.turn(pe, i, first, ident, None if first else (dst.s_T, i))
                pe.wait_ge(src.s_T, i + 1)
                if not first:
                    pe.wait_ge(s["z"], i)
                pe.matmul(ps_z[:], e1[0][:], src.T[:], start=True, stop=False)
                pe.wait_ge(dst.s_T, i + 1)
                pe.matmul(ps_z[:], e1[1][:], dst.T[:], start=False, stop=True).then_inc(s["z_ps"], 1)
                pe.wait_ge(s["z"], i + 1)
                if not first:
                    pe.wait_ge(s["msg"], i)
                pe.matmul(ps_m[0:64, :], e2[:], z[:], start=True, stop=True).then_inc(s["m_ps"], 1)
                if not first:
                    pe.wait_ge(s["hid"], i)
                pe.matmul(ps_hid[0:64, :], n1h[:], dst.T[:], start=True, stop=False)
                gate(pe, s["mean"], i + 1, s["pe_passed"])
                pe.matmul(ps_hid[0:64, :], n1m[:], mean[:], start=False, stop=True).then_inc(s["hid_ps"], 1)
                pe.wait_ge(s["hid"], i + 1)
                if not first:
                    pe.wait_ge(s["u3"] if last else put.s_made, i)
                for u in range(U):
                    ins = pe.matmul(ps_out[:, u * C:(u + 1) * C], slot(hid, u), n2[:], start=True, stop=True)
                ins.then_inc(s["out"], 1)
            steps(pe, NC, body)

        @block.scalar
        def _(act):
            def body(i, first):
                src.copy_out(act, i, first, None if first else (s["z_ps"], i))
                dst.copy_out(act, i, first, None if first else (s["hid_ps"], i))
                act.wait_ge(s["z_ps"], i + 1)
                if not first:
                    act.wait_ge(s["m_ps"], i)
                act.activation(z[:], ps_z[:], ACT.Relu, bias=eb1[:, 0:1]).then_inc(s["z"], 1)
                act.wait_ge(s["hid_ps"], i + 1)
                if not first:
                    act.wait_ge(s["out"], i)
                act.activation(hid[0:64, :], ps_hid[0:64, :], ACT.Relu, bias=nb1[:, 0:1]).then_inc(s["hid"], 1)
                if last:
                    norm3.rootof(act, i)
                    norm4.rootof(act, i)
                else:
                    act.wait_ge(s["out"], i + 1)
                    put.free(act, i, first)
                    act.copy(put.tile[:], ps_out[:].rearrange("p (u c) -> p u c", u=U)).then_inc(put.s_made, 1)
            steps(act, NC, body)

        @block.vector
        def _(dve):
            dve.memset(e2[:], 0.0)
            dve.memset(eps[:], EPS)
            dve.memset(hid[64:65, :], 1.0)
            dve.memset(carry[:], 0.0).then_inc(s["ready"], 1)
            dve.wait_ge(s["weights"], NW)
            dve.wait_ge(s["ready"], 1)

            def body(i, first):
                dve.wait_ge(s["m_ps"], i + 1)
                dve.wait_ge(s["masks"], 80 * (i + 1))
                dve.scalar_tensor_tensor(out=msg[:], in0=ps_m[0:64, :], scalar=eb2[:, 0:1], in1=kind[:],
                                         op0=ALU.add, op1=ALU.mult).then_inc(s["msg"], 1)
                dve.wait_ge(s["msg"], i + 1)
                if not first:
                    dve.wait_ge(s["carry"], i)
                dve.tensor_tensor_scan(agg[:], run[:], msg[:], carry[:, 0:1], ALU.mult, ALU.add).then_inc(s["agg"], 1)
                dve.wait_ge(s["agg"], i + 1)
                dve.tensor_copy(carry[:], agg[:, CH - 1:CH]).then_inc(s["carry"], 1)
                if not first:
                    dve.wait_ge(s["hid_ps"], i)
                dve.tensor_tensor(mean[:], agg[:], inv[:], ALU.mult).then_inc(s["mean"], 1)
                if last:
                    dve.wait_ge(s["out"], i + 1)
                    dve.wait_ge(s["res"], 16 * U * (i + 1))
                    if not first:
                        dve.wait_ge(put.s_made, i)
                    dve.tensor_tensor(u3[:], ps_out[:].rearrange("p (u c) -> p u c", u=U), res[:], ALU.add
                                      ).then_inc(s["u3"], 1)
                    dve.wait_ge(s["u3"], i + 1)
                    norm3.statistics(dve, [u3], i)
                    norm3.inverse(dve, i)
                    put.free(dve, i, first)
                    norm3.normalize(dve, put.tile, u3, put.s_made)
                    dve.wait_ge(put.s_made, i + 1)
                    if not first:
                        dve.wait_ge(put4.s_made, i)
                    dve.tensor_tensor(u4[:], put.tile[:], b2[:], ALU.add).then_inc(s["u4"], 1)
                    dve.wait_ge(s["u4"], i + 1)
                    norm4.statistics(dve, [u4], i)
                    norm4.inverse(dve, i)
                    put4.free(dve, i, first)
                    norm4.normalize(dve, put4.tile, u4, put4.s_made)
            steps(dve, NC, body)


def hyper_edges(nc, name, source, w_name, target, w, flat, affine=None):
    with Phase(nc, name) as ph:
        ident = ph.sb("ident", [P, P])
        wt = ph.sb("wt", [P, C])
        ac = ph.sb("ac", [P, 2])
        run = ph.sb("run", [P, CH])
        inv = ph.sb("inv", [P, CH])
        agg = ph.sb("agg", [P, CH])
        carry = ph.sb("carry", [P, 1])
        mean = ph.sb("mean", [P, CH])
        zero = ph.sb("zero", [1, C])
        ps_src, ps_out = ph.ps("ps_src"), ph.ps("ps_out")
        src = Stream(ph, "src", source, flat["src_d"], ps_src)
        put = Put(ph, "put", target, flat["put_d"], H5 - 1)
        s = {n: ph.sem(n) for n in ("weights", "ready", "masks", "agg", "carry", "mean", "aff", "out", "passed",
                                    "zeroed")}
        block = ph.block()

        @block.sync
        def _(sp):
            sp.dma_start(ident[:], w["ident"]).then_inc(s["weights"], 16)
            sp.dma_start(wt[:], w[w_name]).then_inc(s["weights"], 16)
            if affine is not None:
                sp.dma_start(ac[:], affine).then_inc(s["weights"], 16)
            sp.wait_ge(s["ready"], 1)
            sp.dma_start(target[H5 - 1:H5, :], zero[:]).then_inc(s["zeroed"], 16)

            def body(i, first):
                src.load_index(sp, i, first)
                if not first:
                    sp.wait_ge(s["mean"], i)
                sp.dma_start(run[:], rows(flat["run_d"], i)).then_inc(s["masks"], 16)
                sp.dma_start(inv[:], rows(flat["inv_deg_d"], i)).then_inc(s["masks"], 16)
            sp_steps(sp, body, (put,))

        @block.gpsimd
        def _(pool):
            gate(pool, s["zeroed"], 16, s["passed"])
            pool_steps(pool, (src,), (put,), s["passed"])

        NW = 32 if affine is None else 48

        @block.tensor
        def _(pe):
            pe.wait_ge(s["weights"], NW)

            def body(i, first):
                src.turn(pe, i, first, ident, None if first else (s["agg"], i))
                made = s["mean"] if affine is None else s["aff"]
                pe.wait_ge(made, i + 1)
                if not first:
                    pe.wait_ge(put.s_made, i)
                for u in range(U):
                    ins = pe.matmul(ps_out[:, u * C:(u + 1) * C], slot(mean, u), wt[:], start=True, stop=True)
                ins.then_inc(s["out"], 1)
            steps(pe, NC, body)

        @block.scalar
        def _(act):
            act.wait_ge(s["weights"], NW)

            def body(i, first):
                if affine is not None:
                    act.wait_ge(s["mean"], i + 1)
                    act.activation(mean[:], mean[:], ACT.Identity, scale=ac[:, 0:1], bias=ac[:, 1:2]).then_inc(s["aff"], 1)
                act.wait_ge(s["out"], i + 1)
                put.free(act, i, first)
                act.copy(put.tile[:], ps_out[:].rearrange("p (u c) -> p u c", u=U)).then_inc(put.s_made, 1)
            steps(act, NC, body)

        @block.vector
        def _(dve):
            dve.memset(carry[:], 0.0)
            dve.memset(zero[:], 0.0).then_inc(s["ready"], 1)
            dve.wait_ge(s["ready"], 1)

            def body(i, first):
                dve.wait_ge(src.s_turned, i + 1)
                dve.wait_ge(s["masks"], 32 * (i + 1))
                if not first:
                    dve.wait_ge(s["carry"], i)
                dve.tensor_tensor_scan(agg[:], run[:], ps_src[:], carry[:, 0:1], ALU.mult, ALU.add).then_inc(s["agg"], 1)
                dve.wait_ge(s["agg"], i + 1)
                dve.tensor_copy(carry[:], agg[:, CH - 1:CH]).then_inc(s["carry"], 1)
                if not first:
                    dve.wait_ge(s["out"], i)
                dve.tensor_tensor(mean[:], agg[:], inv[:], ALU.mult).then_inc(s["mean"], 1)
            steps(dve, NC, body)


def nodes_of_edges(nc, name, source, target, w, tab, flat, affine):
    final = target is None
    with Phase(nc, name) as ph:
        ident = ph.sb("ident", [P, P])
        run = ph.sb("run", [P, CH])
        inv = ph.sb("inv", [P, CH])
        agg = ph.sb("agg", [P, CH])
        carry = ph.sb("carry", [P, 1])
        g = ph.sb("g", [P, CH])
        ps_src, ps_out = ph.ps("ps_src"), ph.ps("ps_out")
        src = Stream(ph, "src", source, flat["dst_s"], ps_src)
        put = Put(ph, "put", tab["out"] if final else target, flat["put_s"], N - 1)
        s = {n: ph.sem(n) for n in ("weights", "ready", "masks", "agg", "carry", "g", "out", "passed",
                                    "gl", "bn", "step", "affine", "stats")}
        eps = ph.sb("eps", [P, 1])
        if final:
            b2 = ph.sb("b2", [P, U, C])
            res = Stream(ph, "res", tab["x3"], flat["src_s"], None)
            res.s_turned = ph.sem("res_used")
            resb = ph.sb("resb", [P, U, C])
            u4 = ph.sb("u4", [P, U, C])
            norm = Norm(ph, "norm", eps)
            s |= {n: ph.sem(n) for n in ("resb", "u4")}
        else:
            last = ph.sb("last", [P, CH])
            gl = ph.sb("gl", [P, CH])
            stats = ph.sb("stats", [P, NC, 6])
            gb = ph.sb("gb", [P, 2])
            mv = ph.sb("mv", [P, 2])
            t = {n: ph.sb(n, [P, 1]) for n in ("mean", "sq", "var", "var2", "root", "rstd", "am")}
            ac = ph.sb("ac", [P, 2])
        block = ph.block()

        @block.sync
        def _(sp):
            sp.dma_start(ident[:], w["ident"]).then_inc(s["weights"], 16)
            if final:
                sp.dma_start(b2[:], w["b2"].rearrange("(a b c) -> a b c", a=1, b=1).to_broadcast([P, U, C])
                             ).then_inc(s["weights"], 16)
            else:
                sp.dma_start(gb[:], w["gamma_beta"]).then_inc(s["weights"], 16)

            def body(i, first):
                src.load_index(sp, i, first)
                if final:
                    res.load_index(sp, i, first)
                if not first:
                    sp.wait_ge(s["g"] if final else s["gl"], i)
                sp.dma_start(run[:], rows(flat["run_s"], i)).then_inc(s["masks"], 16)
                sp.dma_start(inv[:], rows(flat["inv_w_s"], i)).then_inc(s["masks"], 16)
                if not final:
                    sp.dma_start(last[:], rows(flat["last_s"], i)).then_inc(s["masks"], 16)
            sp_steps(sp, body, (put,))
            if not final:
                sp.wait_ge(s["bn"], 1)
                sp.dma_start(affine, ac[:]).then_inc(s["affine"], 16)
                sp.wait_ge(s["affine"], 16)

        @block.gpsimd
        def _(pool):
            pool_steps(pool, (src, res) if final else (src,), (put,), s["passed"])

        @block.tensor
        def _(pe):
            pe.wait_ge(s["weights"], 32)

            def body(i, first):
                src.turn(pe, i, first, ident, None if first else (s["agg"], i))
                pe.wait_ge(s["g"], i + 1)
                if not first:
                    pe.wait_ge(s["u4"] if final else put.s_made, i)
                for u in range(U):
                    ins = pe.transpose(ps_out[:, u * C:(u + 1) * C], slot(g, u), ident[:])
                ins.then_inc(s["out"], 1)
            steps(pe, NC, body)

        @block.scalar
        def _(act):
            def body(i, first):
                if final:
                    norm.rootof(act, i)
                else:
                    act.wait_ge(s["out"], i + 1)
                    put.free(act, i, first)
                    act.copy(put.tile[:], ps_out[:].rearrange("p (u c) -> p u c", u=U)).then_inc(put.s_made, 1)
            steps(act, NC, body)
            if not final:
                act.wait_ge(s["step"], 5)
                act.activation(t["root"][:], t["var2"][:], ACT.Sqrt, bias=eps[:, 0:1]).then_inc(s["step"], 1)

        @block.vector
        def _(dve):
            dve.memset(eps[:], EPS)
            dve.memset(carry[:], 0.0)
            dve.memset(g[:], 0.0).then_inc(s["ready"], 1)
            dve.wait_ge(s["ready"], 1)
            dve.wait_ge(s["weights"], 32)

            def body(i, first):
                dve.wait_ge(src.s_turned, i + 1)
                dve.wait_ge(s["masks"], (32 if final else 48) * (i + 1))
                if not first:
                    dve.wait_ge(s["carry"], i)
                dve.tensor_tensor_scan(agg[:], run[:], ps_src[:], carry[:, 0:1], ALU.mult, ALU.add).then_inc(s["agg"], 1)
                dve.wait_ge(s["agg"], i + 1)
                dve.tensor_copy(carry[:], agg[:, CH - 1:CH]).then_inc(s["carry"], 1)
                if not first:
                    dve.wait_ge(s["out"], i)
                dve.tensor_tensor(g[:], agg[:], inv[:], ALU.mult).then_inc(s["g"], 1)
                if final:
                    dve.wait_ge(res.s_rows, 16 * U * (i + 1))
                    dve.tensor_tensor(resb[:], res.tile[:], b2[:], ALU.add).then_inc(res.s_turned, 1)
                    dve.wait_ge(res.s_turned, i + 1)
                    dve.wait_ge(s["out"], i + 1)
                    if not first:
                        dve.wait_ge(put.s_made, i)
                    dve.tensor_tensor(u4[:], ps_out[:].rearrange("p (u c) -> p u c", u=U), resb[:], ALU.add
                                      ).then_inc(s["u4"], 1)
                    dve.wait_ge(s["u4"], i + 1)
                    norm.statistics(dve, [u4], i)
                    norm.inverse(dve, i)
                    put.free(dve, i, first)
                    norm.normalize(dve, put.tile, u4, put.s_made)
                else:
                    dve.wait_ge(s["g"], i + 1)
                    dve.tensor_tensor(gl[:], g[:], last[:], ALU.mult).then_inc(s["gl"], 1)
                    dve.wait_ge(s["gl"], i + 1)
                    dve.bn_stats(stats[:, bass.ds(i, 1), :].rearrange("p a f -> p (a f)"), gl[:]
                                 ).then_inc(s["stats"], 1)
                    dve.wait_ge(s["stats"], i + 1)
            steps(dve, NC, body)
            if not final:
                dve.bn_aggr(mv[:], stats[:].rearrange("p n f -> p (n f)")).then_inc(s["step"], 1)
                dve.wait_ge(s["step"], 1)
                dve.tensor_scalar(t["mean"][:], mv[:, 0:1], EP / N, None, ALU.mult)
                dve.tensor_tensor(t["sq"][:], mv[:, 0:1], mv[:, 0:1], ALU.mult).then_inc(s["step"], 1)
                dve.wait_ge(s["step"], 2)
                dve.tensor_scalar(t["sq"][:], t["sq"][:], (EP / N) * ((N - EP) / N), None, ALU.mult).then_inc(s["step"], 1)
                dve.wait_ge(s["step"], 3)
                dve.tensor_scalar(t["var"][:], mv[:, 1:2], EP / N, None, ALU.mult).then_inc(s["step"], 1)
                dve.wait_ge(s["step"], 4)
                dve.tensor_tensor(t["var2"][:], t["var"][:], t["sq"][:], ALU.add).then_inc(s["step"], 1)
                dve.wait_ge(s["step"], 6)
                dve.reciprocal(t["rstd"][:], t["root"][:]).then_inc(s["step"], 1)
                dve.wait_ge(s["step"], 7)
                dve.tensor_tensor(ac[:, 0:1], t["rstd"][:], gb[:, 0:1], ALU.mult).then_inc(s["step"], 1)
                dve.wait_ge(s["step"], 8)
                dve.tensor_tensor(t["am"][:], ac[:, 0:1], t["mean"][:], ALU.mult).then_inc(s["step"], 1)
                dve.wait_ge(s["step"], 9)
                dve.tensor_tensor(ac[:, 1:2], gb[:, 1:2], t["am"][:], ALU.subtract).then_inc(s["bn"], 1)


def fold_attention(nc, w, att):
    with Phase(nc, "fold") as ph:
        wrt = ph.sb("wrt", [P, R, C])
        wct = ph.sb("wct", [P, C])
        wst = ph.sb("wst", [P, C])
        vec = ph.sb("vec", [P, 2 * R + 2])
        heads = ph.sb("heads", [P, H])
        blocks = ph.sb("blocks", [P, 2 * R + 2, H])
        ps = ph.ps("ps")
        s = {n: ph.sem(n) for n in ("weights", "blocks", "ps", "done")}
        block = ph.block()

        @block.sync
        def _(sp):
            for d, f in ((wrt, "W_rel_T"), (wct, "W_cross_T"), (wst, "W_self_T"), (vec, "att_vectors"), (heads, "heads")):
                sp.dma_start(d[:], w[f]).then_inc(s["weights"], 16)

        @block.vector
        def _(dve):
            dve.wait_ge(s["weights"], 80)
            for q in range(2 * R + 2):
                ins = dve.tensor_scalar(blocks[:, q, :], heads[:], vec[:, q:q + 1], None, ALU.mult)
            ins.then_inc(s["blocks"], 1)
            dve.wait_ge(s["ps"], 1)
            dve.tensor_copy(att[:], ps[:, 0:11 * H]).then_inc(s["done"], 1)
            dve.wait_ge(s["done"], 1)

        @block.tensor
        def _(pe):
            pe.wait_ge(s["blocks"], 1)
            at = 0
            for q in range(2 * R):
                pe.matmul(ps[:, at:at + H], wrt[:, q % R, :], blocks[:, q, :], start=True, stop=True)
                at += H
            for m, q in ((wct, 2 * R), (wst, 2 * R), (wst, 2 * R + 1)):
                ins = pe.matmul(ps[:, at:at + H], m[:], blocks[:, q, :], start=True, stop=True)
                at += H
            ins.then_inc(s["ps"], 1)


def relational_attention(nc, w, tab, flat, att):
    RH = R * H
    K = R + 1
    with Phase(nc, "l0") as ph:
        ident = ph.sb("ident", [P, P])
        wrel = ph.sb("wrel", [P, R, C])
        wcross = ph.sb("wcross", [P, C])
        wself = ph.sb("wself", [P, C])
        spread = ph.sb("spread", [RH, R, C])
        spread3 = ph.sb("spread3", [3 * RH, R, C], BF16)
        brel = ph.sb("brel", [P, R])
        rid = ph.sb("rid", [RH, 1])
        bias = ph.sb("bias", [P, U, C])
        eps = ph.sb("eps", [P, 1])
        reset = ph.sb("reset", [RH, CH])
        rel = ph.sb("rel", [RH, CH])
        q = {n: ph.sb(n, [RH, CH]) for n in ("lg", "cap", "lk", "lm", "d1", "d2", "e", "c", "pe", "p")}
        parts = {n: ph.sb(f"parts_{n}", [3 * RH, CH], BF16) for n in "pcr"}
        left = {n: ph.sb(f"left_{n}", [3 * RH, CH]) for n in "pcr"}
        mbuf = ph.sb("mbuf", [RH, CH + 1])
        den = ph.sb("den", [RH, CH])
        dcarry = ph.sb("dcarry", [RH, 1])
        has, hneg = ([ph.sb(f"{n}{b}", [P, U, RH]) for b in range(2)] for n in ("has", "hneg"))
        dmax, rdT = (ph.sb(n, [P, U, RH]) for n in ("dmax", "rdT"))
        y = [ph.sb(f"y{b}", [P, CH]) for b in range(2)]
        py = ph.sb("py", [P, CH])
        num = [ph.sb(f"num{r}", [P, CH]) for r in range(R)]
        ncarry = ph.sb("ncarry", [P, R])
        ro = [ph.sb(f"ro{b}", [P, CH]) for b in range(2)]
        g = [ph.sb(f"g{b}", [P, CH]) for b in range(2)]
        ent = [ph.sb(f"ent{b}", [P, U, K + 1, C]) for b in range(2)]
        lg = {n: ph.sb(n, [P, U, K, H]) for n in ("lg0", "lg1", "lg2", "lg3", "lge", "alpha")}
        ld, mx, sm, rs = (ph.sb(n, [P, U, H]) for n in ("ld", "mx", "sm", "rs"))
        mixed = ph.sb("mixed", [P, U, K, C])
        outc, outb, u0 = (ph.sb(n, [P, U, C]) for n in ("outc", "outb", "u0"))
        ps_x, ps_l, ps_a, ps_y, ps_p, ps_c, ps_q, ps_h = (
            ph.ps(n) for n in ("ps_x", "ps_l", "ps_a", "ps_y", "ps_p", "ps_c", "ps_q", "ps_h"))
        hw_index = ph.sb("hw_index", [P, U], I32)
        hw_rows = ph.sb("hw_rows", [P, U, 1])
        hw = ph.sb("hw", [P, NC, U])
        src = Stream(ph, "src", tab["x"], flat["src_d"], ps_x)
        dst = Stream(ph, "dst", tab["x"], flat["dst_d"], ps_x)
        T = {n: [st.T, ph.sb(f"{n}_T1", [P, CH])] for n, st in (("src", src), ("dst", dst))}
        put = Put(ph, "put", tab["x1"], flat["put_d"], N - 1)
        norm = Norm(ph, "norm", eps)
        names = ["weights", "ready", "spread3", "masks", "logit", "logit_copy", "cap", "lk", "lm", "m", "mshift", "d1", "e", "c",
                 "p", "den", "dcarry", "denT_ps", "dmax", "rdT", "rd_ps", "ld", "lg0", "lg1", "lg2", "lg3", "lg4",
                 "mx", "lg5", "lge", "sm", "rs", "alpha", "mixed", "outc", "x_ps", "x_copy", "outb", "u0", "passed",
                 "ent0", "ent_ps0", "pe_passed", "hw_index", "hw_rows", "hw", "hw_out"]
        names += [f"{n}{r}" for r in range(R) for n in ("y_ps", "y", "p_ps", "c_ps", "spread_ps", "py", "num", "ro", "g", "h_ps", "ent_r")]
        names += [f"{n}_{x}" for n in "pcr" for x in ("part1", "left1", "part2", "left2", "part3")]
        s = {n: ph.sem(n) for n in names}
        block = ph.block()
        loads = [(ident[:], w["ident"]), (wrel[:], w["W_rel"]), (wcross[:], w["W_cross"]), (wself[:], w["W_self"]),
                 (spread[:], w["spread"]), (brel[:], w["bias_rel"]), (rid[:], w["rid"]),
                 (bias[:], w["bias_lang"].rearrange("(a b c) -> a b c", a=1, b=1).to_broadcast([P, U, C]))]
        NW = 16 * len(loads)
        ps_dT = ps_c[:, 0:U * RH].rearrange("p (u x) -> p u x", u=U)
        ps_lg = ps_a[:, 0:U * (K + 1) * H].rearrange("p (u k h) -> p u k h", u=U, k=K + 1)
        AHEAD = 4

        def rounds(eng, body):
            body(0, 0, 0, True, True)
            body(1, 1, 1, True, True)
            body(2, 0, 2, True, True)
            with eng.Fori(0, (NC - 5) // 2) as j:
                body(j * 2 + 3, 1, 3, True, True)
                body(j * 2 + 4, 0, 3, True, True)
            for i in range(3 + (NC - 5) // 2 * 2, NC):
                body(i, i % 2, 3, i + 1 < NC, i + 2 < NC)

        @block.sync
        def _(sp):
            for d, f in loads:
                sp.dma_start(d, f).then_inc(s["weights"], 16)

            def body(c, first):
                src.load_index(sp, c, first)
                dst.load_index(sp, c, first)
                if not first:
                    sp.wait_ge(s["cap"], c)
                    sp.wait_ge(s["d1"], c)
                sp.dma_start(reset[:], rows(flat["reset_d"], c, RH)).then_inc(s["masks"], 16)
                sp.dma_start(rel[:], rows(flat["rel_d"], c, RH)).then_inc(s["masks"], 16)
                if not first:
                    sp.wait_ge(s["hw"], c)
                sp.dma_start(hw_index[:], chunk(flat["dst_s"], c)).then_inc(s["hw_index"], 16)
            sp_steps(sp, body, (put,), AHEAD)
            sp.wait_ge(s["hw"], NC)
            sp.dma_start(flat["weight_s"].rearrange("(c p u) -> p c u", p=P, u=U), hw[:]).then_inc(s["hw_out"], 16)
            sp.wait_ge(s["hw_out"], 16)

        @block.gpsimd
        def _(pool):
            def weights(c, first):
                if not first:
                    gate(pool, s["hw"], c, s["passed"])
                gate(pool, s["hw_index"], 16 * (c + 1), s["passed"])
                for u in range(U):
                    gather(pool, hw_rows, w["hyper_w"], hw_index, u, s["hw_rows"])
            pool_steps(pool, (src, dst), (put,), s["passed"], weights, AHEAD)

        @block.tensor
        def _(pe):
            pe.wait_ge(s["weights"], NW)
            pe.wait_ge(s["spread3"], 3)

            def turn_src(c, after=True):
                src.turn(pe, c, False, ident, (dst.s_T, c) if after else None)

            def turn_dst(c):
                dst.turn(pe, c, False, ident, (src.s_T, c + 1))

            def logits(c, par, first=False):
                pe.wait_ge(dst.s_T, c + 1)
                if not first:
                    pe.wait_ge(s["r_left1"], c)
                pe.matmul(ps_l[0:RH, :], att[:, 0:RH], T["src"][par][:], start=True, stop=False)
                pe.matmul(ps_l[0:RH, :], att[:, RH:2 * RH], T["dst"][par][:], start=False, stop=True).then_inc(s["logit"], 1)

            def sums_T(c):
                gate(pe, s["den"], c + 1, s["pe_passed"])
                for u in range(U):
                    ins = pe.transpose(ps_dT[:, u, :], slot(den, u), ident[0:RH, 0:RH])
                ins.then_inc(s["denT_ps"], 1)

            def inverse_back(c):
                pe.wait_ge(s["rdT"], c + 1)
                for u in range(U):
                    ins = pe.transpose(slot(ps_l[0:RH], u), rdT[:, u, :], ident[:])
                ins.then_inc(s["rd_ps"], 1)

            def body(i, par, past, next1, next2):
                for n in "pc":
                    pe.wait_ge(s[f"{n}_part3"], i + 1)

                def spread_out(r):
                    if r:
                        pe.wait_ge(s[f"ro{r - 1}"], i + 1)
                    elif past:
                        pe.wait_ge(s[f"ro{R - 1}"], i)
                    pe.matmul(ps_y[:], wrel[:, r, :], T["src"][par][:], start=True, stop=True).then_inc(s[f"y_ps{r}"], 1)
                    pe.matmul(ps_p[:], spread3[:, r, :], parts["p"][:], start=True, stop=True).then_inc(s[f"p_ps{r}"], 1)
                    pe.matmul(ps_c[:], spread3[:, r, :], parts["c"][:], start=True, stop=True).then_inc(s[f"c_ps{r}"], 1)
                    if r == 0:
                        pe.wait_ge(s["r_part3"], i + 1)
                    pe.matmul(ps_q[:], spread3[:, r, :], parts["r"][:], start=True, stop=True).then_inc(s[f"spread_ps{r}"], 1)

                def cross(r):
                    pe.wait_ge(s[f"g{r}"], i + 1)
                    pe.wait_ge(s["ent0"] if r == 0 else s[f"ent_r{r - 1}"], i + 1)
                    for u in range(U):
                        pe.matmul(ps_h[:, u * C:(u + 1) * C], slot(g[r % 2], u), wcross[:], start=True, stop=True)
                        ins = pe.matmul(ps_lg[:, u, r + 1, :], slot(g[r % 2], u), att[:, 8 * H:9 * H], start=True, stop=True)
                    ins.then_inc(s[f"h_ps{r}"], 1)

                def own():
                    if past:
                        pe.wait_ge(s["x_copy"], i)
                        pe.wait_ge(s["lg0"], i)
                    for u in range(U):
                        ins = pe.matmul(ps_h[:, u * C:(u + 1) * C], slot(T["dst"][par], u), wself[:], start=True, stop=True)
                    ins.then_inc(s["ent_ps0"], 1)
                    for u in range(U):
                        pe.matmul(ps_lg[:, u, 0, :], slot(T["dst"][par], u), att[:, 9 * H:10 * H], start=True, stop=True)
                        pe.matmul(ps_lg[:, u, K, :], slot(T["dst"][par], u), att[:, 10 * H:11 * H], start=True, stop=True)

                spread_out(0)
                if next1:
                    turn_dst(i + 1)
                own()
                for r in range(R):
                    if r + 1 < R:
                        spread_out(r + 1)
                    if r == 0 and next1:
                        logits(i + 1, 1 - par)
                    cross(r)
                if next1:
                    sums_T(i + 1)
                pe.wait_ge(s[f"ent_r{R - 1}"], i + 1)
                for u in range(U):
                    ins = pe.transpose(ps_h[:, u * C:(u + 1) * C], slot(T["dst"][par], u), ident[:])
                ins.then_inc(s["x_ps"], 1)
                if next1:
                    inverse_back(i + 1)
                if next2:
                    turn_src(i + 2)

            turn_src(0, False)
            turn_dst(0)
            logits(0, 0, True)
            sums_T(0)
            turn_src(1)
            inverse_back(0)
            rounds(pe, body)

        @block.scalar
        def _(act):
            act.wait_ge(s["weights"], NW)
            for j in range(3):
                act.copy(spread3[j * RH:(j + 1) * RH], spread[:]).then_inc(s["spread3"], 1)

            def turned(n, c, par, first=False):
                st, used = {"src": (src, f"spread_ps{R - 1}"), "dst": (dst, "x_ps")}[n]
                act.wait_ge(st.s_turned, c + 1)
                if not first:
                    act.wait_ge(s[used], c - 1)
                act.copy(T[n][par][:], ps_x[:]).then_inc(st.s_T, 1)

            def copy_logits(c):
                act.wait_ge(s["logit"], c + 1)
                if not isinstance(c, int) or c:
                    act.wait_ge(s["lk"], c)
                act.copy(q["lg"][:], ps_l[0:RH, :]).then_inc(s["logit_copy"], 1)

            def part(n, c, k, source):
                at = slice((k - 1) * RH, k * RH)
                act.copy(parts[n][at], source).then_inc(s[f"{n}_part{k}"], 1)

            def factors(c, first):
                act.wait_ge(s["e"], c + 1)
                act.activation(q["c"][:], q["d2"][:], ACT.Exp)
                act.activation(q["pe"][:], q["e"][:], ACT.Exp).then_inc(s["c"], 1)
                if not first:
                    act.wait_ge(s[f"spread_ps{R - 1}"], c)
                act.wait_ge(s["c"], c + 1)
                part("c", c, 1, q["c"][:])

            def parts_of(names, c, k):
                for n in names:
                    act.wait_ge(s[f"{n}_left{k - 1}"], c + 1)
                    part(n, c, k, left[n][(k - 1) * RH:k * RH])

            def p_part(c):
                act.wait_ge(s["p"], c + 1)
                part("p", c, 1, q["p"][:])

            def inverse_part(c):
                act.wait_ge(s["rd_ps"], c + 1)
                part("r", c, 1, ps_l[0:RH, :])

            def body(i, par, past, next1, next2):
                def rows_out(k, done):
                    act.copy(ent[par][:, :, k, :], ps_h[:].rearrange("p (u c) -> p u c", u=U)).then_inc(done, 1)

                def copy_y(r):
                    act.wait_ge(s[f"y_ps{r}"], i + 1)
                    act.copy(y[r % 2][:], ps_y[:]).then_inc(s[f"y{r}"], 1)

                copy_y(0)
                if next1:
                    turned("dst", i + 1, 1 - par, past == 0)
                act.wait_ge(s["ent_ps0"], i + 1)
                if past > 1:
                    act.wait_ge(s["mixed"], i - 1)
                rows_out(0, s["ent0"])
                for r in range(R):
                    act.wait_ge(s[f"ro{r}"], i + 1)
                    act.activation(g[r % 2][:], ro[r % 2][:], ACT.Gelu, bias=brel[:, r:r + 1]).then_inc(s[f"g{r}"], 1)
                    if r + 1 < R:
                        copy_y(r + 1)
                    if r == 0 and next1:
                        copy_logits(i + 1)
                    if r == R - 1 and next1:
                        factors(i + 1, False)
                    act.wait_ge(s[f"h_ps{r}"], i + 1)
                    rows_out(r + 1, s[f"ent_r{r}"])
                if next1:
                    p_part(i + 1)
                act.wait_ge(s["x_ps"], i + 1)
                if past > 1:
                    act.wait_ge(s["u0"], i - 1)
                rows_out(K, s["x_copy"])
                if next1:
                    parts_of("cp", i + 1, 2)
                    inverse_part(i + 1)
                act.wait_ge(s["lg5"], i + 1)
                act.activation(lg["lge"][:], lg["lg2"][:], ACT.Exp).then_inc(s["lge"], 1)
                if next1:
                    parts_of("cp", i + 1, 3)
                    parts_of("r", i + 1, 2)
                if next2:
                    turned("src", i + 2, par)
                if next1:
                    parts_of("r", i + 1, 3)
                if past:
                    norm.rootof(act, i - 1)

            for n in ("src", "dst"):
                turned(n, 0, 0, True)
            copy_logits(0)
            factors(0, True)
            p_part(0)
            parts_of("cp", 0, 2)
            parts_of("cp", 0, 3)
            turned("src", 1, 1, True)
            inverse_part(0)
            parts_of("r", 0, 2)
            parts_of("r", 0, 3)
            rounds(act, body)
            norm.rootof(act, NC - 1)

        @block.vector
        def _(dve):
            dve.memset(eps[:], EPS)
            dve.memset(mbuf[:], -NEG)
            dve.memset(dcarry[:], 0.0)
            dve.memset(ncarry[:], 0.0).then_inc(s["ready"], 1)
            dve.wait_ge(s["weights"], NW)
            dve.wait_ge(s["ready"], 1)

            def exponents(c, first):
                dve.wait_ge(s["hw_rows"], 16 * U * (c + 1))
                dve.tensor_copy(hw[:, bass.ds(c, 1), :], hw_rows[:].rearrange("p u a -> p a u")).then_inc(s["hw"], 1)
                dve.wait_ge(s["masks"], 32 * (c + 1))
                dve.tensor_scalar(q["cap"][:], rel[:], rid[:, 0:1], 2 * NEG, ALU.is_equal, ALU.mult).then_inc(s["cap"], 1)
                dve.wait_ge(s["logit_copy"], c + 1)
                dve.scalar_tensor_tensor(out=q["lk"][:], in0=q["lg"][:], scalar=LEAK, in1=q["lg"][:],
                                         op0=ALU.mult, op1=ALU.max).then_inc(s["lk"], 1)
                dve.wait_ge(s["lk"], c + 1)
                dve.wait_ge(s["cap"], c + 1)
                dve.scalar_tensor_tensor(out=q["lm"][:], in0=q["cap"][:], scalar=-NEG, in1=q["lk"][:],
                                         op0=ALU.add, op1=ALU.min).then_inc(s["lm"], 1)
                dve.wait_ge(s["lm"], c + 1)
                dve.tensor_tensor_scan(mbuf[:, 1:CH + 1], reset[:], q["lm"][:], mbuf[:, 0:1], ALU.add, ALU.max
                                       ).then_inc(s["m"], 1)
                dve.wait_ge(s["m"], c + 1)
                dve.tensor_tensor(q["d1"][:], mbuf[:, 0:CH], reset[:], ALU.add).then_inc(s["d1"], 1)
                dve.wait_ge(s["d1"], c + 1)
                if not first:
                    dve.wait_ge(s["c"], c)
                dve.tensor_tensor(q["d2"][:], q["d1"][:], mbuf[:, 1:CH + 1], ALU.subtract)
                dve.tensor_tensor(q["e"][:], q["lm"][:], mbuf[:, 1:CH + 1], ALU.subtract).then_inc(s["e"], 1)
                dve.wait_ge(s["e"], c + 1)
                dve.tensor_copy(mbuf[:, 0:1], mbuf[:, CH:CH + 1]).then_inc(s["mshift"], 1)
                dve.wait_ge(s["mshift"], c + 1)

            def leave(n, c, k, whole):
                dve.wait_ge(s[f"{n}_part{k}"], c + 1)
                dve.tensor_tensor(left[n][k * RH:(k + 1) * RH], whole, parts[n][(k - 1) * RH:k * RH],
                                  ALU.subtract).then_inc(s[f"{n}_left{k}"], 1)

            def sums(c):
                dve.wait_ge(s["c"], c + 1)
                dve.scalar_tensor_tensor(out=q["p"][:], in0=q["cap"][:], scalar=0.0, in1=q["pe"][:],
                                         op0=ALU.is_gt, op1=ALU.mult).then_inc(s["p"], 1)
                dve.wait_ge(s["p"], c + 1)
                dve.tensor_tensor_scan(den[:], q["c"][:], q["p"][:], dcarry[:, 0:1], ALU.mult, ALU.add).then_inc(s["den"], 1)
                dve.wait_ge(s["den"], c + 1)
                dve.tensor_copy(dcarry[:], den[:, CH - 1:CH]).then_inc(s["dcarry"], 1)
                leave("c", c, 1, q["c"][:])
                leave("p", c, 1, q["p"][:])

            def inverse_sums(c, par):
                dve.wait_ge(s["denT_ps"], c + 1)
                dve.tensor_scalar(has[par][:], ps_dT, 0.0, None, ALU.is_gt)
                dve.tensor_scalar(dmax[:], ps_dT, 1e-30, None, ALU.max).then_inc(s["dmax"], 1)
                dve.wait_ge(s["dmax"], c + 1)
                dve.reciprocal(rdT[:], dmax[:]).then_inc(s["rdT"], 1)
                dve.tensor_scalar(hneg[par][:], has[par][:], -1.0, NEG, ALU.add, ALU.mult)

            def second_left(c):
                for n in "cp":
                    dve.wait_ge(s[f"{n}_left1"], c + 1)
                    leave(n, c, 2, left[n][RH:2 * RH])

            def relation(r, i, past):
                dve.wait_ge(s[f"p_ps{r}"], i + 1)
                dve.wait_ge(s[f"y{r}"], i + 1)
                dve.tensor_tensor(py[:], ps_p[:], y[r % 2][:], ALU.mult).then_inc(s[f"py{r}"], 1)
                dve.wait_ge(s[f"py{r}"], i + 1)
                dve.wait_ge(s[f"c_ps{r}"], i + 1)
                dve.tensor_tensor_scan(num[r][:], ps_c[:], py[:], ncarry[:, r:r + 1], ALU.mult, ALU.add
                                       ).then_inc(s[f"num{r}"], 1)
                dve.wait_ge(s[f"num{r}"], i + 1)
                dve.tensor_copy(ncarry[:, r:r + 1], num[r][:, CH - 1:CH])
                if r >= 2:
                    dve.wait_ge(s[f"g{r - 2}"], i + 1)
                elif past:
                    dve.wait_ge(s[f"g{r + 2}"], i)
                dve.wait_ge(s[f"spread_ps{r}"], i + 1)
                dve.tensor_tensor(ro[r % 2][:], num[r][:], ps_q[:], ALU.mult).then_inc(s[f"ro{r}"], 1)

            def softmax_front(i, par):
                dve.wait_ge(s[f"h_ps{R - 1}"], i + 1)
                dve.tensor_copy(ld[:], ps_lg[:, :, K, :]).then_inc(s["ld"], 1)
                dve.wait_ge(s["ld"], i + 1)
                for u in range(U):
                    ins = dve.tensor_tensor(lg["lg0"][:, u], ps_lg[:, u, 0:K, :],
                                            ld[:, u:u + 1, :].to_broadcast([P, K, H]), ALU.add)
                ins.then_inc(s["lg0"], 1)
                dve.wait_ge(s["lg0"], i + 1)
                dve.scalar_tensor_tensor(out=lg["lg3"][:], in0=lg["lg0"][:], scalar=LEAK, in1=lg["lg0"][:],
                                         op0=ALU.mult, op1=ALU.max).then_inc(s["lg2"], 1)
                dve.wait_ge(s["lg2"], i + 1)
                hasv = has[par][:].rearrange("p u (r h) -> p u r h", r=R)
                hnegv = hneg[par][:].rearrange("p u (r h) -> p u r h", r=R)
                dve.tensor_tensor(lg["lg3"][:, :, 1:K, :], lg["lg3"][:, :, 1:K, :], hasv, ALU.mult).then_inc(s["lg3"], 1)
                dve.wait_ge(s["lg3"], i + 1)
                dve.tensor_tensor(lg["lg3"][:, :, 1:K, :], lg["lg3"][:, :, 1:K, :], hnegv, ALU.add).then_inc(s["lg4"], 1)
                dve.wait_ge(s["lg4"], i + 1)
                dve.tensor_reduce(mx[:], lg["lg3"][:].rearrange("p u k h -> p u h k"), AX.X, ALU.max).then_inc(s["mx"], 1)
                dve.wait_ge(s["mx"], i + 1)
                for u in range(U):
                    ins = dve.tensor_tensor(lg["lg2"][:, u], lg["lg3"][:, u], mx[:, u:u + 1, :].to_broadcast([P, K, H]),
                                            ALU.subtract)
                ins.then_inc(s["lg5"], 1)

            def softmax_back(i):
                dve.wait_ge(s["lge"], i + 1)
                dve.tensor_reduce(sm[:], lg["lge"][:].rearrange("p u k h -> p u h k"), AX.X, ALU.add).then_inc(s["sm"], 1)
                dve.wait_ge(s["sm"], i + 1)
                dve.reciprocal(rs[:], sm[:]).then_inc(s["rs"], 1)
                dve.wait_ge(s["rs"], i + 1)
                for u in range(U):
                    ins = dve.tensor_tensor(lg["alpha"][:, u], lg["lge"][:, u], rs[:, u:u + 1, :].to_broadcast([P, K, H]),
                                            ALU.mult)
                ins.then_inc(s["alpha"], 1)

            def mix(i, par):
                dve.wait_ge(s["alpha"], i + 1)
                dve.wait_ge(s["x_copy"], i + 1)
                for u in range(U):
                    a = lg["alpha"][:, u].rearrange("p k h -> p (k h)").rearrange("p (x a) -> p x a", a=1)
                    ins = dve.tensor_tensor(mixed[:, u].rearrange("p k (h d) -> p (k h) d", h=H),
                                            ent[par][:, u, 0:K].rearrange("p k (h d) -> p (k h) d", h=H),
                                            a.to_broadcast([P, K * H, D]), ALU.mult)
                ins.then_inc(s["mixed"], 1)

            def mix_sum(i):
                dve.wait_ge(s["mixed"], i + 1)
                dve.tensor_reduce(outc[:], mixed[:].rearrange("p u k c -> p u c k"), AX.X, ALU.add).then_inc(s["outc"], 1)

            def statistics(i, par):
                dve.wait_ge(s["outc"], i + 1)
                dve.tensor_tensor(outb[:], outc[:], bias[:], ALU.add).then_inc(s["outb"], 1)
                dve.wait_ge(s["outb"], i + 1)
                dve.tensor_tensor(u0[:], ent[par][:, :, K, :], outb[:], ALU.add).then_inc(s["u0"], 1)
                dve.wait_ge(s["u0"], i + 1)
                norm.statistics(dve, [u0], i)

            def finish(i, first=False):
                norm.inverse(dve, i)
                put.free(dve, i, first)
                norm.normalize(dve, put.tile, u0, put.s_made)


            def body(i, par, past, next1, next2):
                relation(0, i, past)
                if past > 1:
                    finish(i - 2, past == 2)
                if past:
                    mix(i - 1, 1 - par)
                relation(1, i, past)
                if next1:
                    exponents(i + 1, False)
                relation(2, i, past)
                if past:
                    mix_sum(i - 1)
                relation(3, i, past)
                if past:
                    statistics(i - 1, 1 - par)
                if next1:
                    sums(i + 1)
                    inverse_sums(i + 1, 1 - par)
                softmax_front(i, par)
                if next1:
                    second_left(i + 1)
                    leave("r", i + 1, 1, ps_l[0:RH, :])
                softmax_back(i)
                if next1:
                    dve.wait_ge(s["r_left1"], i + 2)
                    leave("r", i + 1, 2, left["r"][RH:2 * RH])

            exponents(0, True)
            sums(0)
            inverse_sums(0, 0)
            second_left(0)
            leave("r", 0, 1, ps_l[0:RH, :])
            dve.wait_ge(s["r_left1"], 1)
            leave("r", 0, 2, left["r"][RH:2 * RH])
            rounds(dve, body)
            finish(NC - 2)
            mix(NC - 1, (NC - 1) % 2)
            mix_sum(NC - 1)
            statistics(NC - 1, (NC - 1) % 2)
            finish(NC - 1)



def graph_layers(nc, w, out):
    def dram(name, shape, dtype=F32):
        return nc.dram_tensor(name, shape, dtype).ap()

    tab = {n: dram(f"t_{n}", [N, C]) for n in ("x1", "x2", "h1", "h2", "x3")}
    tab |= {"x": w["x"], "out": out}
    edge_tab = [tab["x1"][0:H5, :], tab["x2"][0:H5, :]]
    node_sums = tab["h1"]
    by_dst, by_src = dram("by_dst", [EP + 2, 4], I32), dram("by_src", [EP + 2, 4], I32)
    flat = {n: dram(f"f_{n}", [EP], I32) for n in ("src_d", "dst_d", "put_d", "src_s", "dst_s", "put_s")}
    flat |= {n: dram(f"f_{n}", [EP]) for n in ("run_d", "run_s", "last_s", "rel_d", "kind0_d", "kind1_d", "reset_d", "ones",
                                               "weight_s", "inv0_d", "inv1_d", "inv_deg_d", "inv_w_s")}
    sums = dram("sums", [4, EP])
    affine = dram("affine", [P, 2])

    sort_edges(nc, w["records"], w, by_dst, by_src)
    derive_orders(nc, by_dst, by_src, flat)
    dense_pass(nc, w, tab)
    with nc.sbuf_tensor("att", [P, 11 * H], F32) as att:
        fold_attention(nc, w, att)
        relational_attention(nc, w, tab, flat, att)
    count_runs(nc, flat, sums)
    edge_attention(nc, w, tab, flat)
    for l in range(3):
        edge_perceptrons(nc, l, w, tab, flat)
    hyper_edges(nc, "l3a", tab["x3"], "W1_T", edge_tab[0], w, flat)
    nodes_of_edges(nc, "l3b", edge_tab[0], node_sums, w, tab, flat, affine)
    hyper_edges(nc, "l3c", node_sums, "W2_T", edge_tab[1], w, flat, affine)
    nodes_of_edges(nc, "l3d", edge_tab[1], None, w, tab, flat, affine)


def layouts(i):
    a = np.ascontiguousarray
    dst_src = np.stack([i["dst"], i["src"]]).astype(np.int32)
    records = np.stack([i["dst"], i["src"], i["edge_type_4"], i["edge_type_2"]], axis=1).astype(np.int32)
    padding = np.array([[N, N, R, R]], np.int32).repeat(EP - E, axis=0)
    heads = (np.arange(C)[:, None] // D == np.arange(H)[None]).astype(np.float32)
    spread = np.zeros((R, H, R, C), np.float32)
    for r in range(R):
        spread[r, :, r, :] = heads.T
    return {
        "x": i["x"],
        "records": np.concatenate([records, padding]),
        "dst_src": np.concatenate([dst_src, np.full((2, EP - E), N, np.int32)], axis=1),
        "hyper_w": i["L3_gnn_hyperedge_weight"].reshape(H5, 1),
        "iota": np.tile(np.arange(CH, dtype=np.float32), (P, 1)),
        "tri": np.triu(np.ones((P, P), np.float32), 1),
        "tri_low": np.tril(np.ones((P, P), np.float32), -1),
        "ident": np.eye(P, dtype=np.float32),
        "heads": heads,
        "spread": spread.reshape(R * H, R, C),
        "rid": (np.arange(R * H) // H).astype(np.float32).reshape(R * H, 1),
        "W_rel": a(i["L0_gnn_W_rel"].transpose(1, 0, 2)),
        "W_rel_T": a(i["L0_gnn_W_rel"].transpose(2, 0, 1)),
        "W_cross": i["L0_gnn_W_cross"],
        "W_cross_T": a(i["L0_gnn_W_cross"].T),
        "W_self": i["L0_gnn_W_self"],
        "W_self_T": a(i["L0_gnn_W_self"].T),
        "att_vectors": a(np.concatenate([i["L0_gnn_att_src_rel"].reshape(R, C), i["L0_gnn_att_dst_rel"].reshape(R, C),
                                         i["L0_gnn_att_src_lang"].reshape(1, C),
                                         i["L0_gnn_att_dst_lang"].reshape(1, C)]).T),
        "bias_rel": a(i["L0_gnn_bias_rel"].T),
        "bias_lang": i["L0_gnn_bias_lang"],
        "l1_w23": a(np.stack([i["L1_gnn_W2"], i["L1_gnn_W3"]], axis=1)),
        "eW1": a(i["L2_gnn_eW1"].reshape(3, 2, 2, C, 64).transpose(0, 2, 3, 1, 4)).reshape(3, 2, C, 2 * 64),
        "eb1": i["L2_gnn_eb1"].reshape(3, 128, 1),
        "eW2": i["L2_gnn_eW2"],
        "eb2": i["L2_gnn_eb2"].reshape(3, 64, 1),
        "nW1": i["L2_gnn_nW1"],
        "nb1": a(i["L2_gnn_nb1"].T),
        "nb1_cols": i["L2_gnn_nb1"].reshape(3, 64, 1),
        "nW2": i["L2_gnn_nW2"],
        "nb2": a(i["L2_gnn_nb2"].T),
        "nb2_rows": i["L2_gnn_nb2"],
        "W1_T": a(i["L3_gnn_W1"].T),
        "W2_T": a(i["L3_gnn_W2"].T),
        "b2": i["L3_gnn_b2"],
        "gamma_beta": a(np.stack([i["L3_gnn_gamma"], i["L3_gnn_beta"]], axis=1)),
    }


def kernel(**inputs):
    import concourse.bacc as bacc
    from concourse.bass_utils import run_bass_kernel_spmd as run

    nc = bacc.Bacc("TRN2", target_bir_lowering=False, num_devices=1)
    arrays = {f"in_{n}": np.ascontiguousarray(v)
              for n, v in layouts({k: np.asarray(v) for k, v in inputs.items()}).items()}
    w = {n[3:]: nc.dram_tensor(n, list(v.shape), mybir.dt.from_np(v.dtype), kind="ExternalInput").ap()
         for n, v in arrays.items()}
    out = nc.dram_tensor("out", [N, C], F32, kind="ExternalOutput").ap()
    graph_layers(nc, w, out)
    nc.compile()
    return run(nc, [arrays], core_ids=[0]).results[0]["out"]
```

```python
from contextlib import ExitStack

import numpy as np

import concourse.bass as bass
from concourse import mybir

F32 = mybir.dt.float32
I32 = mybir.dt.int32
BF16 = mybir.dt.bfloat16
ALU = mybir.AluOpType
ACT = mybir.ActivationFunctionType
AX = mybir.AxisListType

P = 128
N = 50000
E = 25000
H5 = 10000
C = 128
R = 4
H = 8
D = C // H
U = 4
CH = P * U
NC = -(-E // CH)
EP = NC * CH
NT = EP // P
NP = N // CH
RP, RC = 98, EP // 98
HI = -(-(N + 1) // P)
NOWHERE = 1 << 20
EPS = 1e-5
LEAK = 0.2
NEG = 1.0e30
MASKED = 3.0e38


class Phase:

    def __init__(self, nc, name):
        self.nc, self.name, self.stack, self.sems = nc, name, ExitStack(), []

    def __enter__(self):
        self.stack.__enter__()
        return self

    def __exit__(self, *exc):
        done = self.stack.__exit__(*exc)
        self.nc.clear_and_free_semaphores(self.sems)
        self.nc.all_engine_barrier()
        return done

    def sb(self, name, shape, dtype=F32):
        return self.stack.enter_context(self.nc.sbuf_tensor(f"{self.name}_{name}", shape, dtype))

    def ps(self, name, shape=(P, CH)):
        return self.stack.enter_context(self.nc.psum_tensor(f"{self.name}_{name}", list(shape), F32))

    def sem(self, name):
        self.sems.append(self.nc.alloc_semaphore(f"{self.name}_{name}"))
        return self.sems[-1]

    def block(self):
        return self.stack.enter_context(self.nc.Block())


def steps(eng, count, body):
    body(0, True)
    if count > 1:
        with eng.Fori(1, count) as i:
            body(i, False)


def skewed(eng, front, body):
    front(0, True)
    body(0, True, True)
    with eng.Fori(1, NC - 1) as i:
        body(i, False, True)
    body(NC - 1, False, False)


def skewed_pairs(eng, front, body, ahead=False):
    front(0, True, (0, 0))
    body(0, True, True, (1, 0))
    with eng.Fori(0, (NC - 4) // 2) as j:
        body(j * 2 + 1, False, True, (0, j + 1))
        body(j * 2 + 2, False, True, (1, j + 1))
    for i in range((NC - 4) // 2 * 2 + 1, NC):
        place = ((i + 1) % 2, (i + 1) // 2)
        if ahead:
            body(i, False, i + 1 < NC, place, i + 3 < NC)
        else:
            body(i, False, i + 1 < NC, place)


def pairs(eng, low, high, body):
    with eng.Fori(low // 2, high // 2) as j:
        body(j * 2, (0, j))
        body(j * 2 + 1, (1, j))
    for i in range(high // 2 * 2, high):
        body(i, (i % 2, i // 2))


def gate(eng, sem, value, passed):
    eng.wait_ge(sem, value)
    eng.sem_inc(passed, 1)


def chunk(flat, i):
    return flat[bass.ds(i * CH, CH)].rearrange("(p u) -> p u", u=U)


def rows(flat, i, parts=P):
    return flat[bass.ds(i * CH, CH)].rearrange("(a e) -> a e", a=1).to_broadcast([parts, CH])


def slot(wide, u):
    return wide[:, u::U]


def gather(pool, tile, table, index, u, done):
    pool.indirect_dma_start(out=tile[:, u, :], out_offset=None, in_=table,
                            in_offset=bass.IndirectOffsetOnAxis(ap=index[:, u:u + 1], axis=0)).then_inc(done, 16)


def scatter(pool, table, tile, index, u, done, last_row):
    pool.indirect_dma_start(out=table, out_offset=bass.IndirectOffsetOnAxis(ap=index[:, u:u + 1], axis=0),
                            in_=tile[:, u, :], in_offset=None, bounds_check=last_row,
                            oob_is_err=False).then_inc(done, 16)



def sort_edges(nc, records, const, by_dst, by_src, from_last):
    both = range(2)
    with Phase(nc, "sort") as ph:
        def two(name, shape, dtype=F32):
            return [ph.sb(f"{name}{k}", shape, dtype) for k in both]

        rec = ph.sb("rec", [P, NT, 4], I32)
        keyi, digit = two("keyi", [P, NT], I32), two("digit", [P, NT], I32)
        key, hi, lo = two("key", [P, NT]), two("hi", [P, NT]), two("lo", [P, NT])
        keys_of = two("keys_of", [P, CH], I32)
        iota = ph.sb("iota", [P, HI])
        tri = ph.sb("tri", [P, P])
        low = ph.sb("low", [P, CH])
        ident = ph.sb("ident", [P, P])
        ident_b = ph.sb("ident_b", [P, P], BF16)
        ones = ph.sb("ones", [P, HI])
        lob, hib = two("lob", [P, U, P], BF16), two("hib", [P, U, HI], BF16)
        loT = two("loT", [P, CH])
        same = [ph.sb(f"same{j}", [P, CH]) for j in range(U)]
        hit = [ph.sb(f"hit{j}", [P, HI]) for j in range(U)]
        rank, looked, posf = two("rank", [P, U]), two("looked", [P, U]), two("posf", [P, U])
        pos, recst = two("pos", [P, U], I32), two("recst", [P, U, 4], I32)
        pos_last = ph.sb("pos_last", [P, U], I32)
        place = two("place", [P, HI])
        total, ends = two("total", [P, HI]), two("ends", [P, HI])
        sent = ph.sb("sent", [1, 4], I32)
        ps_place = [ph.ps(f"ps_place{k}") for k in both]
        ps_look = [[ph.ps(f"ps_look{k}{q}") for q in range(2)] for k in both]
        ps_loT = [ph.stack.enter_context(nc.psum_tensor(f"sort_ps_loT{k}", [P, 2 * CH], BF16)) for k in both]
        s = {x: ph.sem(x) for x in ("loaded", "ones", "sentinel", "sent_out", "passed", "digits")}
        s |= {f"{x}{k}": ph.sem(f"{x}{k}") for k in both for x in (
            "hot", "counted", "table", "before", "ends", "first_place", "hot2", "loT_ps", "loT", "rank", "look",
            "looked", "own_counts", "place", "posf", "pos", "scattered", "keys_of")}
        block = ph.block()

        @block.sync
        def _(sp):
            sp.dma_start(rec[:], records.rearrange("(t p) f -> p t f", p=P)).then_inc(s["loaded"], 16)
            sp.dma_start(iota[:], const["iota"][:, 0:HI]).then_inc(s["loaded"], 16)
            sp.dma_start(tri[:], const["tri"]).then_inc(s["loaded"], 16)
            sp.dma_start(low[:, CH - P:CH], const["tri_low"]).then_inc(s["loaded"], 16)
            sp.dma_start(ident[:], const["ident"]).then_inc(s["loaded"], 16)
            sp.wait_ge(s["sentinel"], 1)
            for ordered in (by_dst, by_src, from_last):
                sp.dma_start(ordered[0:1, :], sent[:]).then_inc(s["sent_out"], 16)
                sp.dma_start(ordered[EP + 1:EP + 2, :], sent[:]).then_inc(s["sent_out"], 16)
            sp.wait_ge(s["sent_out"], 96)

            def position(g, first):
                for k in both:
                    if not first:
                        sp.wait_ge(s[f"rank{k}"], g)
                    sp.dma_start(keys_of[k][:], rows(const["dst_src"][k], g)).then_inc(s[f"keys_of{k}"], 16)
            steps(sp, NC, position)

        @block.vector
        def _(dve):
            dve.memset(sent[:], -1).then_inc(s["sentinel"], 1)
            dve.memset(low[:, 0:CH - P], 1.0)
            dve.memset(ones[:], 1.0).then_inc(s["ones"], 1)
            dve.wait_ge(s["loaded"], 16 * 5)
            dve.tensor_copy(ident_b[:], ident[:]).then_inc(s["ones"], 1)
            dve.wait_ge(s["ones"], 2)
            for k in both:
                dve.tensor_copy(keyi[k][:], rec[:, :, k]).then_inc(s["digits"], 1)
                dve.wait_ge(s["digits"], 5 * k + 1)
                dve.tensor_copy(key[k][:], keyi[k][:])
                dve.tensor_scalar(digit[k][:], keyi[k][:], 7, None, ALU.arith_shift_right).then_inc(s["digits"], 1)
                dve.wait_ge(s["digits"], 5 * k + 2)
                dve.tensor_copy(hi[k][:], digit[k][:]).then_inc(s["digits"], 1)
                dve.wait_ge(s["digits"], 5 * k + 3)
                dve.tensor_scalar(digit[k][:], keyi[k][:], 127, None, ALU.bitwise_and).then_inc(s["digits"], 1)
                dve.wait_ge(s["digits"], 5 * k + 4)
                dve.tensor_copy(lo[k][:], digit[k][:]).then_inc(s["digits"], 1)
                dve.wait_ge(s["digits"], 5 * k + 5)

            def one_hot(g, k, made):
                for j in range(U):
                    at = bass.ds(g * U + j, 1)
                    dve.tensor_scalar(lob[k][:, j, :], iota[:, 0:P], lo[k][:, at], None, ALU.is_equal)
                    ins = dve.tensor_scalar(hib[k][:, j, :], iota[:], hi[k][:, at], None, ALU.is_equal)
                ins.then_inc(made, 1)

            def count(g, first):
                for k in both:
                    if not first:
                        dve.wait_ge(s[f"counted{k}"], g)
                    one_hot(g, k, s[f"hot{k}"])
            steps(dve, NC, count)

            for k in both:
                dve.wait_ge(s[f"counted{k}"], NC)
                dve.tensor_copy(place[k][:], ps_place[k][:, 0:HI]).then_inc(s[f"table{k}"], 1)
            for k in both:
                dve.wait_ge(s[f"before{k}"], 1)
                dve.tensor_copy(total[k][:], ps_look[k][1][:, 0:HI]).then_inc(s[f"ends{k}"], 1)
                dve.wait_ge(s[f"ends{k}"], 1)
                dve.tensor_tensor_scan(ends[k][:], ones[:], total[k][:], 0.0, ALU.mult, ALU.add).then_inc(s[f"ends{k}"], 1)
                dve.wait_ge(s[f"ends{k}"], 2)
                dve.tensor_tensor(ends[k][:], ends[k][:], total[k][:], ALU.subtract).then_inc(s[f"ends{k}"], 1)
                dve.wait_ge(s[f"ends{k}"], 3)
                dve.tensor_tensor(place[k][:], ends[k][:], ps_look[k][0][:, 0:HI], ALU.add).then_inc(s[f"first_place{k}"], 1)

            def position(g, first):
                for k in both:
                    if not first:
                        dve.wait_ge(s[f"own_counts{k}"], g)
                    one_hot(g, k, s[f"hot2{k}"])
                for k in both:
                    dve.wait_ge(s[f"keys_of{k}"], 16 * (g + 1))
                    if not first:
                        dve.wait_ge(s[f"posf{k}"], g)
                    for j in range(U):
                        n = P * (j + 1)
                        if k:
                            dve.wait_ge(s["rank0"], g + 1)
                        elif not first:
                            dve.wait_ge(s["rank1"], g)
                        ins = dve.scalar_tensor_tensor(out=same[j][:, 0:n], in0=keys_of[k][:, 0:n],
                                                       scalar=key[k][:, bass.ds(g * U + j, 1)], in1=low[:, CH - n:CH],
                                                       op0=ALU.is_equal, op1=ALU.mult, accum_out=rank[k][:, j:j + 1])
                        if j == U - 1:
                            ins.then_inc(s[f"rank{k}"], 1)
                        dve.wait_ge(s[f"look{k}"], g * U + j + 1)
                        if k:
                            dve.wait_ge(s["looked0"], (g + 1) * U)
                        elif not first:
                            dve.wait_ge(s["looked1"], g * U)
                        dve.tensor_tensor_reduce(hit[j][:], ps_look[k][j % 2][:, 0:HI], hib[k][:, j, :], 1.0, 0.0,
                                                 ALU.mult, ALU.add, looked[k][:, j:j + 1]).then_inc(s[f"looked{k}"], 1)
                    dve.wait_ge(s[f"looked{k}"], (g + 1) * U)
                    dve.wait_ge(s[f"rank{k}"], g + 1)
                    if not first:
                        dve.wait_ge(s[f"scattered{k}"], 16 * U * (2 - k) * g)
                    dve.scalar_tensor_tensor(out=posf[k][:], in0=looked[k][:], scalar=1.0, in1=rank[k][:],
                                             op0=ALU.add, op1=ALU.add).then_inc(s[f"posf{k}"], 1)
                    dve.tensor_copy(recst[k][:], rec[:, bass.ds(g * U, U), :])
                    dve.wait_ge(s[f"posf{k}"], g + 1)
                    if k == 0:
                        dve.tensor_scalar(pos_last[:], posf[k][:], -1.0, float(EP + 1), ALU.mult, ALU.add)
                    dve.tensor_copy(pos[k][:], posf[k][:]).then_inc(s[f"pos{k}"], 1)
            steps(dve, NC, position)

        @block.tensor
        def _(pe):
            pe.wait_ge(s["loaded"], 16 * 5)

            def add_counts(k, start, stop, done):
                for j in range(U):
                    ins = pe.matmul(ps_place[k][:, 0:HI], lob[k][:, j, :], hib[k][:, j, :], start=start and j == 0,
                                    stop=stop, skip_group_check=True)
                ins.then_inc(done, 1)

            def count(g, first):
                for k in both:
                    pe.wait_ge(s[f"hot{k}"], g + 1)
                    add_counts(k, first, False, s[f"counted{k}"])
            steps(pe, NC, count)
            for k in both:
                pe.wait_ge(s[f"table{k}"], 1)
                pe.matmul(ps_look[k][0][:, 0:HI], tri[:], place[k][:], start=True, stop=True)
                pe.matmul(ps_look[k][1][:, 0:HI], ones[:, 0:P], place[k][:], start=True, stop=True).then_inc(s[f"before{k}"], 1)
            for k in both:
                pe.wait_ge(s[f"first_place{k}"], 1)
                pe.matmul(ps_place[k][:, 0:HI], ident[:], place[k][:], start=True, stop=False, skip_group_check=True)

            def position(g, first):
                def turn_and_count(k):
                    pe.wait_ge(s[f"hot2{k}"], g + 1)
                    if not first:
                        pe.wait_ge(s[f"loT{k}"], g)
                    for j in range(U):
                        ins = pe.transpose(ps_loT[k][:, j * P:(j + 1) * P], lob[k][:, j, :], ident_b[:])
                    ins.then_inc(s[f"loT_ps{k}"], 1)
                    if not first:
                        pe.wait_ge(s[f"place{k}"], g)
                    add_counts(k, False, False, s[f"own_counts{k}"])

                def look(k, tiles):
                    pe.wait_ge(s[f"loT{k}"], g + 1)
                    for j in tiles:
                        if j >= 2 or not first:
                            pe.wait_ge(s[f"looked{k}"], g * U + j - 1)
                        pe.matmul(ps_look[k][j % 2][:, 0:HI], loT[k][:, j * P:(j + 1) * P], place[k][:],
                                  start=True, stop=True).then_inc(s[f"look{k}"], 1)

                turn_and_count(0)
                look(0, (0, 1))
                turn_and_count(1)
                look(0, (2, 3))
                look(1, range(U))
            steps(pe, NC, position)

        @block.scalar
        def _(act):
            def position(g, first):
                for k in both:
                    act.wait_ge(s[f"loT_ps{k}"], g + 1)
                    if not first:
                        act.wait_ge(s[f"look{k}"], g * U)
                    act.copy(loT[k][:], ps_loT[k][:, 0:CH]).then_inc(s[f"loT{k}"], 1)
                for k in both:
                    act.wait_ge(s[f"own_counts{k}"], g + 1)
                    act.wait_ge(s[f"look{k}"], (g + 1) * U)
                    act.copy(place[k][:], ps_place[k][:, 0:HI]).then_inc(s[f"place{k}"], 1)
            steps(act, NC, position)

        @block.gpsimd
        def _(pool):
            def position(g, first):
                for k, targets in enumerate((((by_dst, pos[0]), (from_last, pos_last)), ((by_src, pos[1]),))):
                    gate(pool, s[f"pos{k}"], g + 1, s["passed"])
                    for ordered, at in targets:
                        for j in range(U):
                            pool.indirect_dma_start(
                                out=ordered, out_offset=bass.IndirectOffsetOnAxis(ap=at[:, j:j + 1], axis=0),
                                in_=recst[k][:, j, :], in_offset=None).then_inc(s[f"scattered{k}"], 16)
            steps(pool, NC, position)
            for k in both:
                pool.wait_ge(s[f"scattered{k}"], 16 * NT * (2 - k))



def derive_orders(nc, tables, flat):
    with Phase(nc, "orders") as ph:
        s = {x: ph.sem(x) for x in ("loaded", "step", "ready", "stored")}
        f, goes_on = {}, {}
        cur, prev, nxt = ({o: ph.sb(f"{name}_{o}", [RP, RC, 4], I32) for o in "drs"} for name in ("cur", "prev", "next"))
        names = ["src_d", "dst_d", "put_d", "src_r", "put_r", "src_s", "dst_s", "put_s"]
        for n in names:
            f[n] = ph.sb(n, [RP, RC], I32)
        fl = ["run_d", "run_r", "run_s", "last_s", "rel_d", "kind0_d", "kind1_d", "kind0_r", "kind1_r", "reset_d"]
        for n in fl:
            f[n] = ph.sb(n, [RP, RC])
        for o in "drs":
            goes_on[o] = ph.sb(f"goes_on_{o}", [RP, RC])
        real = ph.sb("real", [RP, RC])
        block = ph.block()

        @block.sync
        def _(sp):
            for o, rec in tables.items():
                for where, at in ((prev, 0), (cur, 1), (nxt, 2)):
                    sp.dma_start(where[o][:], rec[at:at + EP, :].rearrange("(p k) f -> p k f", p=RP)
                                 ).then_inc(s["loaded"], 16)
            sp.wait_ge(s["ready"], 1)
            for n in names + fl:
                sp.dma_start(flat[n].rearrange("(p k) -> p k", p=RP), f[n][:]).then_inc(s["stored"], 16)
            sp.wait_ge(s["stored"], 16 * len(names + fl))

        @block.vector
        def _(dve):
            dve.wait_ge(s["loaded"], 16 * 9)
            for o in "drs":
                k = 1 if o == "s" else 0
                key = cur[o][:, :, k]
                dve.tensor_tensor(f[f"run_{o}"][:], key, prev[o][:, :, k], ALU.is_equal)
                dve.tensor_tensor(goes_on[o][:], key, nxt[o][:, :, k], ALU.is_equal)
                dve.tensor_scalar(f[f"src_{o}"][:], cur[o][:, :, 1], float(N - 1), None, ALU.min)
                if o != "r":
                    dve.tensor_scalar(f[f"dst_{o}"][:], cur[o][:, :, 0], float(N - 1 if o == "d" else H5 - 1), None, ALU.min)
                if o != "s":
                    dve.tensor_scalar(f[f"kind0_{o}"][:], cur[o][:, :, 3], 0.0, None, ALU.is_equal)
                    dve.tensor_scalar(f[f"kind1_{o}"][:], cur[o][:, :, 3], 1.0, None, ALU.is_equal)
            dve.tensor_scalar(real[:], cur["s"][:, :, 1], float(N), None, ALU.is_lt)
            dve.tensor_copy(f["rel_d"][:], cur["d"][:, :, 2]).then_inc(s["step"], 1)
            dve.wait_ge(s["step"], 1)
            dve.tensor_scalar(f["reset_d"][:], f["run_d"][:], -1.0, MASKED, ALU.add, ALU.mult)
            for o in "drs":
                dve.scalar_tensor_tensor(out=f[f"put_{o}"][:], in0=goes_on[o][:], scalar=float(NOWHERE),
                                         in1=cur[o][:, :, 1 if o == "s" else 0], op0=ALU.mult, op1=ALU.add)
            dve.tensor_tensor(f["last_s"][:], real[:], goes_on["s"][:], ALU.is_gt).then_inc(s["ready"], 1)


def count_runs(nc, flat, sums):
    SC = EP // 7
    with Phase(nc, "runs") as ph:
        s = {x: ph.sem(x) for x in ("ones", "loaded0", "loaded1", "summed", "stored", "back", "step", "ready", "out")}
        run = [ph.sb(f"run{j}", [6, SC]) for j in range(2)]
        val = [ph.sb(f"val{j}", [6, SC]) for j in range(2)]
        out = [ph.sb(f"out{j}", [6, SC]) for j in range(2)]
        b = {n: ph.sb(n, [RP, RC]) for n in ("inv0", "inv1", "inv_deg", "weight", "back0", "back1", "pos", "safe",
                                             "inv", "inv_w", "gap", "t0", "t1", "t2", "t3", "t4")}
        ones_row = ph.sb("ones_row", [P, EP // P])
        block = ph.block()
        vals = ["kind0_d", "kind1_d", "ones", "weight_s", "kind0_r", "kind1_r"]
        facs = ["inv0_d", "inv1_d", "inv_deg_d", "inv_w_s", "inv0_r", "inv1_r"]

        @block.sync
        def _(sp):
            sp.wait_ge(s["ones"], 1)
            sp.dma_start(flat["ones"].rearrange("(p k) -> p k", p=P), ones_row[:]).then_inc(s["out"], 16)
            sp.wait_ge(s["out"], 16)

            def load(j):
                if j >= 2:
                    sp.wait_ge(s["summed"], j - 1)
                at, done = slice(j * SC, (j + 1) * SC), s[f"loaded{j % 2}"]
                for q in range(6):
                    order = "run_s" if q == 3 else "run_r" if q > 3 else "run_d"
                    sp.dma_start(run[j % 2][q:q + 1, :], flat[order][at].rearrange("(a e) -> a e", a=1)).then_inc(done, 16)
                    sp.dma_start(val[j % 2][q:q + 1, :], flat[vals[q]][at].rearrange("(a e) -> a e", a=1)).then_inc(done, 16)

            load(0)
            for j in range(7):
                if j + 1 < 7:
                    load(j + 1)
                sp.wait_ge(s["summed"], j + 1)
                if j:
                    sp.wait_ge(s["stored"], 16 * j)
                sp.dma_start(sums[:, j * SC:(j + 1) * SC], out[j % 2][:]).then_inc(s["stored"], 16)
            sp.wait_ge(s["stored"], 16 * 7)
            for q, n in enumerate(("inv0", "inv1", "inv_deg", "weight", "back0", "back1")):
                sp.dma_start(b[n][:], sums[q].rearrange("(p k) -> p k", p=RP)).then_inc(s["back"], 16)
            sp.wait_ge(s["ready"], 1)
            for n, q in zip(facs, ("t0", "t1", "t2", "inv_w", "t3", "t4")):
                sp.dma_start(flat[n].rearrange("(p k) -> p k", p=RP), b[q][:]).then_inc(s["out"], 16)
            sp.wait_ge(s["out"], 16 * 7)

        @block.vector
        def _(dve):
            dve.memset(ones_row[:], 1.0).then_inc(s["ones"], 1)
            for j in range(7):
                dve.wait_ge(s[f"loaded{j % 2}"], 192 * (j // 2 + 1))
                if j >= 2:
                    dve.wait_ge(s["stored"], 16 * (j - 1))
                if j >= 1:
                    dve.wait_ge(s["summed"], j)
                dve.tensor_tensor_scan(out[j % 2][:], run[j % 2][:], val[j % 2][:],
                                       0.0 if j == 0 else out[1 - j % 2][:, SC - 1:SC], ALU.mult, ALU.add
                                       ).then_inc(s["summed"], 1)
            dve.wait_ge(s["back"], 96)
            for n in ("inv0", "inv1", "inv_deg", "back0", "back1"):
                dve.tensor_scalar(b[n][:], b[n][:], 1.0, None, ALU.max)
            dve.tensor_scalar(b["pos"][:], b["weight"][:], 0.0, None, ALU.is_gt).then_inc(s["step"], 1)
            dve.wait_ge(s["step"], 1)
            dve.tensor_scalar(b["gap"][:], b["pos"][:], -1.0, 1.0, ALU.mult, ALU.add)
            dve.tensor_tensor(b["safe"][:], b["weight"][:], b["pos"][:], ALU.mult).then_inc(s["step"], 1)
            dve.wait_ge(s["step"], 2)
            dve.tensor_tensor(b["inv"][:], b["safe"][:], b["gap"][:], ALU.add).then_inc(s["step"], 1)
            dve.wait_ge(s["step"], 3)
            for n, q in (("inv0", "t0"), ("inv1", "t1"), ("inv_deg", "t2"), ("back0", "t3"), ("back1", "t4")):
                dve.reciprocal(b[q][:], b[n][:])
            dve.reciprocal(b["safe"][:], b["inv"][:]).then_inc(s["step"], 1)
            dve.wait_ge(s["step"], 4)
            dve.tensor_tensor(b["inv_w"][:], b["safe"][:], b["pos"][:], ALU.mult).then_inc(s["ready"], 1)



class Norm:

    def __init__(self, ph, name, eps, tiles=1):
        self.stats = ph.sb(f"{name}_stats", [P, tiles * U, 6])
        self.mv = ph.sb(f"{name}_mv", [P, tiles * U, 2])
        self.root = ph.sb(f"{name}_root", [P, tiles * U])
        self.rstd = ph.sb(f"{name}_rstd", [P, tiles * U])
        self.eps = eps
        self.s_stats, self.s_mv, self.s_root, self.s_rstd, self.s_passed = (
            ph.sem(f"{name}_{x}") for x in ("stats", "mv", "root", "rstd", "passed"))

    def statistics(self, dve, srcs, i):
        for k, src in enumerate(srcs):
            for u in range(U):
                ins = dve.bn_stats(self.stats[:, k * U + u, :], src[:, u, :])
        ins.then_inc(self.s_stats, 1)
        gate(dve, self.s_stats, i + 1, self.s_passed)
        for u in range(U * len(srcs)):
            ins = dve.bn_aggr(self.mv[:, u, :], self.stats[:, u, :])
        ins.then_inc(self.s_mv, 1)

    def rootof(self, act, i, tiles=1):
        n = tiles * U
        act.wait_ge(self.s_mv, i + 1)
        act.activation(self.root[:, 0:n], self.mv[:, 0:n, 1], ACT.Sqrt, bias=self.eps[:, 0:1]).then_inc(self.s_root, 1)

    def inverse(self, dve, i, tiles=1):
        n = tiles * U
        dve.wait_ge(self.s_root, i + 1)
        dve.reciprocal(self.rstd[:, 0:n], self.root[:, 0:n]).then_inc(self.s_rstd, 1)
        dve.wait_ge(self.s_rstd, i + 1)

    def normalize(self, dve, out, src, done, k=0):
        for u in range(U):
            at = k * U + u
            ins = dve.tensor_scalar(out[:, u, :], src[:, u, :], self.mv[:, at, 0:1], self.rstd[:, at:at + 1],
                                    ALU.subtract, ALU.mult)
        ins.then_inc(done, 1)



def dense_pass(nc, w, tab):
    W = 4
    GROUPS = NP + 1
    BLOCKS, REST = divmod(GROUPS, W)
    with Phase(nc, "dense") as ph:
        ident = ph.sb("ident", [P, P])
        wself = ph.sb("wself", [P, C])
        wplus = ph.sb("wplus", [P, C])
        bias = ph.sb("bias", [P, U, C])
        b2 = ph.sb("b2", [P, U, C])
        eps = ph.sb("eps", [P, 1])
        w1 = [ph.sb(f"w1_{l}", [P, 64]) for l in range(3)]
        w2 = [ph.sb(f"w2_{l}", [65, C]) for l in range(3)]
        b1 = ph.sb("b1", [64, 3])
        b2c = ph.sb("b2c", [P, 3])

        def tiles(name, shape):
            return [ph.sb(f"{name}_{k}", shape) for k in range(W)]
        x, u, x1, x2, u3, x3, u4, x4 = (tiles(n, [P, U, C]) for n in ("x", "u", "x1", "x2", "u3", "x3", "u4", "x4"))
        hn = [tiles(f"hn{l}", [P, U, C]) for l in range(2)]
        xT = tiles("xT", [P, CH])
        hT = [tiles(f"hT{l}", [P, CH]) for l in range(3)]
        hid = tiles("hid", [65, CH])
        v1, root1, rstd1, sq = (ph.sb(n, [P, W * U]) for n in ("v1", "root1", "rstd1", "sq"))
        norm0, norm3, norm4 = (Norm(ph, n, eps, W) for n in ("norm0", "norm3", "norm4"))
        ps_a = [ph.ps(f"ps_a{k}") for k in range(W)]
        ps_b = [ph.ps(f"ps_b{k}") for k in range(W)]
        s = {n: ph.sem(n) for n in (
            "weights", "ready", "xT_ps", "xT", "s_ps", "u", "x1", "sq", "v1", "root1", "rstd1", "x2", "x2T_ps",
            "hT0", "hid_ps0", "hid_ps1", "hid_ps2", "hid0", "hid1", "hid2", "h_ps0", "h_ps1", "h_ps2", "hT1", "hT2",
            "n_ps0", "n_ps1", "hn0", "hn1", "u3", "x3", "u4", "x4", "passed")}
        s_x = [ph.sem(f"x_in{k}") for k in range(W)]
        s_stored = [ph.sem(f"stored{k}") for k in range(W)]
        block = ph.block()
        STORES = 6

        def at(table, g):
            lo = g * CH if not isinstance(g, int) or g < NP else N - CH
            return table[bass.ds(lo, CH), :].rearrange("(p u) c -> p u c", u=U)

        def blocks_of(eng, body):
            body(0, W, True)
            with eng.Fori(1, BLOCKS) as i:
                body(i, W, False)
            if REST:
                body(BLOCKS, REST, False)

        def each(i, width, step):
            for k in range(width):
                step(i * W + k, k)

        def wide(t):
            return t[:].rearrange("p (u c) -> p u c", u=U)

        loads = [(ident[:], w["ident"]), (wself[:], w["W_self"]), (b1[:], w["nb1"]), (b2c[:], w["nb2"]),
                 (bias[:], w["bias_lang"].rearrange("(a b c) -> a b c", a=1, b=1).to_broadcast([P, U, C])),
                 (b2[:], w["b2"].rearrange("(a b c) -> a b c", a=1, b=1).to_broadcast([P, U, C]))]
        for l in range(3):
            loads += [(w1[l][:], w["nW1"][l, 64:192, :]), (w2[l][0:64, :], w["nW2"][l]),
                      (w2[l][64:65, :], w["nb2_rows"][l:l + 1, :])]
        NW = 16 * len(loads)

        @block.sync
        def _(sp):
            for dst, src in loads:
                sp.dma_start(dst, src).then_inc(s["weights"], 16)

            def body(i, width, first):
                def load(g, k):
                    if not first:
                        sp.wait_ge(s["xT_ps"], g - W + 1)
                    sp.dma_start(x[k][:], at(w["x"], g)).then_inc(s_x[k], 16)
                each(i, width, load)
            blocks_of(sp, body)

        @block.gpsimd
        def _(pool):
            def body(i, width, first):
                def store(name, src, made):
                    def one(g, k):
                        if isinstance(g, int) and g == GROUPS - 1:
                            pool.wait_ge(s_stored[(g - 1) % W], 16 * (STORES * i + order.index(name) + 1))
                        gate(pool, s[made], g + 1, s["passed"])
                        pool.dma_start(at(tab[name], g), src[k][:]).then_inc(s_stored[k], 16)
                    each(i, width, one)
                order = ["x1", "x2", "h1", "h2", "x3", "out"]
                for name, src, made in (("x1", x1, "x1"), ("x2", x2, "x2"), ("h1", hn[0], "hn0"),
                                        ("h2", hn[1], "hn1"), ("x3", x3, "x3"), ("out", x4, "x4")):
                    store(name, src, made)
            blocks_of(pool, body)
            for k in range(W):
                pool.wait_ge(s_stored[k], 16 * STORES * (BLOCKS + (k < REST)))

        @block.tensor
        def _(pe):
            pe.wait_ge(s["weights"], NW)
            pe.wait_ge(s["ready"], 1)

            def body(i, width, first):
                def turn_x(g, k):
                    pe.wait_ge(s_x[k], 16 * (i + 1))
                    if not first:
                        pe.wait_ge(s["u3"], g - W + 1)
                    for j in range(U):
                        ins = pe.transpose(slot(ps_a[k], j), x[k][:, j, :], ident[:])
                    ins.then_inc(s["xT_ps"], 1)

                def self_map(g, k):
                    pe.wait_ge(s["xT"], g + 1)
                    for j in range(U):
                        ins = pe.matmul(ps_b[k][:, j * C:(j + 1) * C], slot(xT[k], j), wplus[:], start=True, stop=True)
                    ins.then_inc(s["s_ps"], 1)

                def turn_x2(g, k):
                    pe.wait_ge(s["x2"], g + 1)
                    for j in range(U):
                        ins = pe.transpose(slot(ps_a[k], j), x2[k][:, j, :], ident[:])
                    ins.then_inc(s["x2T_ps"], 1)

                def hidden(l):
                    def one(g, k):
                        pe.wait_ge(s[f"hT{l}"], g + 1)
                        ps = ps_b[k] if l != 1 else ps_a[k]
                        if l == 2:
                            pe.wait_ge(s["hT2"], g + 1)
                        pe.matmul(ps[0:64, :], w1[l][:], hT[l][k][:], start=True, stop=True).then_inc(s[f"hid_ps{l}"], 1)
                    return one

                def up(l):
                    def one(g, k):
                        pe.wait_ge(s[f"hid{l}"], g + 1)
                        if l == 1:
                            pe.wait_ge(s["hn0"], g + 1)
                        ps = ps_a[k] if l == 0 else ps_b[k]
                        pe.matmul(ps[:], w2[l][0:64, :], hid[k][0:64, :], start=True, stop=True).then_inc(s[f"h_ps{l}"], 1)
                    return one

                def turn_h(l):
                    def one(g, k):
                        pe.wait_ge(s[f"hT{l + 1}"], g + 1)
                        ps = ps_b[k] if l == 0 else ps_a[k]
                        for j in range(U):
                            ins = pe.transpose(ps[:, j * C:(j + 1) * C], slot(hT[l + 1][k], j), ident[:])
                        ins.then_inc(s[f"n_ps{l}"], 1)
                        hidden(l + 1)(g, k)
                    return one

                def out_rows(g, k):
                    pe.wait_ge(s["hid2"], g + 1)
                    pe.wait_ge(s["hn1"], g + 1)
                    for j in range(U):
                        ins = pe.matmul(ps_a[k][:, j * C:(j + 1) * C], slot(hid[k], j), w2[2][:], start=True, stop=True)
                    ins.then_inc(s["h_ps2"], 1)

                for step in (turn_x, self_map, turn_x2, hidden(0), up(0), turn_h(0), up(1), turn_h(1), out_rows):
                    each(i, width, step)
            blocks_of(pe, body)

        @block.scalar
        def _(act):
            def body(i, width, first):
                def copy_x(g, k):
                    act.wait_ge(s["xT_ps"], g + 1)
                    if not first:
                        act.wait_ge(s["s_ps"], g - W + 1)
                    act.copy(xT[k][:], ps_a[k][:]).then_inc(s["xT"], 1)

                def scale_x2(g, k):
                    act.wait_ge(s["x1"], g + 1)
                    if not first:
                        act.wait_ge(s_stored[k], 16 * STORES * i)
                    for j in range(U):
                        ins = act.activation(x2[k][:, j, :], x1[k][:, j, :], ACT.Identity,
                                             scale=rstd1[:, k * U + j:k * U + j + 1])
                    ins.then_inc(s["x2"], 1)

                def copy_x2(g, k):
                    act.wait_ge(s["x2T_ps"], g + 1)
                    act.copy(hT[0][k][:], ps_a[k][:]).then_inc(s["hT0"], 1)

                def relu(l):
                    def one(g, k):
                        act.wait_ge(s[f"hid_ps{l}"], g + 1)
                        ps = ps_b[k] if l != 1 else ps_a[k]
                        if l:
                            act.wait_ge(s[f"h_ps{l - 1}"], g + 1)
                        elif not first:
                            act.wait_ge(s["h_ps2"], g - W + 1)
                        act.activation(hid[k][0:64, :], ps[0:64, :], ACT.Relu, bias=b1[:, l:l + 1]).then_inc(s[f"hid{l}"], 1)
                    return one

                def rows_out(l):
                    def one(g, k):
                        act.wait_ge(s[f"n_ps{l}"], g + 1)
                        ps = ps_b[k] if l == 0 else ps_a[k]
                        act.copy(hn[l][k][:], wide(ps)).then_inc(s[f"hn{l}"], 1)
                        relu(l + 1)(g, k)
                    return one

                each(i, width, copy_x)
                norm0.rootof(act, i, width)
                n = width * U
                act.wait_ge(s["v1"], i + 1)
                act.activation(root1[:, 0:n], v1[:, 0:n], ACT.Sqrt, bias=eps[:, 0:1]).then_inc(s["root1"], 1)
                act.wait_ge(s["rstd1"], i + 1)
                each(i, width, scale_x2)
                each(i, width, copy_x2)
                each(i, width, relu(0))
                each(i, width, rows_out(0))
                each(i, width, rows_out(1))
                norm3.rootof(act, i, width)
                norm4.rootof(act, i, width)
            blocks_of(act, body)

        @block.vector
        def _(dve):
            dve.memset(eps[:], EPS)
            for k in range(W):
                dve.memset(hid[k][64:65, :], 1.0)
            dve.wait_ge(s["weights"], NW)
            dve.tensor_tensor(wplus[:], wself[:], ident[:], ALU.add).then_inc(s["ready"], 1)

            def body(i, width, first):
                n = width * U

                def add_bias(g, k):
                    dve.wait_ge(s["s_ps"], g + 1)
                    dve.tensor_tensor(u[k][:], wide(ps_b[k]), bias[:], ALU.add).then_inc(s["u"], 1)

                def bias_h(l):
                    def one(g, k):
                        dve.wait_ge(s[f"h_ps{l}"], g + 1)
                        ps = ps_a[k] if l == 0 else ps_b[k]
                        dve.tensor_scalar(hT[l + 1][k][:], ps[:], b2c[:, l:l + 1], None, ALU.add).then_inc(s[f"hT{l + 1}"], 1)
                    return one

                def residual(g, k):
                    dve.wait_ge(s["h_ps2"], g + 1)
                    dve.tensor_tensor(u3[k][:], wide(ps_a[k]), x2[k][:], ALU.add).then_inc(s["u3"], 1)

                def add_b2(g, k):
                    dve.wait_ge(s["x3"], g + 1)
                    dve.tensor_tensor(u4[k][:], x3[k][:], b2[:], ALU.add).then_inc(s["u4"], 1)

                each(i, width, add_bias)
                dve.wait_ge(s["u"], i * W + width)
                norm0.statistics(dve, u[:width], i)
                norm0.inverse(dve, i, width)
                dve.tensor_tensor(sq[:, 0:n], norm0.rstd[:, 0:n], norm0.rstd[:, 0:n], ALU.mult).then_inc(s["sq"], 1)
                dve.wait_ge(s["sq"], i + 1)
                dve.tensor_tensor(v1[:, 0:n], sq[:, 0:n], norm0.mv[:, 0:n, 1], ALU.mult).then_inc(s["v1"], 1)
                for k in range(width):
                    if not first:
                        dve.wait_ge(s_stored[k], 16 * STORES * i)
                    norm0.normalize(dve, x1[k], u[k], s["x1"], k)
                dve.wait_ge(s["root1"], i + 1)
                dve.reciprocal(rstd1[:, 0:n], root1[:, 0:n]).then_inc(s["rstd1"], 1)
                each(i, width, bias_h(0))
                each(i, width, bias_h(1))
                each(i, width, residual)
                dve.wait_ge(s["u3"], i * W + width)
                norm3.statistics(dve, u3[:width], i)
                norm3.inverse(dve, i, width)
                for k in range(width):
                    norm3.normalize(dve, x3[k], u3[k], s["x3"], k)
                each(i, width, add_b2)
                dve.wait_ge(s["u4"], i * W + width)
                norm4.statistics(dve, u4[:width], i)
                norm4.inverse(dve, i, width)
                for k in range(width):
                    norm4.normalize(dve, x4[k], u4[k], s["x4"], k)
            blocks_of(dve, body)



class Stream:

    def __init__(self, ph, name, table, index, ps, after=None):
        self.table, self.flat, self.ps = table, index, ps
        self.index = ph.sb(f"{name}_index", [P, U], I32)
        self.tile = ph.sb(f"{name}_tile", [P, U, C])
        self.s_index, self.s_rows, self.s_turned, self.s_T = (
            ph.sem(f"{name}_{x}") for x in ("index", "rows", "turned", "T"))
        self.T = ph.sb(f"{name}_T", [P, CH])

    def load_index(self, sp, i, first):
        if not first:
            sp.wait_ge(self.s_turned, i)
        sp.dma_start(self.index[:], chunk(self.flat, i)).then_inc(self.s_index, 16)

    def fetch(self, pool, i, first, s_passed):
        if not first:
            gate(pool, self.s_turned, i, s_passed)
        gate(pool, self.s_index, 16 * (i + 1), s_passed)
        for u in range(U):
            gather(pool, self.tile, self.table, self.index, u, self.s_rows)

    def turn(self, pe, i, first, ident, busy=None):
        pe.wait_ge(self.s_rows, 16 * U * (i + 1))
        if busy is not None:
            pe.wait_ge(*busy)
        for u in range(U):
            ins = pe.transpose(slot(self.ps, u), self.tile[:, u, :], ident[:])
        ins.then_inc(self.s_turned, 1)

    def copy_out(self, act, i, first, free=None):
        act.wait_ge(self.s_turned, i + 1)
        if free is not None:
            act.wait_ge(*free)
        act.copy(self.T[:], self.ps[:]).then_inc(self.s_T, 1)


class Put:

    def __init__(self, ph, name, table, index, last_row, by_edge=None):
        self.table, self.flat, self.last_row, self.by_edge = table, index, last_row, by_edge
        if by_edge is not None:
            self.s_kept, self.s_passed = ph.sem(f"{name}_kept"), ph.sem(f"{name}_passed")
        self.index = ph.sb(f"{name}_index", [P, U], I32)
        self.tile = ph.sb(f"{name}_tile", [P, U, C])
        self.s_index, self.s_made, self.s_put = (ph.sem(f"{name}_{x}") for x in ("index", "made", "put"))

    def load_index(self, sp, i, first):
        if not first:
            sp.wait_ge(self.s_put, 16 * U * i)
        sp.dma_start(self.index[:], chunk(self.flat, i)).then_inc(self.s_index, 16)

    def keep(self, sp, i):
        if self.by_edge is not None:
            gate(sp, self.s_made, i + 1, self.s_passed)
            sp.dma_start(self.by_edge[bass.ds(i * CH, CH), :].rearrange("(p u) c -> p u c", u=U), self.tile[:]
                         ).then_inc(self.s_kept, 16)

    def put(self, pool, i, s_passed):
        gate(pool, self.s_made, i + 1, s_passed)
        gate(pool, self.s_index, 16 * (i + 1), s_passed)
        for u in range(U):
            scatter(pool, self.table, self.tile, self.index, u, self.s_put, self.last_row)

    def free(self, eng, i, first):
        if not first:
            eng.wait_ge(self.s_put, 16 * U * i)
            if self.by_edge is not None:
                eng.wait_ge(self.s_kept, 16 * i)


class Held:

    def __init__(self, ph, name, by_edge, ps, run):
        self.by_edge, self.ps, self.flat_run = by_edge, ps, run
        self.run = ph.sb(f"{name}_run", [P, CH])
        self.tile = ph.sb(f"{name}_tile", [P, U, C])
        self.fresh = ph.sb(f"{name}_fresh", [P, CH])
        self.carry = ph.sb(f"{name}_carry", [P, 1])
        self.T = ph.sb(f"{name}_T", [P, CH])
        self.s_rows, self.s_turned, self.s_fresh, self.s_T, self.s_carry, self.s_passed, self.s_run = (
            ph.sem(f"{name}_{x}") for x in ("rows", "turned", "fresh", "T", "carry", "passed", "run"))

    def load_rows(self, sp, i, first):
        if not first:
            gate(sp, self.s_turned, i, self.s_passed)
        at = bass.ds((NC - 1) * CH - i * CH, CH)
        sp.dma_start(self.tile[:], self.by_edge[at, :].rearrange("(p u) c -> p u c", u=U)).then_inc(self.s_rows, 16)

    def load_run(self, sp, i, first):
        if not first:
            gate(sp, self.s_T, i, self.s_passed)
        sp.dma_start(self.run[:], rows(self.flat_run, i)).then_inc(self.s_run, 16)

    def turn(self, pe, i, first, flip):
        pe.wait_ge(self.s_rows, 16 * (i + 1))
        if not first:
            pe.wait_ge(self.s_fresh, i)
        for u in range(U):
            ins = pe.matmul(slot(self.ps, u), self.tile[:, U - 1 - u, :], flip[:], start=True, stop=True)
        ins.then_inc(self.s_turned, 1)

    def hold(self, dve, i, first, free=None):
        dve.wait_ge(self.s_turned, i + 1)
        dve.wait_ge(self.s_run, 16 * (i + 1))
        dve.scalar_tensor_tensor(out=self.fresh[:], in0=self.run[:], scalar=-1.0, in1=self.ps[:], op0=ALU.add, op1=ALU.mult
                                 ).then_inc(self.s_fresh, 1)
        dve.wait_ge(self.s_fresh, i + 1)
        if free is not None:
            dve.wait_ge(*free)
        if not first:
            dve.wait_ge(self.s_carry, i)
        dve.tensor_tensor_scan(self.T[:], self.run[:], self.fresh[:], 0.0 if first else self.carry[:, 0:1], ALU.mult,
                               ALU.subtract).then_inc(self.s_T, 1)
        dve.wait_ge(self.s_T, i + 1)
        dve.tensor_copy(self.carry[:], self.T[:, CH - 1:CH]).then_inc(self.s_carry, 1)


def sp_steps(sp, body, puts, ahead=1):
    def scattered(i, first):
        for p in puts:
            p.load_index(sp, i, first)
        for p in puts:
            p.keep(sp, i)

    for i in range(ahead + 1):
        body(i, i == 0)
    scattered(0, True)
    with sp.Fori(ahead + 1, NC) as i:
        body(i, False)
        scattered(i - ahead, False)
    for i in range(NC - ahead, NC):
        scattered(i, False)
    for p in puts:
        if p.by_edge is not None:
            sp.wait_ge(p.s_kept, 16 * NC)


def pool_steps(pool, streams, puts, s_passed, more=None, ahead=1):
    def fetch(i, first):
        for st in streams:
            st.fetch(pool, i, first, s_passed)
        if more:
            more(i, first)

    for i in range(ahead):
        fetch(i, i == 0)
    with pool.Fori(ahead, NC) as i:
        fetch(i, False)
        for put in puts:
            put.put(pool, i - ahead, s_passed)
    for i in range(NC - ahead, NC):
        for put in puts:
            put.put(pool, i, s_passed)
    for put in puts:
        pool.wait_ge(put.s_put, 16 * U * NC)


class PairedStream:

    def __init__(self, ph, name, table, index, ps):
        self.table, self.flat, self.ps = table, index, ps
        self.index = [ph.sb(f"{name}_index{b}", [P, U], I32) for b in range(2)]
        self.tile = [ph.sb(f"{name}_tile{b}", [P, U, C]) for b in range(2)]
        self.s_index = [ph.sem(f"{name}_index{b}") for b in range(2)]
        self.s_rows = [ph.sem(f"{name}_rows{b}") for b in range(2)]
        self.s_turned, self.s_T = ph.sem(f"{name}_turned"), ph.sem(f"{name}_T")
        self.T = ph.sb(f"{name}_T", [P, CH])

    def load_index(self, eng, i, place):
        eng.dma_start(self.index[place[0]][:], chunk(self.flat, i)).then_inc(self.s_index[place[0]], 16)

    def fetch(self, pool, i, place, s_passed, early=False):
        b, used = place
        if not early:
            gate(pool, self.s_turned, i - 1, s_passed)
        gate(pool, self.s_index[b], 16 * (used + 1), s_passed)
        for u in range(U):
            gather(pool, self.tile[b], self.table, self.index[b], u, self.s_rows[b])

    def turn(self, pe, i, first, place, ident, read=None):
        b, used = place
        pe.wait_ge(self.s_rows[b], 16 * U * (used + 1))
        if not first:
            pe.wait_ge(self.s_T if read is None else read, i)
        for u in range(U):
            ins = pe.transpose(slot(self.ps, u), self.tile[b][:, u, :], ident[:])
        ins.then_inc(self.s_turned, 1)

    def copy_out(self, act, i, first, place, free=None, next2=True):
        Stream.copy_out(self, act, i, first, free)
        if next2:
            self.load_index(act, i + 2, place)


class PairedPut(Put):

    def __init__(self, ph, name, table, index, last_row, by_edge=None):
        super().__init__(ph, name, table, index, last_row, by_edge)
        self.indices = [self.index, ph.sb(f"{name}_index1", [P, U], I32)]
        self.s_placed = ph.sem(f"{name}_placed")
        self.s_indices = [self.s_index, ph.sem(f"{name}_index1")]

    def load_index(self, sp, i, place, early=False):
        b, used = place
        if not early:
            gate(sp, self.s_put, 16 * U * (i - 1), self.s_placed)
        sp.dma_start(self.indices[b][:], chunk(self.flat, i)).then_inc(self.s_indices[b], 16)

    def put(self, pool, i, place, s_passed):
        b, used = place
        gate(pool, self.s_made, i + 1, s_passed)
        gate(pool, self.s_indices[b], 16 * (used + 1), s_passed)
        for u in range(U):
            scatter(pool, self.table, self.tile, self.indices[b], u, self.s_put, self.last_row)


def paired_sp_steps(sp, stream, held, body, puts, late=0):
    def indices(i, place, early=False):
        for p in puts:
            p.load_index(sp, i, place, early)

    def loads(i, first=False, more=True):
        if more:
            for h in held:
                h.load_rows(sp, i + 1, False)
        body(i, first)
        if more:
            for h in held:
                h.load_run(sp, i + 1, False)

    def step(i, place):
        b, used = place
        loads(i)
        indices(i - late, (b, used - late // 2))

    stream.load_index(sp, 0, (0, 0))
    stream.load_index(sp, 1, (1, 0))
    for h in held:
        h.load_rows(sp, 0, True)
        h.load_run(sp, 0, True)
    for i in range(late + 2):
        loads(i, i == 0)
        if i >= late:
            indices(i - late, (i % 2, 0), True)
    pairs(sp, late + 2, NC - 1, step)
    loads(NC - 1, more=False)
    for i in range(NC - 1 - late, NC):
        indices(i, (i % 2, i // 2))


def paired_pool_steps(pool, stream, puts, s_passed, behind=2):
    def step(i, place):
        b, used = place
        stream.fetch(pool, i, place, s_passed)
        for p in puts:
            p.put(pool, i - behind, ((b - behind) % 2, used + (b - behind) // 2), s_passed)

    for i in range(behind):
        stream.fetch(pool, i, (i % 2, i // 2), s_passed, i < 2)
    if behind % 2:
        step(behind, (behind % 2, behind // 2))
    pairs(pool, behind + behind % 2, NC, step)
    for i in range(NC - behind, NC):
        for p in puts:
            p.put(pool, i, (i % 2, i // 2), s_passed)
    for p in puts:
        pool.wait_ge(p.s_put, 16 * U * NC)


def edge_attention(nc, w, tab, flat, kept):
    with Phase(nc, "l1") as ph:
        ident = ph.sb("ident", [P, P])
        flip = ph.sb("flip", [P, P])
        w23 = ph.sb("w23", [P, 2])
        w3b = ph.sb("w3b", [P, P])
        ones = ph.sb("ones", [P, P])
        eps = ph.sb("eps", [P, 1])
        run = ph.sb("run", [P, CH])
        prod = ph.sb("prod", [P, CH])
        msg = ph.sb("msg", [P, CH])
        agg = ph.sb("agg", [P, CH])
        carry = ph.sb("carry", [P, 1])
        both = ph.sb("both", [P, CH])
        ps_src, ps_dst, ps_att, ps_out = (ph.ps(n) for n in ("ps_src", "ps_dst", "ps_att", "ps_out"))
        src = PairedStream(ph, "src", tab["x1"], flat["src_r"], ps_src)
        dst = Held(ph, "dst", kept["x1"], ps_dst, flat["run_r"])
        put = PairedPut(ph, "x2", tab["x2"], flat["put_r"], N - 1, kept["x2"])
        norm = Norm(ph, "norm", eps)
        s = {n: ph.sem(n) for n in ("weights", "ready", "run", "prod", "att", "msg", "agg", "carry", "both", "out",
                                    "passed", "sp_passed")}
        block = ph.block()

        @block.sync
        def _(sp):
            sp.dma_start(ident[:], w["ident"]).then_inc(s["weights"], 16)
            sp.dma_start(flip[:], w["flip"]).then_inc(s["weights"], 16)
            sp.dma_start(w23[:], w["l1_w23"]).then_inc(s["weights"], 16)

            def body(i, first):
                if not first:
                    gate(sp, s["agg"], i, s["sp_passed"])
                sp.dma_start(run[:], rows(flat["run_r"], i)).then_inc(s["run"], 16)
            paired_sp_steps(sp, src, (dst,), body, (put,))

        @block.gpsimd
        def _(pool):
            paired_pool_steps(pool, src, (put,), s["passed"])

        @block.tensor
        def _(pe):
            pe.wait_ge(s["weights"], 48)
            pe.wait_ge(s["ready"], 3)

            def front(i, first, place):
                src.turn(pe, i, first, place, ident)
                dst.turn(pe, i, first, flip)

            def body(i, first, more, place):
                pe.wait_ge(s["prod"], i + 1)
                pe.matmul(ps_att[:], w3b[:], prod[:], start=True, stop=True).then_inc(s["att"], 1)
                if more:
                    front(i + 1, False, place)
                pe.wait_ge(s["both"], i + 1)
                if not first:
                    pe.wait_ge(put.s_made, i)
                for u in range(U):
                    ins = pe.transpose(ps_out[:, u * C:(u + 1) * C], slot(both, u), ident[:])
                ins.then_inc(s["out"], 1)
            skewed_pairs(pe, front, body)

        @block.scalar
        def _(act):
            def front(i, first, place, next2=True):
                src.copy_out(act, i, first, place, None if first else (s["msg"], i), next2)

            def body(i, first, more, place, next2=True):
                if more:
                    front(i + 1, False, place, next2)
                norm.rootof(act, i)
                put.keep(act, i)
            skewed_pairs(act, front, body, True)
            act.wait_ge(put.s_kept, 16 * NC)

        @block.vector
        def _(dve):
            dve.memset(eps[:], EPS)
            dve.memset(carry[:], 0.0)
            dve.memset(ones[:], 1.0).then_inc(s["ready"], 1)
            dve.wait_ge(s["ready"], 1)
            dve.wait_ge(s["weights"], 48)
            dve.tensor_scalar(w3b[:], ones[:], w23[:, 1:2], None, ALU.mult).then_inc(s["ready"], 1)
            dve.wait_ge(s["ready"], 2)
            dve.sem_inc(s["ready"], 1)

            def front(i, first):
                dst.hold(dve, i, first, None if first else (s["both"], i))
                dve.wait_ge(src.s_T, i + 1)
                if not first:
                    dve.wait_ge(s["att"], i)
                dve.tensor_tensor(prod[:], src.T[:], dst.T[:], ALU.mult).then_inc(s["prod"], 1)

            def body(i, first, more):
                dve.wait_ge(s["att"], i + 1)
                if not first:
                    dve.wait_ge(s["carry"], i)
                dve.scalar_tensor_tensor(out=msg[:], in0=src.T[:], scalar=w23[:, 0:1], in1=ps_att[:],
                                         op0=ALU.mult, op1=ALU.mult).then_inc(s["msg"], 1)
                dve.wait_ge(s["msg"], i + 1)
                dve.wait_ge(s["run"], 16 * (i + 1))
                dve.tensor_tensor_scan(agg[:], run[:], msg[:], carry[:, 0:1], ALU.mult, ALU.add).then_inc(s["agg"], 1)
                dve.wait_ge(s["agg"], i + 1)
                dve.tensor_copy(carry[:], agg[:, CH - 1:CH]).then_inc(s["carry"], 1)
                if not first:
                    dve.wait_ge(s["out"], i)
                dve.tensor_tensor(both[:], agg[:], dst.T[:], ALU.add).then_inc(s["both"], 1)
                if more:
                    dve.wait_ge(s["both"], i + 1)
                    front(i + 1, False)
                dve.wait_ge(s["out"], i + 1)
                norm.statistics(dve, [ps_out[:].rearrange("p (u c) -> p u c", u=U)], i)
                norm.inverse(dve, i)
                put.free(dve, i, first)
                norm.normalize(dve, put.tile, ps_out[:].rearrange("p (u c) -> p u c", u=U), put.s_made)
            skewed(dve, front, body)


def edge_perceptrons(nc, l, w, tab, flat, kept):
    last = l == 2
    o = "drd"[l]
    with Phase(nc, f"l2_{l}") as ph:
        ident = ph.sb("ident", [P, P])
        flip = ph.sb("flip", [P, P])
        e1 = [ph.sb(f"e1_{x}", [P, C]) for x in ("src", "dst")]
        e2 = ph.sb("e2", [P, 64])
        eb1 = ph.sb("eb1", [P, 1])
        eb2 = ph.sb("eb2", [64, 1])
        n1m = ph.sb("n1m", [64, 64])
        n1h = ph.sb("n1h", [P, 64])
        nb1 = ph.sb("nb1", [64, 1])
        n2 = ph.sb("n2", [65, C])
        eps = ph.sb("eps", [P, 1])
        run = ph.sb("run", [64, CH])
        kind = ph.sb("kind", [64, CH])
        inv = ph.sb("inv", [64, CH])
        z = ph.sb("z", [P, CH])
        msg = ph.sb("msg", [64, CH])
        agg = ph.sb("agg", [64, CH])
        carry = ph.sb("carry", [64, 1])
        mean = ph.sb("mean", [64, CH])
        hid = ph.sb("hid", [65, CH])
        ps_src, ps_dst, ps_z, ps_m, ps_hid, ps_out = (
            ph.ps(n) for n in ("ps_src", "ps_dst", "ps_z", "ps_m", "ps_hid", "ps_out"))
        table = tab[("x2", "h1", "h2")[l]]
        src = PairedStream(ph, "src", table, flat[f"src_{o}"], ps_src)
        dst = Held(ph, "dst", kept[("x2", "h1", "h2")[l]], ps_dst, flat[f"run_{o}"])
        put = PairedPut(ph, "put", tab[("h1", "h2", "x3")[l]], flat[f"put_{o}"], N - 1, kept.get(("h1", "h2", "x3")[l]))
        puts = [put]
        s = {n: ph.sem(n) for n in ("weights", "ready", "masks", "z_ps", "z", "m_ps", "msg", "agg", "carry", "mean",
                                    "own", "hid_ps", "hid", "out", "passed", "pe_passed", "sp_passed")}
        if last:
            b2 = ph.sb("b2", [P, U, C])
            res = Held(ph, "res", kept["x2"], ph.ps("ps_res"), flat[f"run_{o}"])
            u3 = ph.sb("u3", [P, U, C])
            u4 = ph.sb("u4", [P, U, C])
            s |= {n: ph.sem(n) for n in ("u3", "u4")}
            norm3, norm4 = Norm(ph, "norm3", eps), Norm(ph, "norm4", eps)
            put4 = PairedPut(ph, "put4", tab["out"], flat["put_d"], N - 1)
            puts.append(put4)
        block = ph.block()
        loads = [(ident[:], w["ident"]), (flip[:], w["flip"]), (e1[0][:], w["eW1"][l, 0]), (e1[1][:], w["eW1"][l, 1]),
                 (eb1[:], w["eb1"][l]), (eb2[:], w["eb2"][l]), (n1m[:], w["nW1"][l, 0:64, :]),
                 (n1h[:], w["nW1"][l, 64:192, :]), (nb1[:], w["nb1_cols"][l]), (n2[0:64, :], w["nW2"][l]),
                 (n2[64:65, :], w["nb2_rows"][l:l + 1, :])]
        late = [(e2[0:64, 0:32], w["eW2"][l, 0]), (e2[64:128, 32:64], w["eW2"][l, 1])]
        if last:
            loads.append((b2[:], w["b2"].rearrange("(a b c) -> a b c", a=1, b=1).to_broadcast([P, U, C])))
        NW = 16 * (len(loads) + len(late))

        @block.sync
        def _(sp):
            for d, f in loads:
                sp.dma_start(d, f).then_inc(s["weights"], 16)
            sp.wait_ge(s["ready"], 1)
            for d, f in late:
                sp.dma_start(d, f).then_inc(s["weights"], 16)

            def body(i, first):
                if not first:
                    gate(sp, s["mean"], i, s["sp_passed"])
                sp.dma_start(run[:], rows(flat[f"run_{o}"], i, 64)).then_inc(s["masks"], 16)
                for q in range(2):
                    sp.dma_start(kind[32 * q:32 * q + 32, :], rows(flat[f"kind{q}_{o}"], i, 32)).then_inc(s["masks"], 16)
                    sp.dma_start(inv[32 * q:32 * q + 32, :], rows(flat[f"inv{q}_{o}"], i, 32)).then_inc(s["masks"], 16)
            paired_sp_steps(sp, src, (dst, res) if last else (dst,), body, puts, 2 if last else 0)

        @block.gpsimd
        def _(pool):
            paired_pool_steps(pool, src, puts, s["passed"], 3 if last else 2)

        @block.tensor
        def _(pe):
            pe.wait_ge(s["weights"], NW)
            pe.wait_ge(s["ready"], 1)

            def turns(i, first, place):
                src.turn(pe, i, first, place, ident)
                dst.turn(pe, i, first, flip)
                if last:
                    res.turn(pe, i, first, flip)

            def hidden(i, first):
                pe.wait_ge(src.s_T, i + 1)
                if not first:
                    pe.wait_ge(s["z"], i)
                pe.matmul(ps_z[:], e1[0][:], src.T[:], start=True, stop=False)
                pe.wait_ge(dst.s_T, i + 1)
                pe.matmul(ps_z[:], e1[1][:], dst.T[:], start=False, stop=True).then_inc(s["z_ps"], 1)

            def own(i, first):
                if not first:
                    pe.wait_ge(s["hid"], i)
                pe.matmul(ps_hid[0:64, :], n1h[:], dst.T[:], start=True, stop=False).then_inc(s["own"], 1)

            def front(i, first, place):
                turns(i, first, place)
                hidden(i, first)
                own(i, first)

            def body(i, first, more, place):
                pe.wait_ge(s["z"], i + 1)
                if not first:
                    pe.wait_ge(s["msg"], i)
                pe.matmul(ps_m[0:64, :], e2[:], z[:], start=True, stop=True).then_inc(s["m_ps"], 1)
                if more:
                    turns(i + 1, False, place)
                gate(pe, s["mean"], i + 1, s["pe_passed"])
                pe.matmul(ps_hid[0:64, :], n1m[:], mean[:], start=False, stop=True).then_inc(s["hid_ps"], 1)
                if more:
                    hidden(i + 1, False)
                pe.wait_ge(s["hid"], i + 1)
                if not first:
                    pe.wait_ge(s["u3"] if last else put.s_made, i)
                for u in range(U):
                    ins = pe.matmul(ps_out[:, u * C:(u + 1) * C], slot(hid, u), n2[:], start=True, stop=not last)
                    if last:
                        if u == 0:
                            pe.wait_ge(res.s_T, i + 1)
                        ins = pe.matmul(ps_out[:, u * C:(u + 1) * C], slot(res.T, u), ident[:], start=False, stop=True)
                ins.then_inc(s["out"], 1)
                if more:
                    own(i + 1, False)
            skewed_pairs(pe, front, body)

        @block.scalar
        def _(act):
            def copy_src(i, first, place, next2=True):
                src.copy_out(act, i, first, place, None if first else (s["z_ps"], i), next2)

            def hidden(i, first):
                act.wait_ge(s["z_ps"], i + 1)
                if not first:
                    act.wait_ge(s["m_ps"], i)
                act.activation(z[:], ps_z[:], ACT.Relu, bias=eb1[:, 0:1]).then_inc(s["z"], 1)

            def front(i, first, place):
                copy_src(i, first, place)
                hidden(i, first)

            def body(i, first, more, place, next2=True):
                if more:
                    copy_src(i + 1, False, place, next2)
                act.wait_ge(s["hid_ps"], i + 1)
                if not first:
                    act.wait_ge(s["out"], i)
                act.activation(hid[0:64, :], ps_hid[0:64, :], ACT.Relu, bias=nb1[:, 0:1]).then_inc(s["hid"], 1)
                if last and not first:
                    norm3.rootof(act, i - 1)
                if more:
                    hidden(i + 1, False)
                if last and not first:
                    norm4.rootof(act, i - 1)
                    act.wait_ge(put.s_made, i)
                if last:
                    act.wait_ge(s["out"], i + 1)
                    act.copy(u3[:], ps_out[:].rearrange("p (u c) -> p u c", u=U)).then_inc(s["u3"], 1)
                else:
                    act.wait_ge(s["out"], i + 1)
                    put.free(act, i, first)
                    act.copy(put.tile[:], ps_out[:].rearrange("p (u c) -> p u c", u=U)).then_inc(put.s_made, 1)
                    put.keep(act, i)
            skewed_pairs(act, front, body, True)
            if not last:
                act.wait_ge(put.s_kept, 16 * NC)
            if last:
                norm3.rootof(act, NC - 1)
                norm4.rootof(act, NC - 1)

        @block.vector
        def _(dve):
            dve.memset(e2[:], 0.0)
            dve.memset(eps[:], EPS)
            dve.memset(hid[64:65, :], 1.0)
            dve.memset(carry[:], 0.0).then_inc(s["ready"], 1)
            dve.wait_ge(s["weights"], NW)
            dve.wait_ge(s["ready"], 1)

            def hold_own(i, first):
                dst.hold(dve, i, first, None if first else (s["own"], i))

            def hold_residual(i, first):
                if last:
                    res.hold(dve, i, first, None if first else (s["out"], i))

            def front(i, first):
                hold_own(i, first)
                hold_residual(i, first)

            def norm_first(i):
                norm3.inverse(dve, i)
                put.free(dve, i, isinstance(i, int) and i == 0)
                norm3.normalize(dve, put.tile, u3, put.s_made)
                dve.wait_ge(put.s_made, i + 1)
                dve.tensor_tensor(u4[:], put.tile[:], b2[:], ALU.add).then_inc(s["u4"], 1)
                dve.wait_ge(s["u4"], i + 1)
                norm4.statistics(dve, [u4], i)

            def norm_second(i):
                norm4.inverse(dve, i)
                put4.free(dve, i, isinstance(i, int) and i == 0)
                norm4.normalize(dve, put4.tile, u4, put4.s_made)

            def statistics(i):
                dve.wait_ge(s["u3"], i + 1)
                norm3.statistics(dve, [u3], i)

            def body(i, first, more):
                dve.wait_ge(s["masks"], 80 * (i + 1))
                dve.wait_ge(s["m_ps"], i + 1)
                dve.scalar_tensor_tensor(out=msg[:], in0=ps_m[0:64, :], scalar=eb2[:, 0:1], in1=kind[:],
                                         op0=ALU.add, op1=ALU.mult).then_inc(s["msg"], 1)
                dve.wait_ge(s["msg"], i + 1)
                if not first:
                    dve.wait_ge(s["carry"], i)
                dve.tensor_tensor_scan(agg[:], run[:], msg[:], carry[:, 0:1], ALU.mult, ALU.add).then_inc(s["agg"], 1)
                dve.wait_ge(s["agg"], i + 1)
                dve.tensor_copy(carry[:], agg[:, CH - 1:CH]).then_inc(s["carry"], 1)
                if not first:
                    dve.wait_ge(s["hid_ps"], i)
                dve.tensor_tensor(mean[:], agg[:], inv[:], ALU.mult).then_inc(s["mean"], 1)
                if last and not first:
                    statistics(i - 1)
                if more:
                    hold_own(i + 1, False)
                if last and not first:
                    norm_first(i - 1)
                if more:
                    hold_residual(i + 1, False)
                if last and not first:
                    norm_second(i - 1)
            skewed(dve, front, body)
            if last:
                statistics(NC - 1)
                norm_first(NC - 1)
                norm_second(NC - 1)


def hyper_edges(nc, name, source, w_name, target, w, flat, affine=None):
    with Phase(nc, name) as ph:
        ident = ph.sb("ident", [P, P])
        wt = ph.sb("wt", [P, C])
        ac = ph.sb("ac", [P, 2])
        run = ph.sb("run", [P, CH])
        inv = ph.sb("inv", [P, CH])
        agg = ph.sb("agg", [P, CH])
        carry = ph.sb("carry", [P, 1])
        mean = ph.sb("mean", [P, CH])
        zero = ph.sb("zero", [1, C])
        ps_src, ps_out = ph.ps("ps_src"), ph.ps("ps_out")
        src = PairedStream(ph, "src", source, flat["src_d"], ps_src)
        put = PairedPut(ph, "put", target, flat["put_d"], H5 - 1)
        s = {n: ph.sem(n) for n in ("weights", "ready", "masks", "agg", "carry", "mean", "aff", "out", "passed", "sp_passed",
                                    "zeroed")}
        block = ph.block()

        @block.sync
        def _(sp):
            sp.dma_start(ident[:], w["ident"]).then_inc(s["weights"], 16)
            sp.dma_start(wt[:], w[w_name]).then_inc(s["weights"], 16)
            if affine is not None:
                sp.dma_start(ac[:], affine).then_inc(s["weights"], 16)
            sp.wait_ge(s["ready"], 1)
            sp.dma_start(target[H5 - 1:H5, :], zero[:]).then_inc(s["zeroed"], 16)

            def body(i, first):
                if not first:
                    gate(sp, s["mean"], i, s["sp_passed"])
                sp.dma_start(run[:], rows(flat["run_d"], i)).then_inc(s["masks"], 16)
                sp.dma_start(inv[:], rows(flat["inv_deg_d"], i)).then_inc(s["masks"], 16)
            paired_sp_steps(sp, src, (), body, (put,))

        @block.gpsimd
        def _(pool):
            gate(pool, s["zeroed"], 16, s["passed"])
            paired_pool_steps(pool, src, (put,), s["passed"])

        NW = 32 if affine is None else 48

        @block.tensor
        def _(pe):
            pe.wait_ge(s["weights"], NW)

            def front(i, first, place):
                src.turn(pe, i, first, place, ident, s["agg"])

            def body(i, first, more, place):
                if more:
                    front(i + 1, False, place)
                made = s["mean"] if affine is None else s["aff"]
                pe.wait_ge(made, i + 1)
                if not first:
                    pe.wait_ge(put.s_made, i)
                for u in range(U):
                    ins = pe.matmul(ps_out[:, u * C:(u + 1) * C], slot(mean, u), wt[:], start=True, stop=True)
                ins.then_inc(s["out"], 1)
            skewed_pairs(pe, front, body)

        @block.scalar
        def _(act):
            act.wait_ge(s["weights"], NW)

            def indices(i, first, place, next2=True):
                if next2:
                    act.wait_ge(src.s_turned, i + 1)
                    src.load_index(act, i + 2, place)

            def body(i, first, more, place, next2=True):
                if more:
                    indices(i + 1, False, place, next2)
                if affine is not None:
                    act.wait_ge(s["mean"], i + 1)
                    act.activation(mean[:], mean[:], ACT.Identity, scale=ac[:, 0:1], bias=ac[:, 1:2]).then_inc(s["aff"], 1)
                act.wait_ge(s["out"], i + 1)
                put.free(act, i, first)
                act.copy(put.tile[:], ps_out[:].rearrange("p (u c) -> p u c", u=U)).then_inc(put.s_made, 1)
            skewed_pairs(act, indices, body, True)

        @block.vector
        def _(dve):
            dve.memset(carry[:], 0.0)
            dve.memset(zero[:], 0.0).then_inc(s["ready"], 1)
            dve.wait_ge(s["ready"], 1)

            def body(i, first):
                dve.wait_ge(src.s_turned, i + 1)
                dve.wait_ge(s["masks"], 32 * (i + 1))
                if not first:
                    dve.wait_ge(s["carry"], i)
                dve.tensor_tensor_scan(agg[:], run[:], ps_src[:], carry[:, 0:1], ALU.mult, ALU.add).then_inc(s["agg"], 1)
                dve.wait_ge(s["agg"], i + 1)
                dve.tensor_copy(carry[:], agg[:, CH - 1:CH]).then_inc(s["carry"], 1)
                if not first:
                    dve.wait_ge(s["out"], i)
                dve.tensor_tensor(mean[:], agg[:], inv[:], ALU.mult).then_inc(s["mean"], 1)
            steps(dve, NC, body)


def nodes_of_edges(nc, name, source, target, w, tab, flat, affine):
    final = target is None
    with Phase(nc, name) as ph:
        ident = ph.sb("ident", [P, P])
        run = ph.sb("run", [P, CH])
        inv = ph.sb("inv", [P, CH])
        agg = ph.sb("agg", [P, CH])
        carry = ph.sb("carry", [P, 1])
        g = ph.sb("g", [P, CH])
        ps_src, ps_out = ph.ps("ps_src"), ph.ps("ps_out")
        src = Stream(ph, "src", source, flat["dst_s"], ps_src)
        put = Put(ph, "put", tab["out"] if final else target, flat["put_s"], N - 1)
        s = {n: ph.sem(n) for n in ("weights", "ready", "masks", "agg", "carry", "g", "out", "passed",
                                    "gl", "bn", "step", "affine", "stats")}
        eps = ph.sb("eps", [P, 1])
        if final:
            b2 = ph.sb("b2", [P, U, C])
            res = Stream(ph, "res", tab["x3"], flat["src_s"], None)
            res.s_turned = ph.sem("res_used")
            resb = ph.sb("resb", [P, U, C])
            u4 = ph.sb("u4", [P, U, C])
            norm = Norm(ph, "norm", eps)
            s |= {n: ph.sem(n) for n in ("resb", "u4")}
        else:
            last = ph.sb("last", [P, CH])
            gl = ph.sb("gl", [P, CH])
            stats = ph.sb("stats", [P, NC, 6])
            gb = ph.sb("gb", [P, 2])
            mv = ph.sb("mv", [P, 2])
            t = {n: ph.sb(n, [P, 1]) for n in ("mean", "sq", "var", "var2", "root", "rstd", "am")}
            ac = ph.sb("ac", [P, 2])
        block = ph.block()

        @block.sync
        def _(sp):
            sp.dma_start(ident[:], w["ident"]).then_inc(s["weights"], 16)
            if final:
                sp.dma_start(b2[:], w["b2"].rearrange("(a b c) -> a b c", a=1, b=1).to_broadcast([P, U, C])
                             ).then_inc(s["weights"], 16)
            else:
                sp.dma_start(gb[:], w["gamma_beta"]).then_inc(s["weights"], 16)

            def body(i, first):
                src.load_index(sp, i, first)
                if final:
                    res.load_index(sp, i, first)
                if not first:
                    sp.wait_ge(s["g"] if final else s["gl"], i)
                sp.dma_start(run[:], rows(flat["run_s"], i)).then_inc(s["masks"], 16)
                sp.dma_start(inv[:], rows(flat["inv_w_s"], i)).then_inc(s["masks"], 16)
                if not final:
                    sp.dma_start(last[:], rows(flat["last_s"], i)).then_inc(s["masks"], 16)
            sp_steps(sp, body, (put,))
            if not final:
                sp.wait_ge(s["bn"], 1)
                sp.dma_start(affine, ac[:]).then_inc(s["affine"], 16)
                sp.wait_ge(s["affine"], 16)

        @block.gpsimd
        def _(pool):
            pool_steps(pool, (src, res) if final else (src,), (put,), s["passed"])

        @block.tensor
        def _(pe):
            pe.wait_ge(s["weights"], 32)

            def body(i, first):
                src.turn(pe, i, first, ident, None if first else (s["agg"], i))
                pe.wait_ge(s["g"], i + 1)
                if not first:
                    pe.wait_ge(s["u4"] if final else put.s_made, i)
                for u in range(U):
                    ins = pe.transpose(ps_out[:, u * C:(u + 1) * C], slot(g, u), ident[:])
                ins.then_inc(s["out"], 1)
            steps(pe, NC, body)

        @block.scalar
        def _(act):
            def body(i, first):
                if final:
                    norm.rootof(act, i)
                else:
                    act.wait_ge(s["out"], i + 1)
                    put.free(act, i, first)
                    act.copy(put.tile[:], ps_out[:].rearrange("p (u c) -> p u c", u=U)).then_inc(put.s_made, 1)
            steps(act, NC, body)
            if not final:
                act.wait_ge(s["step"], 5)
                act.activation(t["root"][:], t["var2"][:], ACT.Sqrt, bias=eps[:, 0:1]).then_inc(s["step"], 1)

        @block.vector
        def _(dve):
            dve.memset(eps[:], EPS)
            dve.memset(carry[:], 0.0)
            dve.memset(g[:], 0.0).then_inc(s["ready"], 1)
            dve.wait_ge(s["ready"], 1)
            dve.wait_ge(s["weights"], 32)

            def body(i, first):
                dve.wait_ge(src.s_turned, i + 1)
                dve.wait_ge(s["masks"], (32 if final else 48) * (i + 1))
                if not first:
                    dve.wait_ge(s["carry"], i)
                dve.tensor_tensor_scan(agg[:], run[:], ps_src[:], carry[:, 0:1], ALU.mult, ALU.add).then_inc(s["agg"], 1)
                dve.wait_ge(s["agg"], i + 1)
                dve.tensor_copy(carry[:], agg[:, CH - 1:CH]).then_inc(s["carry"], 1)
                if not first:
                    dve.wait_ge(s["out"], i)
                dve.tensor_tensor(g[:], agg[:], inv[:], ALU.mult).then_inc(s["g"], 1)
                if final:
                    dve.wait_ge(res.s_rows, 16 * U * (i + 1))
                    dve.tensor_tensor(resb[:], res.tile[:], b2[:], ALU.add).then_inc(res.s_turned, 1)
                    dve.wait_ge(res.s_turned, i + 1)
                    dve.wait_ge(s["out"], i + 1)
                    if not first:
                        dve.wait_ge(put.s_made, i)
                    dve.tensor_tensor(u4[:], ps_out[:].rearrange("p (u c) -> p u c", u=U), resb[:], ALU.add
                                      ).then_inc(s["u4"], 1)
                    dve.wait_ge(s["u4"], i + 1)
                    norm.statistics(dve, [u4], i)
                    norm.inverse(dve, i)
                    put.free(dve, i, first)
                    norm.normalize(dve, put.tile, u4, put.s_made)
                else:
                    dve.wait_ge(s["g"], i + 1)
                    dve.tensor_tensor(gl[:], g[:], last[:], ALU.mult).then_inc(s["gl"], 1)
                    dve.wait_ge(s["gl"], i + 1)
                    dve.bn_stats(stats[:, bass.ds(i, 1), :].rearrange("p a f -> p (a f)"), gl[:]
                                 ).then_inc(s["stats"], 1)
                    dve.wait_ge(s["stats"], i + 1)
            steps(dve, NC, body)
            if not final:
                dve.bn_aggr(mv[:], stats[:].rearrange("p n f -> p (n f)")).then_inc(s["step"], 1)
                dve.wait_ge(s["step"], 1)
                dve.tensor_scalar(t["mean"][:], mv[:, 0:1], EP / N, None, ALU.mult)
                dve.tensor_tensor(t["sq"][:], mv[:, 0:1], mv[:, 0:1], ALU.mult).then_inc(s["step"], 1)
                dve.wait_ge(s["step"], 2)
                dve.tensor_scalar(t["sq"][:], t["sq"][:], (EP / N) * ((N - EP) / N), None, ALU.mult).then_inc(s["step"], 1)
                dve.wait_ge(s["step"], 3)
                dve.tensor_scalar(t["var"][:], mv[:, 1:2], EP / N, None, ALU.mult).then_inc(s["step"], 1)
                dve.wait_ge(s["step"], 4)
                dve.tensor_tensor(t["var2"][:], t["var"][:], t["sq"][:], ALU.add).then_inc(s["step"], 1)
                dve.wait_ge(s["step"], 6)
                dve.reciprocal(t["rstd"][:], t["root"][:]).then_inc(s["step"], 1)
                dve.wait_ge(s["step"], 7)
                dve.tensor_tensor(ac[:, 0:1], t["rstd"][:], gb[:, 0:1], ALU.mult).then_inc(s["step"], 1)
                dve.wait_ge(s["step"], 8)
                dve.tensor_tensor(t["am"][:], ac[:, 0:1], t["mean"][:], ALU.mult).then_inc(s["step"], 1)
                dve.wait_ge(s["step"], 9)
                dve.tensor_tensor(ac[:, 1:2], gb[:, 1:2], t["am"][:], ALU.subtract).then_inc(s["bn"], 1)


def fold_attention(nc, w, att):
    with Phase(nc, "fold") as ph:
        wrt = ph.sb("wrt", [P, R, C])
        wct = ph.sb("wct", [P, C])
        wst = ph.sb("wst", [P, C])
        vec = ph.sb("vec", [P, 2 * R + 2])
        heads = ph.sb("heads", [P, H])
        blocks = ph.sb("blocks", [P, 2 * R + 2, H])
        ps = ph.ps("ps")
        s = {n: ph.sem(n) for n in ("weights", "blocks", "ps", "done")}
        block = ph.block()

        @block.sync
        def _(sp):
            for d, f in ((wrt, "W_rel_T"), (wct, "W_cross_T"), (wst, "W_self_T"), (vec, "att_vectors"), (heads, "heads")):
                sp.dma_start(d[:], w[f]).then_inc(s["weights"], 16)

        @block.vector
        def _(dve):
            dve.wait_ge(s["weights"], 80)
            for q in range(2 * R + 2):
                ins = dve.tensor_scalar(blocks[:, q, :], heads[:], vec[:, q:q + 1], None, ALU.mult)
            ins.then_inc(s["blocks"], 1)
            dve.wait_ge(s["ps"], 1)
            dve.tensor_copy(att[:], ps[:, 0:11 * H]).then_inc(s["done"], 1)
            dve.wait_ge(s["done"], 1)

        @block.tensor
        def _(pe):
            pe.wait_ge(s["blocks"], 1)
            at = 0
            for q in range(2 * R):
                pe.matmul(ps[:, at:at + H], wrt[:, q % R, :], blocks[:, q, :], start=True, stop=True)
                at += H
            for m, q in ((wct, 2 * R), (wst, 2 * R), (wst, 2 * R + 1)):
                ins = pe.matmul(ps[:, at:at + H], m[:], blocks[:, q, :], start=True, stop=True)
                at += H
            ins.then_inc(s["ps"], 1)


def relational_attention(nc, w, tab, flat, att, kept):
    RH = R * H
    K = R + 1
    with Phase(nc, "l0") as ph:
        ident = ph.sb("ident", [P, P])
        wrel = ph.sb("wrel", [P, R, C])
        wcross = ph.sb("wcross", [P, C])
        wself = ph.sb("wself", [P, C])
        spread = ph.sb("spread", [RH, R, C])
        spread3 = ph.sb("spread3", [3 * RH, R, C], BF16)
        brel = ph.sb("brel", [P, R])
        rid = ph.sb("rid", [RH, 1])
        bias = ph.sb("bias", [P, U, C])
        eps = ph.sb("eps", [P, 1])
        reset = ph.sb("reset", [RH, CH])
        rel = ph.sb("rel", [RH, CH])
        q = {n: ph.sb(n, [RH, CH]) for n in ("lg", "cap", "lk", "lm", "d1", "d2", "e", "c", "pe", "p")}
        parts = {n: ph.sb(f"parts_{n}", [3 * RH, CH], BF16) for n in "pcr"}
        left = {n: ph.sb(f"left_{n}", [3 * RH, CH]) for n in "pcr"}
        mbuf = ph.sb("mbuf", [RH, CH + 1])
        den = ph.sb("den", [RH, CH])
        dcarry = ph.sb("dcarry", [RH, 1])
        has, hneg = ([ph.sb(f"{n}{b}", [P, U, RH]) for b in range(2)] for n in ("has", "hneg"))
        dmax, rdT = (ph.sb(n, [P, U, RH]) for n in ("dmax", "rdT"))
        y = [ph.sb(f"y{b}", [P, CH]) for b in range(2)]
        py = ph.sb("py", [P, CH])
        num = [ph.sb(f"num{r}", [P, CH]) for r in range(R)]
        ncarry = ph.sb("ncarry", [P, R])
        ro = [ph.sb(f"ro{b}", [P, CH]) for b in range(2)]
        g = [ph.sb(f"g{b}", [P, CH]) for b in range(2)]
        ent = [ph.sb(f"ent{b}", [P, U, K + 1, C]) for b in range(2)]
        lg = {n: ph.sb(n, [P, U, K, H]) for n in ("lg0", "lg1", "lg2", "lg3", "lge", "alpha")}
        ld, mx, sm, rs = (ph.sb(n, [P, U, H]) for n in ("ld", "mx", "sm", "rs"))
        mixed = ph.sb("mixed", [P, U, K, C])
        outc, outb, u0 = (ph.sb(n, [P, U, C]) for n in ("outc", "outb", "u0"))
        ps_x, ps_l, ps_a, ps_y, ps_p, ps_c, ps_q, ps_h = (
            ph.ps(n) for n in ("ps_x", "ps_l", "ps_a", "ps_y", "ps_p", "ps_c", "ps_q", "ps_h"))
        hw_index = ph.sb("hw_index", [P, U], I32)
        hw_rows = ph.sb("hw_rows", [P, U, 1])
        hw = ph.sb("hw", [P, NC, U])
        src = Stream(ph, "src", tab["x"], flat["src_d"], ps_x)
        dst = Stream(ph, "dst", tab["x"], flat["dst_d"], ps_x)
        T = {n: [st.T, ph.sb(f"{n}_T1", [P, CH])] for n, st in (("src", src), ("dst", dst))}
        put = Put(ph, "put", tab["x1"], flat["put_d"], N - 1, kept["x1"])
        norm = Norm(ph, "norm", eps)
        names = ["weights", "ready", "spread3", "masks", "logit", "logit_copy", "cap", "lk", "lm", "m", "mshift", "d1", "e", "c",
                 "p", "den", "dcarry", "denT_ps", "dmax", "rdT", "rd_ps", "ld", "lg0", "lg1", "lg2", "lg3", "lg4",
                 "mx", "lg5", "lge", "sm", "rs", "alpha", "mixed", "outc", "x_ps", "x_copy", "outb", "u0", "passed",
                 "ent0", "ent_ps0", "pe_passed", "hw_index", "hw_rows", "hw", "hw_out"]
        names += [f"{n}{r}" for r in range(R) for n in ("y_ps", "y", "p_ps", "c_ps", "spread_ps", "py", "num", "ro", "g", "h_ps", "ent_r")]
        names += [f"{n}_{x}" for n in "pcr" for x in ("part1", "left1", "part2", "left2", "part3")]
        s = {n: ph.sem(n) for n in names}
        block = ph.block()
        loads = [(ident[:], w["ident"]), (wrel[:], w["W_rel"]), (wcross[:], w["W_cross"]), (wself[:], w["W_self"]),
                 (spread[:], w["spread"]), (brel[:], w["bias_rel"]), (rid[:], w["rid"]),
                 (bias[:], w["bias_lang"].rearrange("(a b c) -> a b c", a=1, b=1).to_broadcast([P, U, C]))]
        NW = 16 * len(loads)
        ps_dT = ps_c[:, 0:U * RH].rearrange("p (u x) -> p u x", u=U)
        ps_lg = ps_a[:, 0:U * (K + 1) * H].rearrange("p (u k h) -> p u k h", u=U, k=K + 1)
        AHEAD = 4

        def rounds(eng, body):
            body(0, 0, 0, True, True)
            body(1, 1, 1, True, True)
            body(2, 0, 2, True, True)
            with eng.Fori(0, (NC - 5) // 2) as j:
                body(j * 2 + 3, 1, 3, True, True)
                body(j * 2 + 4, 0, 3, True, True)
            for i in range(3 + (NC - 5) // 2 * 2, NC):
                body(i, i % 2, 3, i + 1 < NC, i + 2 < NC)

        @block.sync
        def _(sp):
            for d, f in loads:
                sp.dma_start(d, f).then_inc(s["weights"], 16)

            def body(c, first):
                src.load_index(sp, c, first)
                dst.load_index(sp, c, first)
                if not first:
                    sp.wait_ge(s["cap"], c)
                    sp.wait_ge(s["d1"], c)
                sp.dma_start(reset[:], rows(flat["reset_d"], c, RH)).then_inc(s["masks"], 16)
                sp.dma_start(rel[:], rows(flat["rel_d"], c, RH)).then_inc(s["masks"], 16)
                if not first:
                    sp.wait_ge(s["hw"], c)
                sp.dma_start(hw_index[:], chunk(flat["dst_s"], c)).then_inc(s["hw_index"], 16)
            sp_steps(sp, body, (put,), AHEAD)
            sp.wait_ge(s["hw"], NC)
            sp.dma_start(flat["weight_s"].rearrange("(c p u) -> p c u", p=P, u=U), hw[:]).then_inc(s["hw_out"], 16)
            sp.wait_ge(s["hw_out"], 16)

        @block.gpsimd
        def _(pool):
            def weights(c, first):
                if not first:
                    gate(pool, s["hw"], c, s["passed"])
                gate(pool, s["hw_index"], 16 * (c + 1), s["passed"])
                for u in range(U):
                    gather(pool, hw_rows, w["hyper_w"], hw_index, u, s["hw_rows"])
            pool_steps(pool, (src, dst), (put,), s["passed"], weights, AHEAD)

        @block.tensor
        def _(pe):
            pe.wait_ge(s["weights"], NW)
            pe.wait_ge(s["spread3"], 3)

            def turn_src(c, after=True):
                src.turn(pe, c, False, ident, (dst.s_T, c) if after else None)

            def turn_dst(c):
                dst.turn(pe, c, False, ident, (src.s_T, c + 1))

            def logits(c, par, first=False):
                pe.wait_ge(dst.s_T, c + 1)
                if not first:
                    pe.wait_ge(s["r_left1"], c)
                pe.matmul(ps_l[0:RH, :], att[:, 0:RH], T["src"][par][:], start=True, stop=False)
                pe.matmul(ps_l[0:RH, :], att[:, RH:2 * RH], T["dst"][par][:], start=False, stop=True).then_inc(s["logit"], 1)

            def sums_T(c):
                gate(pe, s["den"], c + 1, s["pe_passed"])
                for u in range(U):
                    ins = pe.transpose(ps_dT[:, u, :], slot(den, u), ident[0:RH, 0:RH])
                ins.then_inc(s["denT_ps"], 1)

            def inverse_back(c):
                pe.wait_ge(s["rdT"], c + 1)
                for u in range(U):
                    ins = pe.transpose(slot(ps_l[0:RH], u), rdT[:, u, :], ident[:])
                ins.then_inc(s["rd_ps"], 1)

            def body(i, par, past, next1, next2):
                for n in "pc":
                    pe.wait_ge(s[f"{n}_part3"], i + 1)

                def spread_out(r):
                    if r:
                        pe.wait_ge(s[f"ro{r - 1}"], i + 1)
                    elif past:
                        pe.wait_ge(s[f"ro{R - 1}"], i)
                    pe.matmul(ps_y[:], wrel[:, r, :], T["src"][par][:], start=True, stop=True).then_inc(s[f"y_ps{r}"], 1)
                    pe.matmul(ps_p[:], spread3[:, r, :], parts["p"][:], start=True, stop=True).then_inc(s[f"p_ps{r}"], 1)
                    pe.matmul(ps_c[:], spread3[:, r, :], parts["c"][:], start=True, stop=True).then_inc(s[f"c_ps{r}"], 1)
                    if r == 0:
                        pe.wait_ge(s["r_part3"], i + 1)
                    pe.matmul(ps_q[:], spread3[:, r, :], parts["r"][:], start=True, stop=True).then_inc(s[f"spread_ps{r}"], 1)

                def cross(r):
                    pe.wait_ge(s[f"g{r}"], i + 1)
                    pe.wait_ge(s["ent0"] if r == 0 else s[f"ent_r{r - 1}"], i + 1)
                    for u in range(U):
                        pe.matmul(ps_h[:, u * C:(u + 1) * C], slot(g[r % 2], u), wcross[:], start=True, stop=True)
                        ins = pe.matmul(ps_lg[:, u, r + 1, :], slot(g[r % 2], u), att[:, 8 * H:9 * H], start=True, stop=True)
                    ins.then_inc(s[f"h_ps{r}"], 1)

                def own():
                    if past:
                        pe.wait_ge(s["x_copy"], i)
                        pe.wait_ge(s["lg0"], i)
                    for u in range(U):
                        ins = pe.matmul(ps_h[:, u * C:(u + 1) * C], slot(T["dst"][par], u), wself[:], start=True, stop=True)
                    ins.then_inc(s["ent_ps0"], 1)
                    for u in range(U):
                        pe.matmul(ps_lg[:, u, 0, :], slot(T["dst"][par], u), att[:, 9 * H:10 * H], start=True, stop=True)
                        pe.matmul(ps_lg[:, u, K, :], slot(T["dst"][par], u), att[:, 10 * H:11 * H], start=True, stop=True)

                spread_out(0)
                if next1:
                    turn_dst(i + 1)
                own()
                for r in range(R):
                    if r + 1 < R:
                        spread_out(r + 1)
                    if r == 0 and next1:
                        logits(i + 1, 1 - par)
                    cross(r)
                if next1:
                    sums_T(i + 1)
                pe.wait_ge(s[f"ent_r{R - 1}"], i + 1)
                for u in range(U):
                    ins = pe.transpose(ps_h[:, u * C:(u + 1) * C], slot(T["dst"][par], u), ident[:])
                ins.then_inc(s["x_ps"], 1)
                if next1:
                    inverse_back(i + 1)
                if next2:
                    turn_src(i + 2)

            turn_src(0, False)
            turn_dst(0)
            logits(0, 0, True)
            sums_T(0)
            turn_src(1)
            inverse_back(0)
            rounds(pe, body)

        @block.scalar
        def _(act):
            act.wait_ge(s["weights"], NW)
            for j in range(3):
                act.copy(spread3[j * RH:(j + 1) * RH], spread[:]).then_inc(s["spread3"], 1)

            def turned(n, c, par, first=False):
                st, used = {"src": (src, f"spread_ps{R - 1}"), "dst": (dst, "x_ps")}[n]
                act.wait_ge(st.s_turned, c + 1)
                if not first:
                    act.wait_ge(s[used], c - 1)
                act.copy(T[n][par][:], ps_x[:]).then_inc(st.s_T, 1)

            def copy_logits(c):
                act.wait_ge(s["logit"], c + 1)
                if not isinstance(c, int) or c:
                    act.wait_ge(s["lk"], c)
                act.copy(q["lg"][:], ps_l[0:RH, :]).then_inc(s["logit_copy"], 1)

            def part(n, c, k, source):
                at = slice((k - 1) * RH, k * RH)
                act.copy(parts[n][at], source).then_inc(s[f"{n}_part{k}"], 1)

            def factors(c, first):
                act.wait_ge(s["e"], c + 1)
                act.activation(q["c"][:], q["d2"][:], ACT.Exp)
                act.activation(q["pe"][:], q["e"][:], ACT.Exp).then_inc(s["c"], 1)
                if not first:
                    act.wait_ge(s[f"spread_ps{R - 1}"], c)
                act.wait_ge(s["c"], c + 1)
                part("c", c, 1, q["c"][:])

            def parts_of(names, c, k):
                for n in names:
                    act.wait_ge(s[f"{n}_left{k - 1}"], c + 1)
                    part(n, c, k, left[n][(k - 1) * RH:k * RH])

            def p_part(c):
                act.wait_ge(s["p"], c + 1)
                part("p", c, 1, q["p"][:])

            def inverse_part(c):
                act.wait_ge(s["rd_ps"], c + 1)
                part("r", c, 1, ps_l[0:RH, :])

            def body(i, par, past, next1, next2):
                def rows_out(k, done):
                    act.copy(ent[par][:, :, k, :], ps_h[:].rearrange("p (u c) -> p u c", u=U)).then_inc(done, 1)

                def copy_y(r):
                    act.wait_ge(s[f"y_ps{r}"], i + 1)
                    act.copy(y[r % 2][:], ps_y[:]).then_inc(s[f"y{r}"], 1)

                copy_y(0)
                if next1:
                    turned("dst", i + 1, 1 - par, past == 0)
                act.wait_ge(s["ent_ps0"], i + 1)
                if past > 1:
                    act.wait_ge(s["mixed"], i - 1)
                rows_out(0, s["ent0"])
                for r in range(R):
                    act.wait_ge(s[f"ro{r}"], i + 1)
                    act.activation(g[r % 2][:], ro[r % 2][:], ACT.Gelu, bias=brel[:, r:r + 1]).then_inc(s[f"g{r}"], 1)
                    if r + 1 < R:
                        copy_y(r + 1)
                    if r == 0 and next1:
                        copy_logits(i + 1)
                    if r == R - 1 and next1:
                        factors(i + 1, False)
                    act.wait_ge(s[f"h_ps{r}"], i + 1)
                    rows_out(r + 1, s[f"ent_r{r}"])
                if next1:
                    p_part(i + 1)
                act.wait_ge(s["x_ps"], i + 1)
                if past > 1:
                    act.wait_ge(s["u0"], i - 1)
                rows_out(K, s["x_copy"])
                if next1:
                    parts_of("cp", i + 1, 2)
                    inverse_part(i + 1)
                act.wait_ge(s["lg5"], i + 1)
                act.activation(lg["lge"][:], lg["lg2"][:], ACT.Exp).then_inc(s["lge"], 1)
                if next1:
                    parts_of("cp", i + 1, 3)
                    parts_of("r", i + 1, 2)
                if next2:
                    turned("src", i + 2, par)
                if next1:
                    parts_of("r", i + 1, 3)
                if past:
                    norm.rootof(act, i - 1)

            for n in ("src", "dst"):
                turned(n, 0, 0, True)
            copy_logits(0)
            factors(0, True)
            p_part(0)
            parts_of("cp", 0, 2)
            parts_of("cp", 0, 3)
            turned("src", 1, 1, True)
            inverse_part(0)
            parts_of("r", 0, 2)
            parts_of("r", 0, 3)
            rounds(act, body)
            norm.rootof(act, NC - 1)

        @block.vector
        def _(dve):
            dve.memset(eps[:], EPS)
            dve.memset(mbuf[:], -NEG)
            dve.memset(dcarry[:], 0.0)
            dve.memset(ncarry[:], 0.0).then_inc(s["ready"], 1)
            dve.wait_ge(s["weights"], NW)
            dve.wait_ge(s["ready"], 1)

            def exponents(c, first):
                dve.wait_ge(s["hw_rows"], 16 * U * (c + 1))
                dve.tensor_copy(hw[:, bass.ds(c, 1), :], hw_rows[:].rearrange("p u a -> p a u")).then_inc(s["hw"], 1)
                dve.wait_ge(s["masks"], 32 * (c + 1))
                dve.tensor_scalar(q["cap"][:], rel[:], rid[:, 0:1], 2 * NEG, ALU.is_equal, ALU.mult).then_inc(s["cap"], 1)
                dve.wait_ge(s["logit_copy"], c + 1)
                dve.scalar_tensor_tensor(out=q["lk"][:], in0=q["lg"][:], scalar=LEAK, in1=q["lg"][:],
                                         op0=ALU.mult, op1=ALU.max).then_inc(s["lk"], 1)
                dve.wait_ge(s["lk"], c + 1)
                dve.wait_ge(s["cap"], c + 1)
                dve.scalar_tensor_tensor(out=q["lm"][:], in0=q["cap"][:], scalar=-NEG, in1=q["lk"][:],
                                         op0=ALU.add, op1=ALU.min).then_inc(s["lm"], 1)
                dve.wait_ge(s["lm"], c + 1)
                dve.tensor_tensor_scan(mbuf[:, 1:CH + 1], reset[:], q["lm"][:], mbuf[:, 0:1], ALU.add, ALU.max
                                       ).then_inc(s["m"], 1)
                dve.wait_ge(s["m"], c + 1)
                dve.tensor_tensor(q["d1"][:], mbuf[:, 0:CH], reset[:], ALU.add).then_inc(s["d1"], 1)
                dve.wait_ge(s["d1"], c + 1)
                if not first:
                    dve.wait_ge(s["c"], c)
                dve.tensor_tensor(q["d2"][:], q["d1"][:], mbuf[:, 1:CH + 1], ALU.subtract)
                dve.tensor_tensor(q["e"][:], q["lm"][:], mbuf[:, 1:CH + 1], ALU.subtract).then_inc(s["e"], 1)
                dve.wait_ge(s["e"], c + 1)
                dve.tensor_copy(mbuf[:, 0:1], mbuf[:, CH:CH + 1]).then_inc(s["mshift"], 1)
                dve.wait_ge(s["mshift"], c + 1)

            def leave(n, c, k, whole):
                dve.wait_ge(s[f"{n}_part{k}"], c + 1)
                dve.tensor_tensor(left[n][k * RH:(k + 1) * RH], whole, parts[n][(k - 1) * RH:k * RH],
                                  ALU.subtract).then_inc(s[f"{n}_left{k}"], 1)

            def sums(c):
                dve.wait_ge(s["c"], c + 1)
                dve.scalar_tensor_tensor(out=q["p"][:], in0=q["cap"][:], scalar=0.0, in1=q["pe"][:],
                                         op0=ALU.is_gt, op1=ALU.mult).then_inc(s["p"], 1)
                dve.wait_ge(s["p"], c + 1)
                dve.tensor_tensor_scan(den[:], q["c"][:], q["p"][:], dcarry[:, 0:1], ALU.mult, ALU.add).then_inc(s["den"], 1)
                dve.wait_ge(s["den"], c + 1)
                dve.tensor_copy(dcarry[:], den[:, CH - 1:CH]).then_inc(s["dcarry"], 1)
                leave("c", c, 1, q["c"][:])
                leave("p", c, 1, q["p"][:])

            def inverse_sums(c, par):
                dve.wait_ge(s["denT_ps"], c + 1)
                dve.tensor_scalar(has[par][:], ps_dT, 0.0, None, ALU.is_gt)
                dve.tensor_scalar(dmax[:], ps_dT, 1e-30, None, ALU.max).then_inc(s["dmax"], 1)
                dve.wait_ge(s["dmax"], c + 1)
                dve.reciprocal(rdT[:], dmax[:]).then_inc(s["rdT"], 1)
                dve.tensor_scalar(hneg[par][:], has[par][:], -1.0, NEG, ALU.add, ALU.mult)

            def second_left(c):
                for n in "cp":
                    dve.wait_ge(s[f"{n}_left1"], c + 1)
                    leave(n, c, 2, left[n][RH:2 * RH])

            def relation(r, i, past):
                dve.wait_ge(s[f"p_ps{r}"], i + 1)
                dve.wait_ge(s[f"y{r}"], i + 1)
                dve.tensor_tensor(py[:], ps_p[:], y[r % 2][:], ALU.mult).then_inc(s[f"py{r}"], 1)
                dve.wait_ge(s[f"py{r}"], i + 1)
                dve.wait_ge(s[f"c_ps{r}"], i + 1)
                dve.tensor_tensor_scan(num[r][:], ps_c[:], py[:], ncarry[:, r:r + 1], ALU.mult, ALU.add
                                       ).then_inc(s[f"num{r}"], 1)
                dve.wait_ge(s[f"num{r}"], i + 1)
                dve.tensor_copy(ncarry[:, r:r + 1], num[r][:, CH - 1:CH])
                if r >= 2:
                    dve.wait_ge(s[f"g{r - 2}"], i + 1)
                elif past:
                    dve.wait_ge(s[f"g{r + 2}"], i)
                dve.wait_ge(s[f"spread_ps{r}"], i + 1)
                dve.tensor_tensor(ro[r % 2][:], num[r][:], ps_q[:], ALU.mult).then_inc(s[f"ro{r}"], 1)

            def softmax_front(i, par):
                dve.wait_ge(s[f"h_ps{R - 1}"], i + 1)
                dve.tensor_copy(ld[:], ps_lg[:, :, K, :]).then_inc(s["ld"], 1)
                dve.wait_ge(s["ld"], i + 1)
                for u in range(U):
                    ins = dve.tensor_tensor(lg["lg0"][:, u], ps_lg[:, u, 0:K, :],
                                            ld[:, u:u + 1, :].to_broadcast([P, K, H]), ALU.add)
                ins.then_inc(s["lg0"], 1)
                dve.wait_ge(s["lg0"], i + 1)
                dve.scalar_tensor_tensor(out=lg["lg3"][:], in0=lg["lg0"][:], scalar=LEAK, in1=lg["lg0"][:],
                                         op0=ALU.mult, op1=ALU.max).then_inc(s["lg2"], 1)
                dve.wait_ge(s["lg2"], i + 1)
                hasv = has[par][:].rearrange("p u (r h) -> p u r h", r=R)
                hnegv = hneg[par][:].rearrange("p u (r h) -> p u r h", r=R)
                dve.tensor_tensor(lg["lg3"][:, :, 1:K, :], lg["lg3"][:, :, 1:K, :], hasv, ALU.mult).then_inc(s["lg3"], 1)
                dve.wait_ge(s["lg3"], i + 1)
                dve.tensor_tensor(lg["lg3"][:, :, 1:K, :], lg["lg3"][:, :, 1:K, :], hnegv, ALU.add).then_inc(s["lg4"], 1)
                dve.wait_ge(s["lg4"], i + 1)
                dve.tensor_reduce(mx[:], lg["lg3"][:].rearrange("p u k h -> p u h k"), AX.X, ALU.max).then_inc(s["mx"], 1)
                dve.wait_ge(s["mx"], i + 1)
                for u in range(U):
                    ins = dve.tensor_tensor(lg["lg2"][:, u], lg["lg3"][:, u], mx[:, u:u + 1, :].to_broadcast([P, K, H]),
                                            ALU.subtract)
                ins.then_inc(s["lg5"], 1)

            def softmax_back(i):
                dve.wait_ge(s["lge"], i + 1)
                dve.tensor_reduce(sm[:], lg["lge"][:].rearrange("p u k h -> p u h k"), AX.X, ALU.add).then_inc(s["sm"], 1)
                dve.wait_ge(s["sm"], i + 1)
                dve.reciprocal(rs[:], sm[:]).then_inc(s["rs"], 1)
                dve.wait_ge(s["rs"], i + 1)
                for u in range(U):
                    ins = dve.tensor_tensor(lg["alpha"][:, u], lg["lge"][:, u], rs[:, u:u + 1, :].to_broadcast([P, K, H]),
                                            ALU.mult)
                ins.then_inc(s["alpha"], 1)

            def mix(i, par):
                dve.wait_ge(s["alpha"], i + 1)
                dve.wait_ge(s["x_copy"], i + 1)
                for u in range(U):
                    a = lg["alpha"][:, u].rearrange("p k h -> p (k h)").rearrange("p (x a) -> p x a", a=1)
                    ins = dve.tensor_tensor(mixed[:, u].rearrange("p k (h d) -> p (k h) d", h=H),
                                            ent[par][:, u, 0:K].rearrange("p k (h d) -> p (k h) d", h=H),
                                            a.to_broadcast([P, K * H, D]), ALU.mult)
                ins.then_inc(s["mixed"], 1)

            def mix_sum(i):
                dve.wait_ge(s["mixed"], i + 1)
                dve.tensor_reduce(outc[:], mixed[:].rearrange("p u k c -> p u c k"), AX.X, ALU.add).then_inc(s["outc"], 1)

            def statistics(i, par):
                dve.wait_ge(s["outc"], i + 1)
                dve.tensor_tensor(outb[:], outc[:], bias[:], ALU.add).then_inc(s["outb"], 1)
                dve.wait_ge(s["outb"], i + 1)
                dve.tensor_tensor(u0[:], ent[par][:, :, K, :], outb[:], ALU.add).then_inc(s["u0"], 1)
                dve.wait_ge(s["u0"], i + 1)
                norm.statistics(dve, [u0], i)

            def finish(i, first=False):
                norm.inverse(dve, i)
                put.free(dve, i, first)
                norm.normalize(dve, put.tile, u0, put.s_made)


            def body(i, par, past, next1, next2):
                relation(0, i, past)
                if past > 1:
                    finish(i - 2, past == 2)
                if past:
                    mix(i - 1, 1 - par)
                relation(1, i, past)
                if next1:
                    exponents(i + 1, False)
                relation(2, i, past)
                if past:
                    mix_sum(i - 1)
                relation(3, i, past)
                if past:
                    statistics(i - 1, 1 - par)
                if next1:
                    sums(i + 1)
                    inverse_sums(i + 1, 1 - par)
                softmax_front(i, par)
                if next1:
                    second_left(i + 1)
                    leave("r", i + 1, 1, ps_l[0:RH, :])
                softmax_back(i)
                if next1:
                    dve.wait_ge(s["r_left1"], i + 2)
                    leave("r", i + 1, 2, left["r"][RH:2 * RH])

            exponents(0, True)
            sums(0)
            inverse_sums(0, 0)
            second_left(0)
            leave("r", 0, 1, ps_l[0:RH, :])
            dve.wait_ge(s["r_left1"], 1)
            leave("r", 0, 2, left["r"][RH:2 * RH])
            rounds(dve, body)
            finish(NC - 2)
            mix(NC - 1, (NC - 1) % 2)
            mix_sum(NC - 1)
            statistics(NC - 1, (NC - 1) % 2)
            finish(NC - 1)



def graph_layers(nc, w, out):
    def dram(name, shape, dtype=F32):
        return nc.dram_tensor(name, shape, dtype).ap()

    tab = {n: dram(f"t_{n}", [N, C]) for n in ("x1", "x2", "h1", "h2", "x3")}
    tab |= {"x": w["x"], "out": out}
    edge_tab = [tab["x1"][0:H5, :], tab["x2"][0:H5, :]]
    node_sums = tab["h1"]
    by_dst, by_src = dram("by_dst", [EP + 2, 4], I32), dram("by_src", [EP + 2, 4], I32)
    flat = {n: dram(f"f_{n}", [EP], I32) for n in ("src_d", "dst_d", "put_d", "src_r", "put_r", "src_s", "dst_s", "put_s")}
    flat |= {n: dram(f"f_{n}", [EP]) for n in ("run_d", "run_r", "run_s", "last_s", "rel_d", "kind0_d", "kind1_d",
                                               "kind0_r", "kind1_r", "reset_d", "ones",
                                               "weight_s", "inv0_r", "inv1_r", "inv0_d", "inv1_d", "inv_deg_d", "inv_w_s")}
    from_last = dram("from_last", [EP + 2, 4], I32)
    kept = {n: dram(f"kept_{n}", [EP, C]) for n in ("x1", "x2", "h1", "h2")}
    sums = dram("sums", [6, EP])
    affine = dram("affine", [P, 2])

    sort_edges(nc, w["records"], w, by_dst, by_src, from_last)
    derive_orders(nc, {"d": by_dst, "r": from_last, "s": by_src}, flat)
    dense_pass(nc, w, tab)
    with nc.sbuf_tensor("att", [P, 11 * H], F32) as att:
        fold_attention(nc, w, att)
        relational_attention(nc, w, tab, flat, att, kept)
    count_runs(nc, flat, sums)
    edge_attention(nc, w, tab, flat, kept)
    for l in range(3):
        edge_perceptrons(nc, l, w, tab, flat, kept)
    hyper_edges(nc, "l3a", tab["x3"], "W1_T", edge_tab[0], w, flat)
    nodes_of_edges(nc, "l3b", edge_tab[0], node_sums, w, tab, flat, affine)
    hyper_edges(nc, "l3c", node_sums, "W2_T", edge_tab[1], w, flat, affine)
    nodes_of_edges(nc, "l3d", edge_tab[1], None, w, tab, flat, affine)


def layouts(i):
    a = np.ascontiguousarray
    dst_src = np.stack([i["dst"], i["src"]]).astype(np.int32)
    records = np.stack([i["dst"], i["src"], i["edge_type_4"], i["edge_type_2"]], axis=1).astype(np.int32)
    padding = np.array([[N, N, R, R]], np.int32).repeat(EP - E, axis=0)
    heads = (np.arange(C)[:, None] // D == np.arange(H)[None]).astype(np.float32)
    spread = np.zeros((R, H, R, C), np.float32)
    for r in range(R):
        spread[r, :, r, :] = heads.T
    return {
        "x": i["x"],
        "records": np.concatenate([records, padding]),
        "dst_src": np.concatenate([dst_src, np.full((2, EP - E), N, np.int32)], axis=1),
        "hyper_w": i["L3_gnn_hyperedge_weight"].reshape(H5, 1),
        "iota": np.tile(np.arange(CH, dtype=np.float32), (P, 1)),
        "tri": np.triu(np.ones((P, P), np.float32), 1),
        "tri_low": np.tril(np.ones((P, P), np.float32), -1),
        "ident": np.eye(P, dtype=np.float32),
        "flip": a(np.eye(P, dtype=np.float32)[::-1]),
        "heads": heads,
        "spread": spread.reshape(R * H, R, C),
        "rid": (np.arange(R * H) // H).astype(np.float32).reshape(R * H, 1),
        "W_rel": a(i["L0_gnn_W_rel"].transpose(1, 0, 2)),
        "W_rel_T": a(i["L0_gnn_W_rel"].transpose(2, 0, 1)),
        "W_cross": i["L0_gnn_W_cross"],
        "W_cross_T": a(i["L0_gnn_W_cross"].T),
        "W_self": i["L0_gnn_W_self"],
        "W_self_T": a(i["L0_gnn_W_self"].T),
        "att_vectors": a(np.concatenate([i["L0_gnn_att_src_rel"].reshape(R, C), i["L0_gnn_att_dst_rel"].reshape(R, C),
                                         i["L0_gnn_att_src_lang"].reshape(1, C),
                                         i["L0_gnn_att_dst_lang"].reshape(1, C)]).T),
        "bias_rel": a(i["L0_gnn_bias_rel"].T),
        "bias_lang": i["L0_gnn_bias_lang"],
        "l1_w23": a(np.stack([i["L1_gnn_W2"], i["L1_gnn_W3"]], axis=1)),
        "eW1": a(i["L2_gnn_eW1"].reshape(3, 2, 2, C, 64).transpose(0, 2, 3, 1, 4)).reshape(3, 2, C, 2 * 64),
        "eb1": i["L2_gnn_eb1"].reshape(3, 128, 1),
        "eW2": i["L2_gnn_eW2"],
        "eb2": i["L2_gnn_eb2"].reshape(3, 64, 1),
        "nW1": i["L2_gnn_nW1"],
        "nb1": a(i["L2_gnn_nb1"].T),
        "nb1_cols": i["L2_gnn_nb1"].reshape(3, 64, 1),
        "nW2": i["L2_gnn_nW2"],
        "nb2": a(i["L2_gnn_nb2"].T),
        "nb2_rows": i["L2_gnn_nb2"],
        "W1_T": a(i["L3_gnn_W1"].T),
        "W2_T": a(i["L3_gnn_W2"].T),
        "b2": i["L3_gnn_b2"],
        "gamma_beta": a(np.stack([i["L3_gnn_gamma"], i["L3_gnn_beta"]], axis=1)),
    }


def kernel(**inputs):
    import concourse.bacc as bacc
    from concourse.bass_utils import run_bass_kernel_spmd as run

    nc = bacc.Bacc("TRN2", target_bir_lowering=False, num_devices=1)
    arrays = {f"in_{n}": np.ascontiguousarray(v)
              for n, v in layouts({k: np.asarray(v) for k, v in inputs.items()}).items()}
    w = {n[3:]: nc.dram_tensor(n, list(v.shape), mybir.dt.from_np(v.dtype), kind="ExternalInput").ap()
         for n, v in arrays.items()}
    out = nc.dram_tensor("out", [N, C], F32, kind="ExternalOutput").ap()
    graph_layers(nc, w, out)
    nc.compile()
    return run(nc, [arrays], core_ids=[0]).results[0]["out"]
```
